# Optimizing a Trainium2 kernel written in Bass

```python
import numpy as np
import jax
import jax.numpy as jnp

def _softmax(x, axis=-1):
    return jax.nn.softmax(x, axis=axis)

def _gelu(x):
    return jax.nn.gelu(x, approximate=True)

def _silu(x):
    return jax.nn.silu(x)

def _sigmoid(x):
    return jax.nn.sigmoid(x)

def _layernorm(x, axis=-1, eps=1e-05):
    m = jnp.mean(x, axis=axis, keepdims=True)
    v = jnp.var(x, axis=axis, keepdims=True)
    return (x - m) / jnp.sqrt(v + eps)

def _scatter_add(tgt, idx, src, axis=0):
    return tgt.at[idx].add(src)

def _segment_sum(src, seg, n):
    return jax.ops.segment_sum(src, seg, n)
kernel_name = 'mk_adj_preln_d4_adj_r2_31f38f'

def setup_inputs(seed: int=0):
    np.random.seed(seed)
    _w = jnp.asarray

    def _rec_inputs():
        import jax
        import jax.numpy as jnp
        _gk = jax.random.key(seed)
        x = -0.000929 + 1 * jax.random.normal(jax.random.fold_in(_gk, 1), (8, 1024, 64), jnp.float32)
        _w = (1.0 + jnp.arange(1024, dtype=jnp.float32)) ** (-0.5)
        _w = _w / _w.mean()
        _pij = jnp.clip(0.00390625 * _w[:, None] * _w[None, :], 0.0, 1.0)
        _a = jax.random.uniform(jax.random.fold_in(_gk, 2), (1024, 1024)) < _pij
        _a = jnp.logical_or(_a, jnp.eye(1024, dtype=bool))
        _af = _a.astype(jnp.float32)
        adj = _af
        return (x, adj)
    x, adj = _rec_inputs()

    def _L0_gnn_setup():
        import jax, jax.numpy as jnp
        import numpy as np
        NEG = -1000000000.0
        key = jax.random.key(seed)
        ks = jax.random.split(key, 14)
        B, N, E, NF, NH = (8, 1024, 64, 64, 64)
        x = jax.random.normal(ks[0], (B, N, NF), dtype=jnp.float32)
        base = jax.nn.one_hot(jax.random.randint(ks[1], (N,), 0, E), E, dtype=jnp.float32)
        extra = (jax.random.uniform(ks[2], (N, E)) < 0.03).astype(jnp.float32)
        H = jnp.clip(base + extra, 0.0, 1.0)
        adj = (jax.random.uniform(ks[3], (N, N)) < 0.01).astype(jnp.float32)
        adj = jnp.clip(adj + jnp.eye(N, dtype=jnp.float32), 0.0, 1.0)
        s_in = 1.0 / np.sqrt(NF)
        s_h = 1.0 / np.sqrt(NH)
        W = jax.random.normal(ks[4], (NF, NH), dtype=jnp.float32) * s_in
        W_ind = jax.random.normal(ks[5], (NF, NH), dtype=jnp.float32) * s_in
        a_node = jax.random.normal(ks[6], (NH,), dtype=jnp.float32) * s_h
        a_gn = jax.random.normal(ks[7], (NH,), dtype=jnp.float32) * s_h
        a_ge = jax.random.normal(ks[8], (NH,), dtype=jnp.float32) * s_h
        fcW = jax.random.normal(ks[9], (NH, 2 * NH), dtype=jnp.float32) * s_h
        fcb = jnp.zeros((2 * NH,), dtype=jnp.float32)
        av = jax.random.normal(ks[10], (2 * NH,), dtype=jnp.float32) / np.sqrt(2 * NH)
        return {'x': x, 'H': H, 'adj': adj, 'nhid': NH, 'W': W, 'W_ind': W_ind, 'a_node': a_node, 'a_gn': a_gn, 'a_ge': a_ge, 'fcW': fcW, 'fcb': fcb, 'av': av}
    _L0_gnn_all = _L0_gnn_setup()
    _L0_gnn_in = {k: v for k, v in _L0_gnn_all.items() if k in ('H', 'W', 'W_ind', 'a_node', 'a_gn', 'a_ge', 'fcW', 'fcb', 'av')}
    del _L0_gnn_all

    def _L1_gnn_setup():
        import jax, jax.numpy as jnp
        import numpy as np
        MAX_STEPS = 3
        key = jax.random.key(seed)
        ks = jax.random.split(key, 7)
        B, N, D = (1, 4096, 64)
        return {'causal_vars': jax.random.normal(ks[0], (B, N, D), dtype=jnp.float32), 'adj_matrix': jax.random.uniform(ks[1], (N, N), dtype=jnp.float32), 'intervention_value': jax.random.normal(ks[2], (B, D), dtype=jnp.float32), 'W1': jax.random.normal(ks[3], (D, 2 * D), dtype=jnp.float32) * (1.0 / np.sqrt(2 * D)), 'b1': jax.random.normal(ks[4], (D,), dtype=jnp.float32) * 0.01, 'W2': jax.random.normal(ks[5], (D, D), dtype=jnp.float32) * (1.0 / np.sqrt(D)), 'b2': jax.random.normal(ks[6], (D,), dtype=jnp.float32) * 0.01, 'intervention_idx': 0}
    _L1_gnn_all = _L1_gnn_setup()
    _L1_gnn_in = {k: v for k, v in _L1_gnn_all.items() if k in ('intervention_value', 'W1', 'b1', 'W2', 'b2')}
    del _L1_gnn_all

    def _L2_gnn_setup():
        import jax, jax.numpy as jnp
        import numpy as np
        NEG_INF = -1e+16

        def gat_layer(x, graph, W, b):
            h = x @ W
            s = jnp.einsum('bnd,bmd->bnm', h, h) * graph
            s = jnp.where(s == 0.0, NEG_INF, s)
            a = jax.nn.softmax(s, axis=2)
            return jnp.einsum('bnm,bmd->bnd', a, h) + b
        key = jax.random.key(seed)
        k1, k2, k3, k4, k5, k6 = jax.random.split(key, 6)
        B, N, C_IN, HID, HEADS, C_OUT = (16, 512, 64, 128, 8, 64)
        flow_x = jax.random.normal(k1, (B, N, C_IN), dtype=jnp.float32)
        graph = jax.random.randint(k2, (N, N), 0, 2).astype(jnp.float32)
        Wh = jax.random.normal(k3, (HEADS, C_IN, HID), dtype=jnp.float32)
        bh = jax.random.normal(k4, (HEADS, HID), dtype=jnp.float32)
        W_out = jax.random.normal(k5, (HID * HEADS, C_OUT), dtype=jnp.float32)
        b_out = jax.random.normal(k6, (C_OUT,), dtype=jnp.float32)
        return {'flow_x': flow_x, 'graph': graph, 'Wh': Wh, 'bh': bh, 'W_out': W_out, 'b_out': b_out}
    _L2_gnn_all = _L2_gnn_setup()
    _L2_gnn_in = {k: v for k, v in _L2_gnn_all.items() if k in ('Wh', 'bh', 'W_out', 'b_out')}
    del _L2_gnn_all

    def _L3_gnn_setup():
        import jax, jax.numpy as jnp
        import numpy as np
        key = jax.random.key(seed)
        k1, k2, k3 = jax.random.split(key, 3)
        B, N, D = (4, 4096, 64)
        X = jax.random.normal(k1, (B, N, D), dtype=jnp.float32)
        A = jax.random.uniform(k2, (N, N), dtype=jnp.float32)
        W = jax.random.truncated_normal(k3, -2.0, 2.0, (D, D), dtype=jnp.float32) * 0.05
        return {'X': X, 'A': A, 'W': W}
    _L3_gnn_all = _L3_gnn_setup()
    _L3_gnn_in = {k: v for k, v in _L3_gnn_all.items() if k in ('W',)}
    del _L3_gnn_all
    return {'x': x, 'adj': adj, 'L0_gnn_H': _L0_gnn_in['H'], 'L0_gnn_W': _L0_gnn_in['W'], 'L0_gnn_W_ind': _L0_gnn_in['W_ind'], 'L0_gnn_a_node': _L0_gnn_in['a_node'], 'L0_gnn_a_gn': _L0_gnn_in['a_gn'], 'L0_gnn_a_ge': _L0_gnn_in['a_ge'], 'L0_gnn_fcW': _L0_gnn_in['fcW'], 'L0_gnn_fcb': _L0_gnn_in['fcb'], 'L0_gnn_av': _L0_gnn_in['av'], 'L1_gnn_intervention_value': _L1_gnn_in['intervention_value'], 'L1_gnn_W1': _L1_gnn_in['W1'], 'L1_gnn_b1': _L1_gnn_in['b1'], 'L1_gnn_W2': _L1_gnn_in['W2'], 'L1_gnn_b2': _L1_gnn_in['b2'], 'L2_gnn_Wh': _L2_gnn_in['Wh'], 'L2_gnn_bh': _L2_gnn_in['bh'], 'L2_gnn_W_out': _L2_gnn_in['W_out'], 'L2_gnn_b_out': _L2_gnn_in['b_out'], 'L3_gnn_W': _L3_gnn_in['W']}

def reference(x, adj, L0_gnn_H, L0_gnn_W, L0_gnn_W_ind, L0_gnn_a_node, L0_gnn_a_gn, L0_gnn_a_ge, L0_gnn_fcW, L0_gnn_fcb, L0_gnn_av, L1_gnn_intervention_value, L1_gnn_W1, L1_gnn_b1, L1_gnn_W2, L1_gnn_b2, L2_gnn_Wh, L2_gnn_bh, L2_gnn_W_out, L2_gnn_b_out, L3_gnn_W):
    import jax
    import jax.numpy as jnp

    def _L0_gnn_ref(x, H, adj, nhid, W, W_ind, a_node, a_gn, a_ge, fcW, fcb, av):
        import jax, jax.numpy as jnp
        import numpy as np
        NEG = -1000000000.0
        h = x @ W
        maskEN = H.T
        s = jax.nn.leaky_relu(h @ a_node, 0.2)
        logits = jnp.where(maskEN[None, :, :] > 0, s[:, None, :], NEG)
        alpha = jax.nn.softmax(logits, axis=-1)
        agg = jnp.einsum('ben,bnf->bef', alpha, h)
        beta = jax.nn.sigmoid((h @ a_gn)[:, None, :] + (agg @ a_ge)[:, :, None])
        all_he = beta[..., None] * h[:, None, :, :] + (1.0 - beta[..., None]) * agg[:, :, None, :]
        deg = jnp.maximum(adj.sum(-1), 1.0)[:, None]
        industry = jnp.einsum('nm,bmf->bnf', adj / deg, x @ W_ind)
        all_he = jax.nn.elu(all_he)
        he = jax.nn.elu(agg)

        def attn_scores(f):
            return jnp.tanh(f @ fcW + fcb) @ av
        se = attn_scores(he)
        logits2 = jnp.where(H[None, :, :] > 0, se[:, None, :], NEG)
        coefs1 = jax.nn.softmax(logits2, axis=-1)
        g = jnp.einsum('bne,benf->bnf', coefs1, all_he)
        pair = jnp.stack([industry, g], axis=2)
        coefs2 = jax.nn.softmax(attn_scores(pair), axis=-1)
        out = jnp.einsum('bnk,bnkf->bnf', coefs2, pair)
        return out

    def _L1_gnn_ref(causal_vars, adj_matrix, intervention_value, W1, b1, W2, b2, intervention_idx):
        import jax, jax.numpy as jnp
        import numpy as np
        MAX_STEPS = 3
        v = causal_vars.at[:, intervention_idx].set(intervention_value)
        for _ in range(MAX_STEPS):
            effects = jnp.einsum('nm,bmd->bnd', adj_matrix, v)
            h = jnp.concatenate([v, effects], axis=-1)
            h = jax.nn.relu(jnp.einsum('bnk,dk->bnd', h, W1) + b1)
            v = jnp.einsum('bnk,dk->bnd', h, W2) + b2
        return v

    def _L2_gnn_ref(flow_x, graph, Wh, bh, W_out, b_out):
        import jax, jax.numpy as jnp
        import numpy as np
        NEG_INF = -1e+16

        def gat_layer(x, graph, W, b):
            h = x @ W
            s = jnp.einsum('bnd,bmd->bnm', h, h) * graph
            s = jnp.where(s == 0.0, NEG_INF, s)
            a = jax.nn.softmax(s, axis=2)
            return jnp.einsum('bnm,bmd->bnd', a, h) + b
        heads = jax.vmap(lambda W, b: gat_layer(flow_x, graph, W, b))(Wh, bh)
        H, B, N, D = heads.shape
        cat = jnp.moveaxis(heads, 0, 2).reshape(B, N, H * D)
        x = jax.nn.leaky_relu(cat, negative_slope=0.01)
        out = gat_layer(x, graph, W_out, b_out)
        return jax.nn.leaky_relu(out, negative_slope=0.01)

    def _L3_gnn_ref(X, A, W):
        import jax, jax.numpy as jnp
        import numpy as np
        n = A.shape[0]
        A_td = A + jnp.eye(n, dtype=A.dtype)
        deg = jnp.sum(A_td, axis=1)
        dinv = jax.lax.rsqrt(deg)
        A_hat = dinv[:, None] * A_td * dinv[None, :]
        H = jnp.einsum('bmd,nm->bnd', X, A_hat)
        X_p = jnp.einsum('bnd,kd->bnk', H, W)
        return X_p
    h = jnp.maximum(_layernorm(x, axis=-1), 0.0)
    x = x + _L0_gnn_ref(h, L0_gnn_H, adj, 64, L0_gnn_W, L0_gnn_W_ind, L0_gnn_a_node, L0_gnn_a_gn, L0_gnn_a_ge, L0_gnn_fcW, L0_gnn_fcb, L0_gnn_av)
    h = jnp.maximum(_layernorm(x, axis=-1), 0.0)
    x = x + _L1_gnn_ref(h, adj, L1_gnn_intervention_value, L1_gnn_W1, L1_gnn_b1, L1_gnn_W2, L1_gnn_b2, 0)
    h = jnp.maximum(_layernorm(x, axis=-1), 0.0)
    x = x + _L2_gnn_ref(h, adj, L2_gnn_Wh, L2_gnn_bh, L2_gnn_W_out, L2_gnn_b_out)
    h = jnp.maximum(_layernorm(x, axis=-1), 0.0)
    x = x + _L3_gnn_ref(h, adj, L3_gnn_W)
    return x

_drawn_inputs = setup_inputs


def setup_inputs(seed=0):
    import zlib

    import numpy as np

    out = dict(_drawn_inputs(seed))
    spreads = {'L0_gnn_fcb': (0.0, 1.838)}
    factors = {'L1_gnn_b1': 3.301, 'L2_gnn_b_out': 7.968, 'L3_gnn_W': 24.595, 'L0_gnn_H': 2.678}
    for name, (base, spread) in spreads.items():
        noise = np.random.default_rng([zlib.crc32(name.encode()), seed]).standard_normal(out[name].shape)
        drawn = base * np.exp(spread * noise) if base else spread * noise
        out[name] = jnp.asarray(drawn.astype(out[name].dtype))
    for name, factor in factors.items():
        out[name] = (out[name] * factor).astype(out[name].dtype)
    return out
```

```python
from contextlib import ExitStack

import concourse.bass as bass
from concourse import mybir

B, N, F = 8, 1024, 64
E = 64
P = 128
T = N // P
BF = B * F
BP = B // 2
HEADS, HID = 8, 128
HP = HEADS // 2
HALF = 512
EPS = 1e-5
NEG_EDGE = -1e9
NEG_GAT = -1e16
BASE_SLOTS = 10
SAFE_MAX = 104.0
MAX_STEPS = 3

fp32 = mybir.dt.float32
i32 = mybir.dt.int32
ALU = mybir.AluOpType
ACT = mybir.ActivationFunctionType
X = mybir.AxisListType.X


class Steps:

    def __init__(self, eng, sem):
        self.eng, self.sem, self.base, self.n = eng, sem, 0, 0

    def did(self, ins):
        ins.then_inc(self.sem, 1)
        self.n += 1
        return self.n

    def wait(self, back=0):
        self.eng.wait_ge(self.sem, self.base + (self.n - back))


def hyper_gat_stack(nc, x, adj, H, W, W_ind, a_node, a_gn, a_ge, fcW, fcb, av, iv, W1, b1, W2, b2,
                    Wh, bh, W_out, b_out, W3, out):
    life = ExitStack()
    with life:
        def sb(name, shape, dt=fp32, scope=life):
            return scope.enter_context(nc.sbuf_tensor(name, shape, dt))

        in_use = []

        def sem(name):
            in_use.append(nc.alloc_semaphore(name=name))
            return in_use[-1]

        def retire_semaphores():
            nc.clear_and_free_semaphores(list(in_use))
            in_use.clear()
            nc.all_engine_barrier()

        bank = [life.enter_context(nc.psum_tensor(f"bank{i}", [P, HALF], fp32)) for i in range(8)]

        xs = sb("xs", [P, T, BF])
        hn = sb("hn", [P, T, BF])
        hT = sb("hT", [P, BP, N])
        adjN = sb("adjN", [P, T, N])
        adjT = sb("adjT", [P, T, N])
        ident = sb("ident", [P, P])
        ln_sum = sb("ln_sum", [P, T * B])
        ln_std = sb("ln_std", [P, T * B])
        eps_col = sb("eps_col", [P, 1])
        one_col = sb("one_col", [P, 1])
        flags = sb("flags", [1, 2], i32)
        deg = sb("deg", [P, T])
        rows = sb("rows", [P, T])
        bd = sb("bd", [P, 4, P])
        b1_col = sb("b1_col", [P, 1])
        b2_col = sb("b2_col", [P, 1])
        b2_row = sb("b2_row", [P, F])
        bout_row = sb("bout_row", [P, F])

        def views(a):
            return a[:, :, :].rearrange("p t (b f) -> p (t b) f", b=B)

        def per_group(col):
            return col[:, :].unsqueeze(2).to_broadcast([P, T * B, F])

        def layernorm_stage(name, src_x, dst, scratch, adds=None):
            v_done, sq_done, std_done, mean_done = (sem(f"{name}_{s}") for s in ("v", "square", "std", "mean"))
            with nc.Block() as block:
                @block.vector
                def _(eng):
                    st = Steps(eng, v_done)
                    if adds is not None:
                        st.did(nc.vector.tensor_tensor(src_x[:, :, :], src_x[:, :, :], adds[:, :, :], ALU.add))
                        st.wait()
                    st.did(nc.vector.tensor_reduce(ln_sum[:, :], views(src_x), X, ALU.add))
                    st.wait()
                    st.did(nc.vector.tensor_scalar(ln_sum[:, :], ln_sum[:, :], 1.0 / F, None, ALU.mult))
                    st.wait()
                    nc.vector.tensor_tensor(views(dst), views(src_x), per_group(ln_sum), ALU.subtract)\
                        .then_inc(mean_done, 1)
                    eng.wait_ge(sq_done, 1)
                    st.did(nc.vector.tensor_reduce(ln_sum[:, :], views(scratch), X, ALU.add))
                    eng.wait_ge(std_done, 1)
                    st.did(nc.vector.reciprocal(ln_std[:, :], ln_std[:, :]))
                    st.wait()
                    st.did(nc.vector.scalar_tensor_tensor(views(dst), views(dst), 0.0, per_group(ln_std),
                                                          ALU.max, ALU.mult))
                    st.wait()

                @block.scalar
                def _(eng):
                    eng.wait_ge(mean_done, 1)
                    nc.scalar.activation(scratch[:, :, :], dst[:, :, :], ACT.Square).then_inc(sq_done, 1)
                    eng.wait_ge(v_done, 4 if adds is not None else 3)
                    nc.scalar.activation(ln_std[:, :], ln_sum[:, :], ACT.Sqrt, bias=eps_col[:, :], scale=1.0 / F)\
                        .then_inc(std_done, 1)

        def transpose_stage(name, groups):
            filled, emptied = sem(f"{name}_filled"), [sem(f"{name}_emptied{i}") for i in range(2)]
            with nc.Block() as block:
                @block.tensor
                def _(eng):
                    for i, (_, srcs) in enumerate(groups):
                        if i >= 4:
                            eng.wait_ge(emptied[i % 2], (i - 4) // 2 + 1)
                        for j, s in enumerate(srcs):
                            mm = nc.tensor.transpose(bank[i % 4][:, j * P:(j + 1) * P], s, ident[:, :])
                        mm.then_inc(filled, 1)

                @block.vector
                def _(eng):
                    for i in range(0, len(groups), 2):
                        eng.wait_ge(filled, i + 1)
                        nc.vector.tensor_copy(groups[i][0], bank[i % 4][:, :]).then_inc(emptied[0], 1)
                    eng.wait_ge(emptied[0], (len(groups) + 1) // 2)

                @block.scalar
                def _(eng):
                    for i in range(1, len(groups), 2):
                        eng.wait_ge(filled, i + 1)
                        nc.scalar.activation(groups[i][0], bank[i % 4][:, :], ACT.Copy).then_inc(emptied[1], 1)
                    eng.wait_ge(emptied[1], len(groups) // 2)

        def natural_to_transposed(src, dst):
            return [(dst[:, bp, h * HALF:(h + 1) * HALF],
                     [src[:, h * 4 + j, bp * P:(bp + 1) * P] for j in range(4)])
                    for bp in range(BP) for h in range(2)]

        l0 = ExitStack()
        H_s = sb("H_s", [P, T, E], scope=l0)
        rhsW = sb("rhsW", [P, 258], scope=l0)
        W_dup = sb("W_dup", [P, F], scope=l0)
        node_row = sb("node_row", [P, F], scope=l0)
        gn_row = sb("gn_row", [P, F], scope=l0)
        ge_row = sb("ge_row", [P, F], scope=l0)
        fcW_s = sb("fcW_s", [P, 2 * F], scope=l0)
        fcb_col = sb("fcb_col", [P, 1], scope=l0)
        av_col = sb("av_col", [P, 1], scope=l0)
        av_rep = sb("av_rep", [P, P], scope=l0)
        s_rep = sb("s_rep", [P, P], scope=l0)
        w_prod = sb("w_prod", [P, 2, F], scope=l0)
        w_cols = sb("w_cols", [P, 2], scope=l0)
        raw = sb("raw", [P, 4, P], scope=l0)

        loaded, zeroed, id_done, cst_done = sem("loaded"), sem("zeroed"), sem("id_done"), sem("cst_done")
        blocks_loaded = sem("blocks_loaded")
        with nc.Block() as block:
            n_loads = []

            @block.sync
            def _(eng):
                def load(dst, src):
                    eng.dma_start(dst, src).then_inc(loaded, 16)
                    n_loads.append(1)
                for t in range(T):
                    load(xs[:, t, :].rearrange("p (b f) -> p b f", b=B),
                         x[:, t * P:(t + 1) * P, :].rearrange("b p f -> p b f"))
                for t in range(0, T, 4):
                    load(adjN[:, t:t + 4, :], adj[t * P:(t + 4) * P, :].rearrange("(t p) m -> p t m", p=P))
                load(H_s[:, :, :], H.rearrange("(t p) e -> p t e", p=P))
                for h in range(2):
                    s = slice(h * F, (h + 1) * F)
                    load(W_dup[s, :], W)
                    load(fcW_s[s, :], fcW)
                    load(b1_col[s, :], b1.unsqueeze(1))
                    load(b2_col[s, :], b2.unsqueeze(1))
                for row, src in ((node_row, a_node), (gn_row, a_gn), (ge_row, a_ge), (b2_row, b2), (bout_row, b_out)):
                    load(row[:, :], src.unsqueeze(0).to_broadcast([P, F]))
                load(fcb_col[:, :], fcb.unsqueeze(1))
                load(av_col[:, :], av.unsqueeze(1))
                eng.wait_ge(loaded, 16 * len(n_loads))

            @block.gpsimd
            def _(eng):
                nc.gpsimd.memset(ident[:, :], 0.0).then_inc(id_done, 1)
                nc.gpsimd.memset(raw[:, :, :], 0.0).then_inc(zeroed, 1)
                nc.gpsimd.memset(rhsW[:, :], 0.0).then_inc(zeroed, 1)
                nc.gpsimd.memset(s_rep[:, :], 0.0).then_inc(zeroed, 1)
                nc.gpsimd.memset(eps_col[:, :], EPS).then_inc(cst_done, 1)
                nc.gpsimd.memset(one_col[:, :], 1.0).then_inc(cst_done, 1)
                nc.gpsimd.memset(flags[:, :], 0).then_inc(cst_done, 1)
                eng.wait_ge(id_done, 1)
                eng.affine_select(out=ident[:, :], in_=ident[:, :], compare_op=ALU.not_equal, fill=1.0,
                                  base=0, pattern=[[-1, P]], channel_multiplier=1).then_inc(id_done, 1)
                eng.wait_ge(id_done, 2)
                eng.wait_ge(cst_done, 3)

            @block.scalar
            def _(eng):
                eng.wait_ge(zeroed, 2)
                n = 0
                for h in range(2):
                    s = slice(h * F, (h + 1) * F)
                    for dst, src in ((raw[s, 0, s], W1[:, 0:F]), (raw[s, 1, s], W1[:, F:2 * F]),
                                     (raw[s, 2, s], W2), (raw[s, 3, s], W3),
                                     (rhsW[s, s], W), (rhsW[s, 130 + h * F:130 + (h + 1) * F], W_ind)):
                        eng.dma_start(dst, src).then_inc(blocks_loaded, 16)
                        n += 16
                eng.wait_ge(blocks_loaded, n)

        v_done, p_tr = sem("cst_v"), sem("bd_transposed")
        with nc.Block() as block:
            @block.vector
            def _(eng):
                st = Steps(eng, v_done)
                st.did(nc.vector.tensor_tensor(w_prod[:, 0, :], W_dup[:, :], node_row[:, :], ALU.mult))
                st.did(nc.vector.tensor_tensor(w_prod[:, 1, :], W_dup[:, :], gn_row[:, :], ALU.mult))
                st.wait()
                st.did(nc.vector.tensor_reduce(w_cols[:, :], w_prod[:, :, :], X, ALU.add))
                st.wait()
                for h in range(2):
                    s = slice(h * F, (h + 1) * F)
                    st.did(nc.vector.tensor_copy(s_rep[s, s], w_cols[s, 0:1].to_broadcast([F, F])))
                    st.did(nc.vector.tensor_copy(rhsW[s, P + h:P + h + 1], w_cols[s, 1:2]))
                st.did(nc.vector.tensor_copy(av_rep[:, :], av_col[:, :].to_broadcast([P, P])))
                eng.wait_ge(p_tr, 1)
                st.did(nc.vector.tensor_copy(bd[:, :, :].rearrange("p a c -> p (a c)"), bank[0][:, :]))
                st.wait()

            @block.tensor
            def _(eng):
                for j in range(4):
                    mm = nc.tensor.transpose(bank[0][:, j * P:(j + 1) * P], raw[:, j, :], ident[:, :])
                mm.then_inc(p_tr, 1)

        transpose_stage("adj_t", [(adjT[:, mt, h * HALF:(h + 1) * HALF],
                                   [adjN[:, h * 4 + j, mt * P:(mt + 1) * P] for j in range(4)])
                                  for mt in range(T) for h in range(2)])

        hW = sb("hW", [P, T, BF], scope=l0)
        hWi = sb("hWi", [P, T, BF], scope=l0)
        acc = sb("acc", [P, T, BF], scope=l0)
        layernorm_stage("ln0", xs, hn, acc)
        transpose_stage("h0_t", natural_to_transposed(hn, hT))

        p_n = sb("p_n", [P, T, B], scope=l0)
        mx = sb("mx", [P, T, B], scope=l0)
        ne = sb("ne", [P, T], scope=l0)
        cnt = sb("cnt", [P, T], scope=l0)
        rankT = sb("rankT", [E, N], scope=l0)
        aggx = sb("aggx", [E, BF], scope=l0)
        qs = sb("qs", [E, 2, B], scope=l0)

        l0a = ExitStack()
        MN = sb("MN", [P, T, 2, E], scope=l0a)
        MT = sb("MT", [P, N], scope=l0a)
        NT = sb("NT", [P, N], scope=l0a)
        NN = sb("NN", [P, T, E], scope=l0a)
        cum = sb("cum", [P, T, E], scope=l0a)
        onesE = sb("onesE", [P, E], scope=l0a)
        cmax = sb("cmax", [P, 1], scope=l0a)

        proj_done, proj_v, proj_s = sem("proj_done"), sem("proj_v"), sem("proj_s")
        with nc.Block() as block:
            @block.tensor
            def _(eng):
                for i in range(T * BP):
                    t, bp = divmod(i, BP)
                    if i >= 4:
                        eng.wait_ge(proj_v, i - 3)
                        eng.wait_ge(proj_s, i - 3)
                    nc.tensor.matmul(bank[i % 4][:, 0:258], hT[:, bp, t * P:(t + 1) * P], rhsW[:, :],
                                     start=True, stop=True).then_inc(proj_done, 1)

            @block.vector
            def _(eng):
                for i in range(T * BP):
                    t, bp = divmod(i, BP)
                    eng.wait_ge(proj_done, i + 1)
                    nc.vector.tensor_copy(hWi[:, t, bp * P:(bp + 1) * P], bank[i % 4][:, 130:258]).then_inc(proj_v, 1)
                eng.wait_ge(proj_v, T * BP)

            @block.scalar
            def _(eng):
                for i in range(T * BP):
                    t, bp = divmod(i, BP)
                    eng.wait_ge(proj_v, i + 1)
                    nc.scalar.activation(p_n[:, t, bp * 2:bp * 2 + 2], bank[i % 4][:, 128:130], ACT.Copy)
                    nc.scalar.activation(hW[:, t, bp * P:(bp + 1) * P], bank[i % 4][:, 0:128], ACT.Copy)\
                        .then_inc(proj_s, 1)
                eng.wait_ge(proj_s, T * BP)

        m_done, mt_done, mt_s = sem("mask_done"), sem("mask_t_done"), sem("mask_s")
        with nc.Block() as block:
            @block.vector
            def _(eng):
                st = Steps(eng, m_done)
                for j in range(2):
                    st.did(nc.vector.tensor_scalar(MN[:, :, j, :], H_s[:, :, :], 0.0, None, ALU.is_gt))
                st.did(nc.vector.memset(onesE[:, :], 1.0))
                st.wait()
                st.did(nc.vector.tensor_scalar(NN[:, :, :], MN[:, :, 0, :], -1.0, -NEG_EDGE, ALU.add, ALU.mult))
                st.did(nc.vector.tensor_reduce(ne[:, :], MN[:, :, 0, :], X, ALU.add))
                st.did(nc.vector.tensor_reduce(rows[:, :], adjN[:, :, :], X, ALU.add))
                st.wait()
                st.did(nc.vector.tensor_scalar(ne[:, :], ne[:, :], 1.0, None, ALU.min))
                st.did(nc.vector.tensor_scalar(deg[:, :], rows[:, :], 1.0, None, ALU.max))
                st.wait()
                st.did(nc.vector.reciprocal(deg[:, :], deg[:, :]))
                st.did(nc.vector.tensor_scalar(cnt[:, :], ne[:, :], -1.0, 1.0, ALU.mult, ALU.add))
                st.wait()
                st.did(nc.vector.tensor_tensor(H_s[:, :, :], MN[:, :, 0, :],
                                               cnt[:, :].unsqueeze(2).to_broadcast([P, T, E]), ALU.max))
                st.wait()
                for t in range(T):
                    st.did(nc.vector.tensor_tensor_scan(cum[:, t, :], onesE[:, :], H_s[:, t, :], 0.0,
                                                        ALU.mult, ALU.add))
                st.wait()
                st.did(nc.vector.tensor_copy(cnt[:, :], cum[:, :, E - 1]))
                st.wait()
                st.did(nc.vector.tensor_tensor(cum[:, :, :], cum[:, :, :], H_s[:, :, :], ALU.mult))
                st.wait()
                st.did(nc.vector.tensor_reduce(cmax[:, :], cnt[:, :], X, ALU.max))
                eng.wait_ge(mt_done, 1)
                for h in range(2):
                    st.did(nc.vector.tensor_copy(MT[:, h * HALF:(h + 1) * HALF], bank[h][:, :]))
                    st.did(nc.vector.tensor_copy(rankT[:, h * HALF:(h + 1) * HALF], bank[2 + h][0:E, :]))
                st.wait()
                st.did(nc.vector.tensor_scalar(NT[:, :], MT[:, :], -1.0, -NEG_EDGE, ALU.add, ALU.mult))
                eng.wait_ge(mt_done, 2)
                st.did(nc.vector.tensor_reduce(cmax[0:1, :], bank[4][0:1, 0:P], X, ALU.max))
                st.wait()
                st.did(nc.vector.tensor_copy(flags[0:1, 0:1], cmax[0:1, :]))
                st.wait()

            @block.tensor
            def _(eng):
                eng.wait_ge(m_done, 22)
                for t in range(T):
                    h, j = divmod(t, 4)
                    nc.tensor.transpose(bank[h][:, j * P:(j + 1) * P],
                                        MN[:, t, :, :].rearrange("p a e -> p (a e)"), ident[:, :])
                    mm = nc.tensor.transpose(bank[2 + h][0:E, j * P:(j + 1) * P], cum[:, t, :], ident[:, :])
                mm.then_inc(mt_done, 1)
                nc.tensor.transpose(bank[4][0:1, 0:P], cmax[:, :], ident[:, :]).then_inc(mt_done, 1)

        LG = acc[:, :, :].rearrange("p (q c) n -> p q (c n)", c=2)
        alT = adjN[:, 0:BP, :].rearrange("p q (t e) -> p q t e", t=T)
        amax = sb("amax", [P, BP], scope=l0a)
        asum = sb("asum", [P, BP], scope=l0a)
        s_done, s_cp, a_v, a_pool, a_exp, a_tr, a_tc, a_agg, a_dots = (
            sem(f"alpha_{s}") for s in ("s", "cp", "v", "pool", "exp", "tr", "tc", "agg", "dots"))
        geb = sb("geb", [E, BF], scope=l0a)
        with nc.Block() as block:
            @block.tensor
            def _(eng):
                for i in range(BP * 2):
                    bp, h = divmod(i, 2)
                    if i >= 2:
                        eng.wait_ge(s_cp, i - 1)
                    nc.tensor.matmul(bank[h][:, :], s_rep[:, :], hT[:, bp, h * HALF:(h + 1) * HALF],
                                     start=True, stop=True).then_inc(s_done, 1)
                for i in range(BP * 2):
                    bp, h = divmod(i, 2)
                    if h == 0:
                        eng.wait_ge(a_exp, bp + 1)
                    if i >= 2:
                        eng.wait_ge(a_tc, i - 1)
                    for j in range(4):
                        t = h * 4 + j
                        mm = nc.tensor.transpose(bank[2 + h][:, j * P:(j + 1) * P],
                                                 LG[:, bp, t * P:(t + 1) * P], ident[:, :])
                    mm.then_inc(a_tr, 1)
                for bp in range(BP):
                    eng.wait_ge(a_tc, 2 * bp + 2)
                    for t in range(T):
                        mm = nc.tensor.matmul(bank[4 + bp][:, 0:P], alT[:, bp, t, :],
                                              hW[:, t, bp * P:(bp + 1) * P], start=t == 0, stop=t == T - 1)
                    mm.then_inc(a_agg, 1)

            @block.scalar
            def _(eng):
                for i in range(BP * 2):
                    bp, h = divmod(i, 2)
                    eng.wait_ge(s_done, i + 1)
                    nc.scalar.activation(LG[:, bp, h * HALF:(h + 1) * HALF], bank[h][:, :], ACT.Copy)\
                        .then_inc(s_cp, 1)
                for bp in range(BP):
                    eng.wait_ge(a_v, 3 * bp + 3)
                    nc.scalar.activation(LG[:, bp, :], LG[:, bp, :], ACT.Exp, bias=amax[:, bp:bp + 1],
                                         accum_out=asum[:, bp:bp + 1]).then_inc(a_exp, 1)
                for i in range(BP * 2):
                    bp, h = divmod(i, 2)
                    eng.wait_ge(a_tr, i + 1)
                    nc.scalar.activation(alT[:, bp, h * 4:h * 4 + 4, :].rearrange("p t e -> p (t e)"),
                                         bank[2 + h][:, :], ACT.Copy).then_inc(a_tc, 1)

            @block.gpsimd
            def _(eng):
                for bp in range(BP):
                    eng.wait_ge(a_v, 3 * bp + 1)
                    nc.gpsimd.tensor_tensor(LG[:, bp, :], LG[:, bp, :], MT[:, :], ALU.mult).then_inc(a_pool, 1)

            @block.vector
            def _(eng):
                st = Steps(eng, a_v)
                for bp in range(BP):
                    eng.wait_ge(s_cp, 2 * bp + 2)
                    st.did(nc.vector.scalar_tensor_tensor(LG[:, bp, :], LG[:, bp, :], 0.2, LG[:, bp, :],
                                                          ALU.mult, ALU.max))
                    eng.wait_ge(a_pool, bp + 1)
                    st.did(nc.vector.tensor_tensor(LG[:, bp, :], LG[:, bp, :], NT[:, :], ALU.add))
                    st.wait()
                    st.did(nc.vector.tensor_reduce(amax[:, bp:bp + 1], LG[:, bp, :], X, ALU.max, negate=True))
                eng.wait_ge(a_exp, BP)
                st.did(nc.vector.reciprocal(asum[:, :], asum[:, :]))
                st.wait()
                for bp in range(BP):
                    eng.wait_ge(a_agg, bp + 1)
                    for h in range(2):
                        b, s = 2 * bp + h, slice(h * E, (h + 1) * E)
                        st.did(nc.vector.tensor_scalar(aggx[:, b * F:(b + 1) * F], bank[4 + bp][s, s],
                                                       asum[s, bp:bp + 1], None, ALU.mult))
                st.wait()
                st.did(nc.vector.tensor_tensor(geb[:, :].rearrange("e (b f) -> e b f", b=B),
                                               aggx[:, :].rearrange("e (b f) -> e b f", b=B),
                                               ge_row[0:E, :].unsqueeze(1).to_broadcast([E, B, F]), ALU.mult))
                st.wait()
                st.did(nc.vector.tensor_reduce(qs[:, 0, :], geb[:, :].rearrange("e (b f) -> e b f", b=B), X, ALU.add))
                st.wait()

        heT = sb("heT", [P, BP, E], scope=l0a)
        th = sb("th", [P, 2, BP, E], scope=l0a)
        exg = sb("exg", [E, BF], scope=l0a)
        sc = adjN[:, BP:2 * BP, :].rearrange("p q (a b e) -> p (q a) b e", a=2, b=B)
        se_bc = sb("se_bc", [P, B, E], scope=l0a)
        e_exp, e_v, e_tr, e_z, e_th, e_se, e_sc = (sem(f"edge_{s}") for s in ("exp", "v", "tr", "z", "th", "se", "sc"))
        with nc.Block() as block:
            @block.scalar
            def _(eng):
                nc.scalar.activation(exg[:, :], aggx[:, :], ACT.Exp).then_inc(e_exp, 1)
                eng.wait_ge(e_z, 1)
                for h in range(2):
                    nc.scalar.activation(th[:, h, :, :].rearrange("k b e -> k (b e)"), bank[[1, 4][h]][:, 0:BP * E],
                                         ACT.Tanh, bias=fcb_col[:, :]).then_inc(e_th, 1)

            @block.tensor
            def _(eng):
                eng.wait_ge(e_v, 2)
                for bp in range(BP):
                    mm = nc.tensor.transpose(bank[0][:, bp * E:(bp + 1) * E], geb[:, bp * P:(bp + 1) * P],
                                             ident[0:E, 0:E])
                mm.then_inc(e_tr, 1)
                eng.wait_ge(e_v, 3)
                for h in range(2):
                    s = slice(h * F, (h + 1) * F)
                    mm = nc.tensor.matmul(bank[[1, 4][h]][:, 0:BP * E], fcW_s[s, :],
                                          heT[s, :, :].rearrange("f b e -> f (b e)"), start=True, stop=True)
                mm.then_inc(e_z, 1)
                eng.wait_ge(e_th, 2)
                nc.tensor.matmul(bank[2][:, :], av_rep[:, :], th[:, :, :, :].rearrange("k a b e -> k (a b e)"),
                                 start=True, stop=True)
                for b in range(B):
                    mm = nc.tensor.matmul(bank[3][0:E, b:b + 1], th[:, b % 2, b // 2, :], av_col[:, :],
                                          start=True, stop=True)
                mm.then_inc(e_se, 1)

            @block.vector
            def _(eng):
                st = Steps(eng, e_v)
                st.did(nc.vector.tensor_scalar(geb[:, :], aggx[:, :], 0.0, -1.0, ALU.max, ALU.add))
                eng.wait_ge(e_exp, 1)
                st.wait()
                st.did(nc.vector.scalar_tensor_tensor(geb[:, :], exg[:, :], 1.0, geb[:, :], ALU.min, ALU.add))
                eng.wait_ge(e_tr, 1)
                st.did(nc.vector.tensor_copy(heT[:, :, :].rearrange("f b e -> f (b e)"), bank[0][:, 0:BP * E]))
                eng.wait_ge(e_se, 1)
                st.did(nc.vector.tensor_copy(qs[:, 1, :], bank[3][0:E, 0:B]))
                st.did(nc.vector.tensor_copy(se_bc[:, :, :].rearrange("p (q a) e -> p a q e", a=2),
                                             bank[2][:, :].rearrange("p (a q e) -> p a q e", a=2, e=E)))
                st.wait()
                for t in range(T):
                    st.did(nc.vector.tensor_tensor(sc[:, t, :, :], se_bc[:, :, :],
                                                   MN[:, t, 0, :].unsqueeze(1).to_broadcast([P, B, E]), ALU.mult))
                st.wait()
                for t in range(T):
                    st.did(nc.vector.tensor_tensor(sc[:, t, :, :], sc[:, t, :, :],
                                                   NN[:, t, :].unsqueeze(1).to_broadcast([P, B, E]), ALU.add))
                st.wait()
                st.did(nc.vector.tensor_reduce(mx[:, :, :], sc[:, :, :, :], X, ALU.max))
                st.wait()

        l0a.close()

        l0b = ExitStack()
        kc = sb("kc", [P, 1], scope=l0b)
        zacc = sb("zacc", [P, T, B], scope=l0b)
        sel = sb("sel", [E, 2, N], scope=l0b)
        beta = sb("beta", [P, 2, T, B], scope=l0b)
        wgt = sb("wgt", [P, 2, T, B], scope=l0b)
        ex2 = sb("ex2", [P, 2, 2, T, B], scope=l0b)
        valid = sb("valid", [P, T], scope=l0b)
        R = 4
        dd, zz, ee = (adjN[:, 2 * i:2 * i + 2, :].rearrange("p q (a n) -> p (q a) n", a=2) for i in range(3))

        i_v = sem("init_v")
        with nc.Block() as block:
            @block.vector
            def _(eng):
                nc.vector.memset(acc[:, :, :], 0.0).then_inc(i_v, 1)
                nc.vector.memset(zacc[:, :, :], 0.0).then_inc(i_v, 1)
                nc.vector.memset(kc[:, :], 0.0).then_inc(i_v, 1)
                eng.wait_ge(i_v, 3)

        def slots_stage(name, count, guarded):
            sel_done, small_done, gath, small_v, exp2, b_done, d_done, d2_done, z_done, e_done, w_done, \
                wc_done, acc_done, kc_done, own_v = (sem(f"{name}_{s}") for s in (
                    "sel", "small", "gathered", "small_v", "exp2", "beta", "diff", "blend", "z", "elu_exp", "elu",
                    "weighed", "acc", "kc", "own_v"))

            def body(fn):
                def run(eng):
                    def loop():
                        with eng.Fori(0, count // 2) as i:
                            fn(eng, i)
                    if guarded:
                        need = eng.value_load(flags[0:1, 0:1], min_val=0, max_val=E)
                        with eng.If(need > BASE_SLOTS):
                            loop()
                    else:
                        loop()
                return run

            with nc.Block() as block:
                def pool(eng, i):
                    for u in range(2):
                        k = i * 2 + u
                        eng.wait_ge(b_done, k)
                        nc.gpsimd.tensor_tensor(kc[:, :], kc[:, :], one_col[:, :], ALU.add).then_inc(kc_done, 1)
                        eng.wait_ge(b_done, k + 1)
                        for s in range(T + 2):
                            if s < T:
                                t = s
                                eng.wait_ge(d_done, k * T + t + 1)
                                nc.gpsimd.tensor_tensor(
                                    dd[:, t % R, :].rearrange("p (b f) -> p b f", b=B),
                                    dd[:, t % R, :].rearrange("p (b f) -> p b f", b=B),
                                    beta[:, u, t, :].unsqueeze(2).to_broadcast([P, B, F]), ALU.mult)\
                                    .then_inc(d2_done, 1)
                            if s >= 2:
                                t = s - 2
                                eng.wait_ge(w_done, k * T + t + 1)
                                nc.gpsimd.tensor_tensor(
                                    ee[:, t % R, :].rearrange("p (b f) -> p b f", b=B),
                                    ee[:, t % R, :].rearrange("p (b f) -> p b f", b=B),
                                    wgt[:, u, t, :].unsqueeze(2).to_broadcast([P, B, F]), ALU.mult)\
                                    .then_inc(wc_done, 1)
                body_pool = body(pool)

                def tensor(eng, i):
                    for u in range(2):
                        k = i * 2 + u
                        eng.wait_ge(sel_done, k + 1)
                        eng.wait_ge(small_v, k)
                        for t in range(T):
                            mm = nc.tensor.matmul(bank[7][:, t * 16:(t + 1) * 16], sel[:, u, t * P:(t + 1) * P],
                                                  qs[:, :, :].rearrange("e a b -> e (a b)"), start=True, stop=True)
                        mm.then_inc(small_done, 1)
                        for t in range(T):
                            if t < R:
                                eng.wait_ge(z_done, k * T)
                            else:
                                eng.wait_ge(z_done, k * T + t - R + 1)
                            nc.tensor.matmul(bank[t % R][:, :], sel[:, u, t * P:(t + 1) * P], aggx[:, :],
                                             start=True, stop=True).then_inc(gath, 1)
                body_tensor = body(tensor)

                def scalar(eng, i):
                    for u in range(2):
                        k = i * 2 + u
                        eng.wait_ge(small_v, k + 1)
                        nc.scalar.activation(ex2[:, u, :, :, :].rearrange("p a t b -> p (a t b)"),
                                             ex2[:, u, :, :, :].rearrange("p a t b -> p (a t b)"), ACT.Exp)\
                            .then_inc(exp2, 1)
                        for t in range(T):
                            eng.wait_ge(z_done, k * T + t + 1)
                            if t < R:
                                eng.wait_ge(acc_done, k * T)
                            else:
                                eng.wait_ge(acc_done, k * T + t - R + 1)
                            nc.scalar.activation(ee[:, t % R, :], zz[:, t % R, :], ACT.Exp, bias=neg_one[:, :])\
                                .then_inc(e_done, 1)
                body_scalar = body(scalar)

                def vector(eng, i):
                    OWN = 6
                    for u in range(2):
                        k = i * 2 + u
                        eng.wait_ge(kc_done, k + 1)
                        eng.wait_ge(gath, k * T)
                        nc.vector.tensor_scalar(sel[:, u, :], rankT[:, :], kc[0:E, :], None, ALU.is_equal)\
                            .then_inc(sel_done, 1)
                        eng.wait_ge(small_done, k + 1)
                        sm = bank[7][:, 0:T * 16].rearrange("p (t a b) -> p a t b", a=2, b=B)
                        nc.vector.scalar_tensor_tensor(ex2[:, u, 0, :, :], sm[:, 0], -1.0, p_n[:, :, :],
                                                       ALU.mult, ALU.subtract).then_inc(own_v, 1)
                        nc.vector.tensor_tensor(ex2[:, u, 1, :, :], sm[:, 1], mx[:, :, :], ALU.subtract)\
                            .then_inc(own_v, 1)
                        eng.wait_ge(own_v, k * OWN + 2)
                        nc.vector.tensor_tensor(ex2[:, u, 1, :, :], ex2[:, u, 1, :, :],
                                                ne[:, :].unsqueeze(2).to_broadcast([P, T, B]), ALU.mult)\
                            .then_inc(small_v, 1)
                        eng.wait_ge(kc_done, k + 1)
                        nc.vector.tensor_scalar(valid[:, :], cnt[:, :], kc[:, :], None, ALU.is_ge).then_inc(own_v, 1)
                        eng.wait_ge(exp2, k + 1)
                        nc.vector.tensor_scalar(beta[:, u, :, :], ex2[:, u, 0, :, :], 1.0, None, ALU.add)\
                            .then_inc(own_v, 1)
                        eng.wait_ge(own_v, k * OWN + 4)
                        nc.vector.reciprocal(beta[:, u, :, :], beta[:, u, :, :]).then_inc(own_v, 1)
                        nc.vector.tensor_tensor(wgt[:, u, :, :], ex2[:, u, 1, :, :],
                                                valid[:, :].unsqueeze(2).to_broadcast([P, T, B]), ALU.mult)\
                            .then_inc(own_v, 1)
                        eng.wait_ge(own_v, k * OWN + 6)
                        nc.vector.tensor_tensor(zacc[:, :, :], zacc[:, :, :], wgt[:, u, :, :], ALU.add)\
                            .then_inc(b_done, 1)
                        for s in range(T + 3):
                            if s < T:
                                t = s
                                eng.wait_ge(gath, k * T + t + 1)
                                nc.vector.tensor_tensor(dd[:, t % R, :], hW[:, t, :], bank[t % R][:, :],
                                                        ALU.subtract).then_inc(d_done, 1)
                            if 1 <= s < T + 1:
                                t = s - 1
                                eng.wait_ge(d2_done, k * T + t + 1)
                                nc.vector.scalar_tensor_tensor(zz[:, t % R, :], dd[:, t % R, :], 1.0,
                                                               bank[t % R][:, :], ALU.add, ALU.add)\
                                    .then_inc(z_done, 1)
                            if 2 <= s < T + 2:
                                t = s - 2
                                eng.wait_ge(e_done, k * T + t + 1)
                                nc.vector.scalar_tensor_tensor(ee[:, t % R, :], ee[:, t % R, :], 1.0,
                                                               zz[:, t % R, :], ALU.min, ALU.max)\
                                    .then_inc(w_done, 1)
                            if s >= 3:
                                t = s - 3
                                eng.wait_ge(wc_done, k * T + t + 1)
                                nc.vector.tensor_tensor(acc[:, t, :], acc[:, t, :], ee[:, t % R, :], ALU.add)\
                                    .then_inc(acc_done, 1)
                    eng.wait_ge(acc_done, (i + 1) * 2 * T)
                body_vector = body(vector)

                block.gpsimd(body_pool)
                block.tensor(body_tensor)
                block.scalar(body_scalar)
                block.vector(body_vector)

        neg_one = sb("neg_one", [P, 1], scope=l0b)
        n1 = sem("neg_one_set")
        with nc.Block() as block:
            @block.vector
            def _(eng):
                nc.vector.memset(neg_one[:, :], -1.0).then_inc(n1, 1)
                eng.wait_ge(n1, 1)

        slots_stage("slots", BASE_SLOTS, False)
        slots_stage("more_slots", E - BASE_SLOTS, True)
        l0b_keep = zacc

        ind = hn
        i_done, i_read, g_v = sem("ind_done"), sem("ind_read"), sem("g_v")
        with nc.Block() as block:
            @block.tensor
            def _(eng):
                for nt in range(T):
                    for mt in range(T):
                        mm = nc.tensor.matmul(bank[nt][:, :], adjT[:, mt, nt * P:(nt + 1) * P], hWi[:, mt, :],
                                              start=mt == 0, stop=mt == T - 1)
                    mm.then_inc(i_done, 1)

            @block.scalar
            def _(eng):
                for nt in range(T):
                    eng.wait_ge(i_done, nt + 1)
                    nc.scalar.activation(ind[:, nt, :], bank[nt][:, :], ACT.Copy, scale=deg[:, nt:nt + 1])\
                        .then_inc(i_read, 1)
                eng.wait_ge(i_read, T)

            @block.vector
            def _(eng):
                st = Steps(eng, g_v)
                st.did(nc.vector.reciprocal(zacc[:, :, :], zacc[:, :, :]))
                st.wait()
                st.did(nc.vector.tensor_tensor(views(acc), views(acc),
                                               zacc[:, :, :].rearrange("p t b -> p (t b)").unsqueeze(2)
                                               .to_broadcast([P, T * B, F]), ALU.mult))
                st.wait()
                st.did(nc.vector.tensor_scalar(acc[:, :, :], acc[:, :, :], -1.0, None, ALU.add))
                st.wait()
        l0b.close()

        l0c = ExitStack()
        prT = sb("prT", [P, 2, HALF], scope=l0c)
        thp = sb("thp", [P, 2, HALF], scope=l0c)
        scp = sb("scp", [P, 2, T, B], scope=l0c)
        dif = sb("dif", [P, T, B], scope=l0c)
        for kind, src in enumerate((ind, acc)):
            transpose_stage(f"pair{kind}_t", natural_to_transposed(src, hT))
            z_d, th_d, sc_d, sc_c = (sem(f"pair{kind}_{s}") for s in ("z", "tanh", "score", "copied"))
            with nc.Block() as block:
                @block.tensor
                def _(eng):
                    def scores(i):
                        bp, h, a = i // 4, i // 2 % 2, i % 2
                        eng.wait_ge(th_d, i + 1)
                        for j in range(4):
                            t, b = h * 4 + j, 2 * bp + a
                            mm = nc.tensor.matmul(bank[4][:, t * B + b:t * B + b + 1],
                                                  thp[:, i % 2, j * P:(j + 1) * P], av_col[:, :],
                                                  start=True, stop=True)
                        mm.then_inc(sc_d, 1)
                    for i in range(BP * 4):
                        bp, h, a = i // 4, i // 2 % 2, i % 2
                        s = slice(a * F, (a + 1) * F)
                        if i >= 2:
                            eng.wait_ge(th_d, i - 1)
                        nc.tensor.matmul(bank[i % 2][:, :], fcW_s[s, :], hT[s, bp, h * HALF:(h + 1) * HALF],
                                         start=True, stop=True).then_inc(z_d, 1)
                        if i >= 1:
                            scores(i - 1)
                    scores(BP * 4 - 1)

                @block.scalar
                def _(eng):
                    for i in range(BP * 4):
                        eng.wait_ge(z_d, i + 1)
                        if i >= 2:
                            eng.wait_ge(sc_d, i - 1)
                        nc.scalar.activation(thp[:, i % 2, :], bank[i % 2][:, :], ACT.Tanh, bias=fcb_col[:, :])\
                            .then_inc(th_d, 1)

                @block.vector
                def _(eng):
                    eng.wait_ge(sc_d, BP * 4)
                    nc.vector.tensor_copy(scp[:, kind, :, :].rearrange("p t b -> p (t b)"),
                                          bank[4][:, 0:T * B]).then_inc(sc_c, 1)
                    eng.wait_ge(sc_c, 1)

        f_v, f_s = sem("mix_v"), sem("mix_s")
        with nc.Block() as block:
            @block.vector
            def _(eng):
                st = Steps(eng, f_v)
                st.did(nc.vector.tensor_tensor(dif[:, :, :], scp[:, 1, :, :], scp[:, 0, :, :], ALU.subtract))
                st.did(nc.vector.tensor_tensor(ind[:, :, :], ind[:, :, :], acc[:, :, :], ALU.subtract))
                st.did(nc.vector.tensor_tensor(xs[:, :, :], xs[:, :, :], acc[:, :, :], ALU.add))
                eng.wait_ge(f_s, 1)
                st.did(nc.vector.tensor_scalar(dif[:, :, :], dif[:, :, :], 1.0, None, ALU.add))
                st.wait()
                st.did(nc.vector.reciprocal(dif[:, :, :], dif[:, :, :]))
                st.wait()
                st.did(nc.vector.tensor_tensor(views(ind), views(ind),
                                               dif[:, :, :].rearrange("p t b -> p (t b)").unsqueeze(2)
                                               .to_broadcast([P, T * B, F]), ALU.mult))
                st.wait()
                st.did(nc.vector.tensor_tensor(xs[:, :, :], xs[:, :, :], ind[:, :, :], ALU.add))
                st.wait()

            @block.scalar
            def _(eng):
                eng.wait_ge(f_v, 1)
                nc.scalar.activation(dif[:, :, :], dif[:, :, :], ACT.Exp).then_inc(f_s, 1)
        l0c.close()
        l0.close()
        retire_semaphores()

        l1 = ExitStack()
        effT = sb("effT", [P, BP, N], scope=l1)
        hidT = sb("hidT", [P, BP, N], scope=l1)
        layernorm_stage("ln1", xs, hn, effT[:, :, :].rearrange("p b (c n) -> p (b c) n", c=2))
        iv_in, adj_in = sem("intervention_in"), sem("adj_in")
        with nc.Block() as block:
            @block.sync
            def _(eng):
                for b in range(B):
                    eng.dma_start(hn[0:1, 0, b * F:(b + 1) * F], iv).then_inc(iv_in, 16)
                eng.wait_ge(iv_in, 16 * B)

            @block.gpsimd
            def _(eng):
                for t in range(0, T, 4):
                    eng.dma_start(adjN[:, t:t + 4, :],
                                  adj[t * P:(t + 4) * P, :].rearrange("(t p) m -> p t m", p=P)).then_inc(adj_in, 16)
                eng.wait_ge(adj_in, 32)
        transpose_stage("v_t", natural_to_transposed(hn, hT))
        b2_b = b2_row[:, :].unsqueeze(1).to_broadcast([P, 2, F])

        e_d, e_c, h_d, h_c, v_d, v_c, n_d, n_c = (sem(f"l1_{s}") for s in (
            "effects", "effects_out", "hidden", "hidden_out", "vT", "vT_out", "v", "v_out"))
        G = BP * 2
        with nc.Block() as block:
            @block.tensor
            def _(eng):
                with eng.Fori(0, MAX_STEPS) as step:
                    eng.wait_ge(n_c, step * 4 * T)
                    for g in range(G):
                        bp, h = divmod(g, 2)
                        if g < 2:
                            eng.wait_ge(e_c, step * G)
                        else:
                            eng.wait_ge(e_c, step * G + g - 1)
                        for mt in range(T):
                            mm = nc.tensor.matmul(bank[g % 2][:, :], hn[:, mt, bp * P:(bp + 1) * P],
                                                  adjT[:, mt, h * HALF:(h + 1) * HALF],
                                                  start=mt == 0, stop=mt == T - 1)
                        mm.then_inc(e_d, 1)
                    for g in range(G):
                        bp, h = divmod(g, 2)
                        s = slice(h * HALF, (h + 1) * HALF)
                        if g == 0:
                            eng.wait_ge(v_c, step * G)
                        eng.wait_ge(e_c, step * G + g + 1)
                        if g < 2:
                            eng.wait_ge(h_c, step * G)
                        else:
                            eng.wait_ge(h_c, step * G + g - 1)
                        nc.tensor.matmul(bank[2 + g % 2][:, :], bd[:, 0, :], hT[:, bp, s], start=True, stop=False)
                        nc.tensor.matmul(bank[2 + g % 2][:, :], bd[:, 1, :], effT[:, bp, s], start=False, stop=True)\
                            .then_inc(h_d, 1)
                    for g in range(G):
                        bp, h = divmod(g, 2)
                        s = slice(h * HALF, (h + 1) * HALF)
                        eng.wait_ge(h_c, step * G + g + 1)
                        if g < 2:
                            eng.wait_ge(v_c, step * G)
                        else:
                            eng.wait_ge(v_c, step * G + g - 1)
                        nc.tensor.matmul(bank[4 + g % 2][:, :], bd[:, 2, :], hidT[:, bp, s], start=True, stop=True)\
                            .then_inc(v_d, 1)
                        for j in range(4):
                            q = g * 4 + j
                            if j == 0:
                                if g < 2:
                                    eng.wait_ge(n_c, step * 4 * T)
                                else:
                                    eng.wait_ge(n_c, step * 4 * T + (g - 1) * 4)
                            mm = nc.tensor.matmul(bank[6 + g % 2][:, j * P:(j + 1) * P],
                                                  hidT[:, bp, (h * 4 + j) * P:(h * 4 + j + 1) * P], bd[:, 2, :],
                                                  start=True, stop=True)
                        mm.then_inc(n_d, 1)

            @block.scalar
            def _(eng):
                with eng.Fori(0, MAX_STEPS) as step:
                    for g in range(G):
                        bp, h = divmod(g, 2)
                        eng.wait_ge(e_d, step * G + g + 1)
                        nc.scalar.activation(effT[:, bp, h * HALF:(h + 1) * HALF], bank[g % 2][:, :], ACT.Copy)\
                            .then_inc(e_c, 1)
                    for g in range(G):
                        bp, h = divmod(g, 2)
                        eng.wait_ge(h_d, step * G + g + 1)
                        nc.scalar.activation(hidT[:, bp, h * HALF:(h + 1) * HALF], bank[2 + g % 2][:, :], ACT.Relu,
                                             bias=b1_col[:, :]).then_inc(h_c, 1)
                    for g in range(G):
                        bp, h = divmod(g, 2)
                        eng.wait_ge(v_d, step * G + g + 1)
                        nc.scalar.activation(hT[:, bp, h * HALF:(h + 1) * HALF], bank[4 + g % 2][:, :], ACT.Identity,
                                             bias=b2_col[:, :]).then_inc(v_c, 1)

            @block.vector
            def _(eng):
                with eng.Fori(0, MAX_STEPS) as step:
                    for g in range(G):
                        bp, h = divmod(g, 2)
                        eng.wait_ge(n_d, step * G + g + 1)
                        for j in range(4):
                            t = h * 4 + j
                            nc.vector.tensor_tensor(
                                hn[:, t, bp * P:(bp + 1) * P].rearrange("p (a f) -> p a f", a=2),
                                bank[6 + g % 2][:, j * P:(j + 1) * P].rearrange("p (a f) -> p a f", a=2),
                                b2_b, ALU.add).then_inc(n_c, 1)
                eng.wait_ge(n_c, MAX_STEPS * 4 * T)
        l1.close()
        retire_semaphores()

        l2 = ExitStack()
        r2 = sb("r2", [P, T, BF], scope=l2)
        add_done = sem("add1")
        with nc.Block() as block:
            @block.vector
            def _(eng):
                nc.vector.tensor_tensor(xs[:, :, :], xs[:, :, :], hn[:, :, :], ALU.add).then_inc(add_done, 1)
                eng.wait_ge(add_done, 1)
        layernorm_stage("ln2", xs, hn, r2)

        Wh_s = sb("Wh_s", [P, HEADS, HID], scope=l2)
        Wo_s = sb("Wo_s", [P, HEADS, F], scope=l2)
        bh_s = sb("bh_s", [P, HEADS], scope=l2)
        GG = sb("GG", [F, HP, P], scope=l2)
        WT = sb("WT", [P, HEADS, F], scope=l2)
        w_in, w_t, w_tc, g_d, g_c = (sem(f"l2_{s}") for s in ("w", "wt", "wt_out", "g", "g_out"))
        with nc.Block() as block:
            @block.sync
            def _(eng):
                for h in range(2):
                    eng.dma_start(Wh_s[h * F:(h + 1) * F, :, :], Wh.rearrange("h f d -> f h d")).then_inc(w_in, 16)
                eng.dma_start(Wo_s[:, :, :], W_out.rearrange("(h d) o -> d h o", d=HID)).then_inc(w_in, 16)
                for h in range(HEADS):
                    eng.dma_start(bh_s[:, h:h + 1], bh[h, :].unsqueeze(1)).then_inc(w_in, 16)
                eng.wait_ge(w_in, 16 * (3 + HEADS))

            @block.tensor
            def _(eng):
                eng.wait_ge(w_in, 16 * (3 + HEADS))
                for h in range(HEADS):
                    mm = nc.tensor.transpose(bank[0][:, h * F:(h + 1) * F], Wh_s[0:F, h, :], ident[0:F, 0:F])
                mm.then_inc(w_t, 1)
                eng.wait_ge(w_tc, 1)
                for h in range(HEADS):
                    mm = nc.tensor.matmul(bank[1][0:F, h * F:(h + 1) * F], WT[:, h, :], WT[:, h, :],
                                          start=True, stop=True)
                mm.then_inc(g_d, 1)

            @block.vector
            def _(eng):
                eng.wait_ge(w_t, 1)
                nc.vector.tensor_copy(WT[:, :, :].rearrange("d h f -> d (h f)"), bank[0][:, :]).then_inc(w_tc, 1)
                eng.wait_ge(g_d, 1)
                nc.vector.tensor_copy(GG[:, :, :].rearrange("f a c -> f (a c)"), bank[1][0:F, :]).then_inc(g_c, 1)
                eng.wait_ge(g_c, 1)

        xb = sb("xb", [P, T, 2, F], scope=l2)
        V = sb("V", [P, T, F + 1], scope=l2)
        kT = sb("kT", [P, N], scope=l2)
        yT = sb("yT", [P, N], scope=l2)
        G_s = sb("G_s", [F, P], scope=l2)
        Wh_p = sb("Wh_p", [P, HID], scope=l2)
        Wo_p = sb("Wo_p", [P, 2, F], scope=l2)
        bh_p = sb("bh_p", [P, 2], scope=l2)
        U = sb("U", [P, 2, N], scope=l2)
        Pr = sb("Pr", [P, 2, N], scope=l2)
        PT = sb("PT", [P, 2, N], scope=l2)
        nm = sb("nm", [P, 2], scope=l2)
        rz = sb("rz", [P, 2], scope=l2)
        oh = sb("oh", [P, T, P], scope=l2)
        oT = sb("oT", [P, HALF], scope=l2)
        cat = sb("cat", [P, HALF], scope=l2)
        h2 = sb("h2", [P, T, F], scope=l2)
        lo = sb("lo", [P, 1], scope=l2)

        S_bank = [0, 2]
        OP, MP = bank[6], bank[7]

        def attention_stage(name, general):
            names = ("pool", "s", "u", "p", "tr", "tv", "ts", "o", "norm", "own", "x", "kt", "ktc", "y", "yc",
                     "ot", "otc", "cat", "catc", "catv", "h2", "h2c", "own2", "w")
            q = {n: sem(f"{name}_{n}") for n in names}
            UNROLL = 2 * T
            PER_B = HP * UNROLL + T

            def body(fn):
                def run(eng):
                    if general:
                        need = eng.value_load(flags[0:1, 1:2], min_val=0, max_val=1)
                        with eng.If(need > 0):
                            fn(eng)
                    else:
                        fn(eng)
                return run

            def tiles_tensor(eng, g0, tiles, y, k):
                def scores(i):
                    eng.wait_ge(q["u"], g0 + i)
                    for h in range(2):
                        mm = nc.tensor.matmul(bank[S_bank[i % 2] + h][:, :], y(i), k(i, h), start=True, stop=True)
                    mm.then_inc(q["s"], 1)

                def transposes(i):
                    eng.wait_ge(q["p"], g0 + i + 1)
                    for h in range(2):
                        eng.wait_ge(q["tv"] if h == 0 else q["ts"], g0 + i)
                        for j in range(4):
                            c = (h * 4 + j) * P
                            mm = nc.tensor.transpose(bank[4 + h][:, j * P:(j + 1) * P], Pr[:, i % 2, c:c + P],
                                                     ident[:, :])
                        mm.then_inc(q["tr"], 1)

                def values(i):
                    eng.wait_ge(q["tv"], g0 + i + 1)
                    eng.wait_ge(q["ts"], g0 + i + 1)
                    eng.wait_ge(q["norm"], g0 + i)
                    for mt in range(T):
                        mm = nc.tensor.matmul(OP[:, 0:F + 1], PT[:, i % 2, mt * P:(mt + 1) * P], V[:, mt, :],
                                              start=mt == 0, stop=mt == T - 1)
                    mm.then_inc(q["o"], 1)
                for s in range(tiles + 2):
                    if s < tiles:
                        scores(s)
                    if 1 <= s <= tiles:
                        transposes(s - 1)
                    if s >= 2:
                        values(s - 2)

            def tiles_scalar(eng, g0, tiles):
                for s in range(tiles + 1):
                    if s < tiles:
                        eng.wait_ge(q["u"], g0 + s + 2)
                        nc.scalar.activation(Pr[:, s % 2, :], U[:, s % 2, :], ACT.Exp, bias=nm[:, s % 2:s % 2 + 1])\
                            .then_inc(q["p"], 1)
                    if s >= 1:
                        i = s - 1
                        eng.wait_ge(q["tr"], (g0 + i) * 2 + 2)
                        eng.wait_ge(q["o"], g0 + i - 1 + 1) if i >= 1 else eng.wait_ge(q["o"], g0)
                        nc.scalar.activation(PT[:, i % 2, HALF:N], bank[5][:, :], ACT.Copy).then_inc(q["ts"], 1)

            def tiles_vector(eng, g0, tiles, row, out_of):
                OWN = 4 if general else 2
                for s in range(tiles + 2):
                    if s < tiles:
                        i, t = s, s % T
                        eng.wait_ge(q["s"], g0 + i + 1)
                        eng.wait_ge(q["p"], g0 + i - 1 if i >= 1 else g0)
                        m = nm[:, i % 2:i % 2 + 1]
                        sc2 = [bank[S_bank[i % 2] + h][:, :] for h in range(2)]
                        for h in range(2):
                            ins = nc.vector.tensor_tensor(U[:, i % 2, h * HALF:(h + 1) * HALF], sc2[h],
                                                          row(t)[:, h * HALF:(h + 1) * HALF], ALU.mult)
                        ins.then_inc(q["own"], 1)
                        eng.wait_ge(q["own"], (g0 + i) * OWN + 1)
                        n = 1
                        if general:
                            nc.vector.tensor_scalar(Pr[:, i % 2, :], U[:, i % 2, :], 0.0, NEG_GAT,
                                                    ALU.is_equal, ALU.mult).then_inc(q["own"], 1)
                            eng.wait_ge(q["own"], (g0 + i) * OWN + 2)
                            nc.vector.tensor_tensor(U[:, i % 2, :], U[:, i % 2, :], Pr[:, i % 2, :], ALU.add)\
                                .then_inc(q["own"], 1)
                            eng.wait_ge(q["own"], (g0 + i) * OWN + 3)
                            n = 3
                        nc.vector.tensor_reduce(m, U[:, i % 2, :], X, ALU.max, negate=True).then_inc(q["own"], 1)
                        eng.wait_ge(q["own"], (g0 + i) * OWN + n + 1)
                        nc.vector.tensor_tensor(lo[:, :], lo[:, :], m, ALU.max).then_inc(q["u"], 1)
                    if 1 <= s <= tiles:
                        i = s - 1
                        eng.wait_ge(q["tr"], (g0 + i) * 2 + 1)
                        eng.wait_ge(q["o"], g0 + i)
                        nc.vector.tensor_copy(PT[:, i % 2, 0:HALF], bank[4][:, :]).then_inc(q["tv"], 1)
                    if s >= 2:
                        i = s - 2
                        eng.wait_ge(q["o"], g0 + i + 1)
                        nc.vector.reciprocal(rz[:, i % 2:i % 2 + 1], OP[:, F:F + 1]).then_inc(q["own2"], 1)
                        eng.wait_ge(q["own2"], g0 + i + 1)
                        nc.vector.tensor_scalar(out_of(i), OP[:, 0:F], rz[:, i % 2:i % 2 + 1], None, ALU.mult)\
                            .then_inc(q["norm"], 1)

            with nc.Block() as block:
                def pool(eng):
                    nc.gpsimd.memset(V[:, :, F:F + 1], 1.0).then_inc(q["pool"], 1)
                    eng.wait_ge(q["pool"], 1)
                    with eng.Fori(0, B) as b:
                        eng.wait_ge(q["norm"], b * PER_B)
                        xv = hn[:, :, bass.ts(b, F)]
                        nc.gpsimd.tensor_copy(xb[:, :, 0, :], xv)
                        nc.gpsimd.tensor_copy(xb[:, :, 1, :], xv)
                        nc.gpsimd.tensor_copy(V[:, :, 0:F], xv).then_inc(q["x"], 1)
                block.gpsimd(body(pool))

                def keys_tensor(eng, n):
                    eng.wait_ge(q["x"], n + 1)
                    for h in range(2):
                        for j in range(4):
                            mm = nc.tensor.transpose(bank[4 + h][:, j * P:(j + 1) * P],
                                                     xb[:, h * 4 + j, :, :].rearrange("p a f -> p (a f)"),
                                                     ident[:, :])
                    mm.then_inc(q["kt"], 1)

                def tensor(eng):
                    with eng.Fori(0, B) as b:
                        keys_tensor(eng, b * 2)
                        with eng.Fori(0, HP) as hp:
                            n = b * HP + hp
                            eng.wait_ge(q["ktc"], b * 4 + 2)
                            eng.wait_ge(q["w"], (n + 1) * 5)
                            for h in range(2):
                                if h == 1:
                                    eng.wait_ge(q["yc"], n * 2 + 1)
                                else:
                                    eng.wait_ge(q["h2c"], n)
                                nc.tensor.matmul(MP[:, :], G_s[:, :], kT[0:F, h * HALF:(h + 1) * HALF],
                                                 start=True, stop=True).then_inc(q["y"], 1)
                            eng.wait_ge(q["yc"], n * 2 + 2)

                            def part(i):
                                return slice((i // T) * F, (i // T + 1) * F)
                            tiles_tensor(eng, b * PER_B + hp * UNROLL + 0, UNROLL,
                                         lambda i: yT[part(i), (i % T) * P:(i % T + 1) * P],
                                         lambda i, h: kT[part(i), h * HALF:(h + 1) * HALF])
                            eng.wait_ge(q["norm"], b * PER_B + (hp + 1) * UNROLL)
                            for h in range(2):
                                if h == 1:
                                    eng.wait_ge(q["otc"], n * 2 + 1)
                                for j in range(4):
                                    mm = nc.tensor.transpose(bank[4][:, j * P:(j + 1) * P], oh[:, h * 4 + j, :],
                                                             ident[:, :])
                                mm.then_inc(q["ot"], 1)
                                eng.wait_ge(q["otc"], n * 2 + h + 1)
                                for a in range(2):
                                    s = slice(a * F, (a + 1) * F)
                                    nc.tensor.matmul(bank[5][:, :], Wh_p[s, :], oT[s, :],
                                                     start=True, stop=True).then_inc(q["cat"], 1)
                                    eng.wait_ge(q["catv"], n * 4 + h * 2 + a + 1)
                                    for j in range(4):
                                        t = h * 4 + j
                                        mm = nc.tensor.matmul(
                                            bank[a * 2][:, t * F:(t + 1) * F],
                                            cat[:, j * P:(j + 1) * P], Wo_p[:, a, :], start=True, stop=True)
                                    mm.then_inc(q["h2"], 1)
                            eng.wait_ge(q["h2c"], n + 1)
                        keys_tensor(eng, b * 2 + 1)
                        eng.wait_ge(q["ktc"], b * 4 + 4)
                        tiles_tensor(eng, b * PER_B + HP * UNROLL, T,
                                     lambda i: kT[0:F, i * P:(i + 1) * P],
                                     lambda i, h: kT[0:F, h * HALF:(h + 1) * HALF])
                        eng.wait_ge(q["norm"], (b + 1) * PER_B)
                block.tensor(body(tensor))

                def scalar(eng):
                    with eng.Fori(0, B) as b:
                        with eng.Fori(0, HP) as hp:
                            n = b * HP + hp
                            eng.wait_ge(q["h2c"], n)
                            for dst, src in ((G_s[:, :], GG[:, hp, :]), (Wh_p[0:F, :], Wh_s[0:F, hp * 2, :]),
                                             (Wh_p[F:P, :], Wh_s[F:P, hp * 2 + 1, :]),
                                             (Wo_p[:, :, :], Wo_s[:, bass.ts(hp, 2), :]),
                                             (bh_p[:, :], bh_s[:, bass.ts(hp, 2)])):
                                nc.scalar.activation(dst, src, ACT.Copy).then_inc(q["w"], 1)
                            for h in range(2):
                                eng.wait_ge(q["y"], n * 2 + h + 1)
                                nc.scalar.activation(yT[:, h * HALF:(h + 1) * HALF], MP[:, :], ACT.Copy)\
                                    .then_inc(q["yc"], 1)
                            tiles_scalar(eng, b * PER_B + hp * UNROLL, UNROLL)
                            for c in range(4):
                                h, a = divmod(c, 2)
                                eng.wait_ge(q["cat"], n * 4 + c + 1)
                                eng.wait_ge(q["h2"], n * 4 + c)
                                eng.wait_ge(q["w"], (n + 1) * 5)
                                nc.scalar.activation(cat[:, :], bank[5][:, :], ACT.Identity, bias=bh_p[:, a:a + 1])\
                                    .then_inc(q["catc"], 1)
                        eng.wait_ge(q["h2c"], (b + 1) * HP)
                        for a in range(2):
                            nc.scalar.activation(xb[:, :, a, :], h2[:, :, :], ACT.Copy)
                        nc.scalar.activation(V[:, :, 0:F], h2[:, :, :], ACT.Copy).then_inc(q["x"], 1)
                        tiles_scalar(eng, b * PER_B + HP * UNROLL, T)
                block.scalar(body(scalar))

                def vector(eng):
                    def copy_keys(n):
                        eng.wait_ge(q["kt"], n + 1)
                        for h in range(2):
                            nc.vector.tensor_copy(kT[:, h * HALF:(h + 1) * HALF], bank[4 + h][:, :])\
                                .then_inc(q["ktc"], 1)

                    nc.vector.memset(lo[:, :], NEG_GAT * 4).then_inc(q["u"], 1)
                    eng.wait_ge(q["u"], 1)
                    with eng.Fori(0, B) as b:
                        copy_keys(b * 2)
                        nc.vector.memset(h2[:, :, :], 0.0).then_inc(q["h2z"], 1)
                        with eng.Fori(0, HP) as hp:
                            n = b * HP + hp
                            tiles_vector(eng, b * PER_B + hp * UNROLL, UNROLL, lambda t: adjN[:, t, :],
                                         lambda i: oh[:, i % T, (i // T) * F:(i // T + 1) * F])
                            for h in range(2):
                                eng.wait_ge(q["ot"], n * 2 + h + 1)
                                nc.vector.tensor_copy(oT[:, :], bank[4][:, :]).then_inc(q["otc"], 1)
                                for a in range(2):
                                    c = h * 2 + a
                                    eng.wait_ge(q["catc"], n * 4 + c + 1)
                                    nc.vector.scalar_tensor_tensor(cat[:, :], cat[:, :], 0.01, cat[:, :],
                                                                   ALU.mult, ALU.max).then_inc(q["catv"], 1)
                            eng.wait_ge(q["h2"], n * 4 + 4)
                            eng.wait_ge(q["h2z"], b + 1)
                            nc.vector.tensor_tensor(h2[:, :, :].rearrange("p t f -> p (t f)"),
                                                    h2[:, :, :].rearrange("p t f -> p (t f)"), bank[0][:, :],
                                                    ALU.add).then_inc(q["h2v"], 1)
                            eng.wait_ge(q["h2v"], n + 1)
                            nc.vector.tensor_tensor(h2[:, :, :].rearrange("p t f -> p (t f)"),
                                                    h2[:, :, :].rearrange("p t f -> p (t f)"), bank[2][:, :],
                                                    ALU.add).then_inc(q["h2c"], 1)
                            eng.wait_ge(q["h2c"], n + 1)
                        copy_keys(b * 2 + 1)
                        tiles_vector(eng, b * PER_B + HP * UNROLL, T, lambda t: adjN[:, t, :],
                                     lambda i: oh[:, i, 0:F])
                        eng.wait_ge(q["norm"], (b + 1) * PER_B)
                        nc.vector.tensor_tensor(oh[:, :, 0:F], oh[:, :, 0:F],
                                                bout_row[:, :].unsqueeze(1).to_broadcast([P, T, F]), ALU.add)\
                            .then_inc(q["fin"], 1)
                        eng.wait_ge(q["fin"], b * 2 + 1)
                        nc.vector.scalar_tensor_tensor(r2[:, :, bass.ts(b, F)], oh[:, :, 0:F], 0.01, oh[:, :, 0:F],
                                                       ALU.mult, ALU.max).then_inc(q["fin"], 1)
                        eng.wait_ge(q["fin"], b * 2 + 2)
                for n in ("h2z", "h2v", "fin"):
                    q[n] = sem(f"{name}_{n}")
                block.vector(body(vector))

        attention_stage("gat", False)

        lo_t, lo_v = sem("lo_t"), sem("lo_v")
        with nc.Block() as block:
            @block.tensor
            def _(eng):
                nc.tensor.transpose(bank[0][0:1, 0:P], lo[:, :], ident[:, :]).then_inc(lo_t, 1)

            @block.vector
            def _(eng):
                eng.wait_ge(lo_t, 1)
                nc.vector.tensor_reduce(lo[0:1, :], bank[0][0:1, 0:P], X, ALU.max).then_inc(lo_v, 1)
                eng.wait_ge(lo_v, 1)
                nc.vector.tensor_scalar(flags[0:1, 1:2], lo[0:1, :], -SAFE_MAX, None, ALU.is_gt).then_inc(lo_v, 1)
                eng.wait_ge(lo_v, 2)
        attention_stage("gat_any", True)

        layernorm_stage_add = sem("add2")
        with nc.Block() as block:
            @block.vector
            def _(eng):
                nc.vector.tensor_tensor(xs[:, :, :], xs[:, :, :], r2[:, :, :], ALU.add)\
                    .then_inc(layernorm_stage_add, 1)
                eng.wait_ge(layernorm_stage_add, 1)
        layernorm_stage("ln3", xs, hn, r2)
        l2.close()
        retire_semaphores()
        l3 = ExitStack()
        dinv = sb("dinv", [P, T], scope=l3)
        z3 = sb("z3", [P, T, BF], scope=l3)
        d_v, d_s = sem("dinv_v"), sem("dinv_s")
        transpose_stage("h3_t", natural_to_transposed(hn, hT))
        with nc.Block() as block:
            @block.vector
            def _(eng):
                eng.wait_ge(d_s, 1)
                nc.vector.reciprocal(dinv[:, :], dinv[:, :]).then_inc(d_v, 1)
                eng.wait_ge(d_v, 1)

            @block.scalar
            def _(eng):
                nc.scalar.activation(dinv[:, :], rows[:, :], ACT.Sqrt, bias=one_col[:, :]).then_inc(d_s, 1)

        z_d, z_c, a_d, a_v, f_v, o_d = (sem(f"l3_{s}") for s in ("z", "z_out", "az", "az_v", "sum_v", "stored"))
        with nc.Block() as block:
            @block.tensor
            def _(eng):
                for t in range(T):
                    if t >= 4:
                        eng.wait_ge(z_c, t - 3)
                    for bp in range(BP):
                        mm = nc.tensor.matmul(bank[t % 4][:, bp * P:(bp + 1) * P], hT[:, bp, t * P:(t + 1) * P],
                                              bd[:, 3, :], start=True, stop=True)
                    mm.then_inc(z_d, 1)
                eng.wait_ge(z_c, T)
                for nt in range(T):
                    if nt >= 4:
                        eng.wait_ge(a_v, (nt - 3) * 2)
                    for mt in range(T):
                        mm = nc.tensor.matmul(bank[4 + nt % 4][:, :], adjT[:, mt, nt * P:(nt + 1) * P],
                                              z3[:, mt, :], start=mt == 0, stop=mt == T - 1)
                    mm.then_inc(a_d, 1)

            @block.scalar
            def _(eng):
                for t in range(T):
                    eng.wait_ge(z_d, t + 1)
                    nc.scalar.activation(z3[:, t, :], bank[t % 4][:, :], ACT.Copy, scale=dinv[:, t:t + 1])\
                        .then_inc(z_c, 1)

            @block.vector
            def _(eng):
                eng.wait_ge(z_c, T)
                for nt in range(T):
                    eng.wait_ge(a_d, nt + 1)
                    nc.vector.tensor_tensor(hn[:, nt, :], bank[4 + nt % 4][:, :], z3[:, nt, :], ALU.add)\
                        .then_inc(a_v, 1)
                    eng.wait_ge(a_v, nt * 2 + 1)
                    nc.vector.scalar_tensor_tensor(xs[:, nt, :], hn[:, nt, :], dinv[:, nt:nt + 1], xs[:, nt, :],
                                                   ALU.mult, ALU.add).then_inc(a_v, 1)

            @block.sync
            def _(eng):
                for t in range(T):
                    eng.wait_ge(a_v, t * 2 + 2)
                    eng.dma_start(out[:, t * P:(t + 1) * P, :].rearrange("b p f -> p b f"),
                                  xs[:, t, :].rearrange("p (b f) -> p b f", b=B)).then_inc(o_d, 16)
                eng.wait_ge(o_d, 16 * T)
        l3.close()


_INS = ["x", "adj", "L0_gnn_H", "L0_gnn_W", "L0_gnn_W_ind", "L0_gnn_a_node", "L0_gnn_a_gn", "L0_gnn_a_ge",
        "L0_gnn_fcW", "L0_gnn_fcb", "L0_gnn_av", "L1_gnn_intervention_value", "L1_gnn_W1", "L1_gnn_b1",
        "L1_gnn_W2", "L1_gnn_b2", "L2_gnn_Wh", "L2_gnn_bh", "L2_gnn_W_out", "L2_gnn_b_out", "L3_gnn_W"]


def kernel(**inputs):
    import numpy as _np
    import concourse.bacc as _bacc
    from concourse import mybir as _mybir
    from concourse.bass_utils import run_bass_kernel_spmd as _run

    nc = _bacc.Bacc("TRN2", target_bir_lowering=False, num_devices=1)
    arrays, args = {}, []
    for name in _INS:
        a = _np.ascontiguousarray(inputs[name])
        arrays[f"in_{name}_dram"] = a
        args.append(nc.dram_tensor(f"in_{name}_dram", a.shape, _mybir.dt.from_np(a.dtype), kind="ExternalInput").ap())
    out = nc.dram_tensor("out_dram", (B, N, F), _mybir.dt.float32, kind="ExternalOutput").ap()
    hyper_gat_stack(nc, *args, out)
    r = _run(nc, [arrays], core_ids=[0])
    return r.results[0]["out_dram"]
```

```python
from contextlib import ExitStack

import concourse.bass as bass
from concourse import mybir

B, N, F = 8, 1024, 64
E = 64
P = 128
T = N // P
BF = B * F
BP = B // 2
HEADS, HID = 8, 128
HP = HEADS // 2
HALF = 512
EPS = 1e-5
NEG_EDGE = -1e9
NEG_GAT = -1e16
BASE_SLOTS = 10
SAFE_MAX = 104.0
MAX_STEPS = 3

CAP = 512
CT = CAP // P

fp32 = mybir.dt.float32
bf16 = mybir.dt.bfloat16
i32 = mybir.dt.int32
ALU = mybir.AluOpType
ACT = mybir.ActivationFunctionType
X = mybir.AxisListType.X


class Steps:

    def __init__(self, eng, sem):
        self.eng, self.sem, self.base, self.n = eng, sem, 0, 0

    def did(self, ins):
        ins.then_inc(self.sem, 1)
        self.n += 1
        return self.n

    def wait(self, back=0):
        self.eng.wait_ge(self.sem, self.base + (self.n - back))


def hyper_gat_stack(nc, x, adj, H, W, W_ind, a_node, a_gn, a_ge, fcW, fcb, av, iv, W1, b1, W2, b2,
                    Wh, bh, W_out, b_out, W3, out):
    life = ExitStack()
    with life:
        def sb(name, shape, dt=fp32, scope=life):
            return scope.enter_context(nc.sbuf_tensor(name, shape, dt))

        in_use = []

        def sem(name):
            in_use.append(nc.alloc_semaphore(name=name))
            return in_use[-1]

        def retire_semaphores():
            nc.clear_and_free_semaphores(list(in_use))
            in_use.clear()
            nc.all_engine_barrier()

        ps = life.enter_context(nc.psum_tensor("ps", [P, 8, HALF], fp32))
        bank = [ps[:, i, :] for i in range(8)]

        xs = sb("xs", [P, T, BF])
        hn = sb("hn", [P, T, BF])
        hT = sb("hT", [P, BP, N])
        adjT = sb("adjT", [P, T, N])
        pos = sb("pos", [P, T, T])
        most = sb("most", [P, 2])
        ident = sb("ident", [P, P])
        ln_sum = sb("ln_sum", [P, T * B])
        ln_std = sb("ln_std", [P, T * B])
        eps_col = sb("eps_col", [P, 1])
        one_col = sb("one_col", [P, 1])
        flags = sb("flags", [1, 2], i32)
        deg = sb("deg", [P, T])
        rows = sb("rows", [P, T])
        bd = sb("bd", [P, 4, P])
        b1_col = sb("b1_col", [P, 1])
        b2_col = sb("b2_col", [P, 1])
        b2_row = sb("b2_row", [P, F])
        bout_row = sb("bout_row", [P, F])

        def views(a):
            return a[:, :, :].rearrange("p t (b f) -> p (t b) f", b=B)

        def per_group(col):
            return col[:, :].unsqueeze(2).to_broadcast([P, T * B, F])

        def layernorm_stage(name, src_x, dst, scratch, adds=None):
            v_done, sq_done, std_done, mean_done = (sem(f"{name}_{s}") for s in ("v", "square", "std", "mean"))
            with nc.Block() as block:
                @block.vector
                def _(eng):
                    st = Steps(eng, v_done)
                    if adds is not None:
                        st.did(nc.vector.tensor_tensor(src_x[:, :, :], src_x[:, :, :], adds[:, :, :], ALU.add))
                        st.wait()
                    st.did(nc.vector.tensor_reduce(ln_sum[:, :], views(src_x), X, ALU.add))
                    st.wait()
                    st.did(nc.vector.tensor_scalar(ln_sum[:, :], ln_sum[:, :], 1.0 / F, None, ALU.mult))
                    st.wait()
                    nc.vector.tensor_tensor(views(dst), views(src_x), per_group(ln_sum), ALU.subtract)\
                        .then_inc(mean_done, 1)
                    eng.wait_ge(sq_done, 1)
                    st.did(nc.vector.tensor_reduce(ln_sum[:, :], views(scratch), X, ALU.add))
                    eng.wait_ge(std_done, 1)
                    st.did(nc.vector.reciprocal(ln_std[:, :], ln_std[:, :]))
                    st.wait()
                    st.did(nc.vector.scalar_tensor_tensor(views(dst), views(dst), 0.0, per_group(ln_std),
                                                          ALU.max, ALU.mult))
                    st.wait()

                @block.scalar
                def _(eng):
                    eng.wait_ge(mean_done, 1)
                    nc.scalar.activation(scratch[:, :, :], dst[:, :, :], ACT.Square).then_inc(sq_done, 1)
                    eng.wait_ge(v_done, 4 if adds is not None else 3)
                    nc.scalar.activation(ln_std[:, :], ln_sum[:, :], ACT.Sqrt, bias=eps_col[:, :], scale=1.0 / F)\
                        .then_inc(std_done, 1)

        def transpose_stage(name, groups):
            filled, emptied = sem(f"{name}_filled"), [sem(f"{name}_emptied{i}") for i in range(2)]
            with nc.Block() as block:
                @block.tensor
                def _(eng):
                    for i, (_, srcs) in enumerate(groups):
                        if i >= 4:
                            eng.wait_ge(emptied[i % 2], (i - 4) // 2 + 1)
                        for j, s in enumerate(srcs):
                            mm = nc.tensor.transpose(bank[i % 4][:, j * P:(j + 1) * P], s, ident[:, :])
                        mm.then_inc(filled, 1)

                @block.vector
                def _(eng):
                    for i in range(0, len(groups), 2):
                        eng.wait_ge(filled, i + 1)
                        nc.vector.tensor_copy(groups[i][0], bank[i % 4][:, :]).then_inc(emptied[0], 1)
                    eng.wait_ge(emptied[0], (len(groups) + 1) // 2)

                @block.scalar
                def _(eng):
                    for i in range(1, len(groups), 2):
                        eng.wait_ge(filled, i + 1)
                        nc.scalar.activation(groups[i][0], bank[i % 4][:, :], ACT.Copy).then_inc(emptied[1], 1)
                    eng.wait_ge(emptied[1], len(groups) // 2)

        def natural_to_transposed(src, dst):
            return [(dst[:, bp, h * HALF:(h + 1) * HALF],
                     [src[:, h * 4 + j, bp * P:(bp + 1) * P] for j in range(4)])
                    for bp in range(BP) for h in range(2)]

        l0 = ExitStack()
        adjN = sb("adjN", [P, T, N], scope=l0)
        H_s = sb("H_s", [P, T, E], scope=l0)
        rhsW = sb("rhsW", [P, 258], scope=l0)
        W_dup = sb("W_dup", [P, F], scope=l0)
        node_row = sb("node_row", [P, F], scope=l0)
        gn_row = sb("gn_row", [P, F], scope=l0)
        ge_row = sb("ge_row", [P, F], scope=l0)
        fcW_s = sb("fcW_s", [P, 2 * F], scope=l0)
        fcb_col = sb("fcb_col", [P, 1], scope=l0)
        av_col = sb("av_col", [P, 1], scope=l0)
        av_rep = sb("av_rep", [P, P], scope=l0)
        s_rep = sb("s_rep", [P, P], scope=l0)
        w_prod = sb("w_prod", [P, 2, F], scope=l0)
        w_cols = sb("w_cols", [P, 2], scope=l0)
        raw = sb("raw", [P, 4, P], scope=l0)

        loaded, zeroed, id_done, cst_done = sem("loaded"), sem("zeroed"), sem("id_done"), sem("cst_done")
        blocks_loaded = sem("blocks_loaded")
        with nc.Block() as block:
            n_loads = []

            @block.sync
            def _(eng):
                def load(dst, src):
                    eng.dma_start(dst, src).then_inc(loaded, 16)
                    n_loads.append(1)
                for b in range(B):
                    load(xs[:, :, b * F:(b + 1) * F], x[b].rearrange("(p t) f -> p t f", t=T))
                load(adjN[:, :, :], adj.rearrange("(p t) m -> p t m", t=T))
                load(H_s[:, :, :], H.rearrange("(p t) e -> p t e", t=T))
                for h in range(2):
                    s = slice(h * F, (h + 1) * F)
                    load(W_dup[s, :], W)
                    load(fcW_s[s, :], fcW)
                    load(b1_col[s, :], b1.unsqueeze(1))
                    load(b2_col[s, :], b2.unsqueeze(1))
                for row, src in ((node_row, a_node), (gn_row, a_gn), (ge_row, a_ge), (b2_row, b2), (bout_row, b_out)):
                    load(row[:, :], src.unsqueeze(0).to_broadcast([P, F]))
                load(fcb_col[:, :], fcb.unsqueeze(1))
                load(av_col[:, :], av.unsqueeze(1))
                eng.wait_ge(loaded, 16 * len(n_loads))

            @block.gpsimd
            def _(eng):
                nc.gpsimd.memset(ident[:, :], 0.0).then_inc(id_done, 1)
                nc.gpsimd.memset(raw[:, :, :], 0.0).then_inc(zeroed, 1)
                nc.gpsimd.memset(rhsW[:, :], 0.0).then_inc(zeroed, 1)
                nc.gpsimd.memset(s_rep[:, :], 0.0).then_inc(zeroed, 1)
                nc.gpsimd.memset(eps_col[:, :], EPS).then_inc(cst_done, 1)
                nc.gpsimd.memset(one_col[:, :], 1.0).then_inc(cst_done, 1)
                nc.gpsimd.memset(flags[:, :], 0).then_inc(cst_done, 1)
                eng.wait_ge(id_done, 1)
                eng.affine_select(out=ident[:, :], in_=ident[:, :], compare_op=ALU.not_equal, fill=1.0,
                                  base=0, pattern=[[-1, P]], channel_multiplier=1).then_inc(id_done, 1)
                eng.wait_ge(id_done, 2)
                eng.wait_ge(cst_done, 3)

            @block.scalar
            def _(eng):
                eng.wait_ge(zeroed, 2)
                n = 0
                for h in range(2):
                    s = slice(h * F, (h + 1) * F)
                    for dst, src in ((raw[s, 0, s], W1[:, 0:F]), (raw[s, 1, s], W1[:, F:2 * F]),
                                     (raw[s, 2, s], W2), (raw[s, 3, s], W3),
                                     (rhsW[s, s], W), (rhsW[s, 130 + h * F:130 + (h + 1) * F], W_ind)):
                        eng.dma_start(dst, src).then_inc(blocks_loaded, 16)
                        n += 16
                eng.wait_ge(blocks_loaded, n)

        v_done, p_tr = sem("cst_v"), sem("bd_transposed")
        with nc.Block() as block:
            @block.vector
            def _(eng):
                st = Steps(eng, v_done)
                st.did(nc.vector.tensor_tensor(w_prod[:, 0, :], W_dup[:, :], node_row[:, :], ALU.mult))
                st.did(nc.vector.tensor_tensor(w_prod[:, 1, :], W_dup[:, :], gn_row[:, :], ALU.mult))
                st.wait()
                st.did(nc.vector.tensor_reduce(w_cols[:, :], w_prod[:, :, :], X, ALU.add))
                st.wait()
                for h in range(2):
                    s = slice(h * F, (h + 1) * F)
                    st.did(nc.vector.tensor_copy(s_rep[s, s], w_cols[s, 0:1].to_broadcast([F, F])))
                    st.did(nc.vector.tensor_copy(rhsW[s, P + h:P + h + 1], w_cols[s, 1:2]))
                st.did(nc.vector.tensor_copy(av_rep[:, :], av_col[:, :].to_broadcast([P, P])))
                eng.wait_ge(p_tr, 1)
                st.did(nc.vector.tensor_copy(bd[:, :, :].rearrange("p a c -> p (a c)"), bank[0][:, :]))
                st.wait()

            @block.tensor
            def _(eng):
                for j in range(4):
                    mm = nc.tensor.transpose(bank[0][:, j * P:(j + 1) * P], raw[:, j, :], ident[:, :])
                mm.then_inc(p_tr, 1)

        transpose_stage("adj_t", [(adjT[:, mt, h * HALF:(h + 1) * HALF],
                                   [adjN[:, h * 4 + j, mt:N:T] for j in range(4)])
                                  for mt in range(T) for h in range(2)])

        nb = ExitStack()
        adjR = sb("adjR", [P, T, N], bf16, scope=nb)
        anyf = sb("anyf", [P, T, T], scope=nb)
        anyb = sb("anyb", [P, T, T], bf16, scope=nb)
        tri = sb("tri", [P, P], bf16, scope=nb)
        oneb = sb("oneb", [P, P], bf16, scope=nb)
        nb_v, nb_g, nb_t, nb_s, nb_p = (sem(f"neighbours_{q}") for q in ("v", "tri", "counted", "rounded", "left"))
        with nc.Block() as block:
            @block.gpsimd
            def _(eng):
                nc.gpsimd.memset(tri[:, :], 1.0).then_inc(nb_g, 1)
                nc.gpsimd.memset(oneb[:, :], 1.0).then_inc(nb_g, 1)
                eng.wait_ge(nb_g, 2)
                eng.affine_select(out=tri[:, :], in_=tri[:, :], compare_op=ALU.is_ge, fill=0.0,
                                  base=0, pattern=[[1, P]], channel_multiplier=-1).then_inc(nb_g, 1)
                eng.wait_ge(nb_s, 1)
                nc.gpsimd.tensor_tensor(adjN[:, :, :], adjT[:, :, :], adjR[:, :, :], ALU.subtract).then_inc(nb_p, 1)
                eng.wait_ge(nb_p, 1)

            @block.scalar
            def _(eng):
                eng.wait_ge(nb_v, 1)
                nc.scalar.activation(adjR[:, :, :], adjT[:, :, :], ACT.Copy).then_inc(nb_s, 1)

            @block.tensor
            def _(eng):
                eng.wait_ge(nb_g, 3)
                eng.wait_ge(nb_v, 3)
                for mt in range(T):
                    for k in range(mt + 1):
                        mm = nc.tensor.matmul(bank[0][:, mt * T:(mt + 1) * T], (tri if k == mt else oneb)[:, :],
                                              anyb[:, k, :], start=k == 0, stop=k == mt)
                mm.then_inc(nb_t, 1)

            @block.vector
            def _(eng):
                st = Steps(eng, nb_v)
                st.did(nc.vector.tensor_reduce(rows[:, :], adjN[:, :, :], X, ALU.add))
                st.did(nc.vector.tensor_reduce(anyf[:, :, :], adjT[:, :, :].rearrange("p q (t n) -> p q t n", t=T),
                                               X, ALU.max, apply_absolute_value=True))
                st.wait()
                st.did(nc.vector.tensor_scalar(anyb[:, :, :], anyf[:, :, :], 0.0, None, ALU.is_gt))
                st.wait()
                eng.wait_ge(nb_t, 1)
                st.did(nc.vector.tensor_tensor(pos[:, :, :].rearrange("p q t -> p (q t)"), bank[0][:, 0:T * T],
                                               anyb[:, :, :].rearrange("p q t -> p (q t)"), ALU.mult))
                st.wait()
                st.did(nc.vector.tensor_reduce(most[:, 0:1], pos[:, :, :].rearrange("p q t -> p (q t)"), X, ALU.max))
                eng.wait_ge(nb_p, 1)
                st.did(nc.vector.tensor_reduce(most[:, 1:2], adjN[:, :, :].rearrange("p q n -> p (q n)"), X,
                                               ALU.max, apply_absolute_value=True))
                st.wait()
        nb.close()

        hW = sb("hW", [P, T, BF], scope=l0)
        hWi = sb("hWi", [P, T, BF], scope=l0)
        acc = sb("acc", [P, T, BF], scope=l0)
        layernorm_stage("ln0", xs, hn, acc)
        transpose_stage("h0_t", natural_to_transposed(hn, hT))

        p_n = sb("p_n", [P, T, B], scope=l0)
        mx = sb("mx", [P, T, B], scope=l0)
        ne = sb("ne", [P, T], scope=l0)
        cnt = sb("cnt", [P, T], scope=l0)
        rankT = sb("rankT", [E, N], scope=l0)
        aggx = sb("aggx", [E, BF], scope=l0)
        qs = sb("qs", [E, 2, B], scope=l0)

        l0a = ExitStack()
        MN = sb("MN", [P, T, 2, E], scope=l0a)
        MT = sb("MT", [P, N], scope=l0a)
        NT = sb("NT", [P, N], scope=l0a)
        NN = sb("NN", [P, T, E], scope=l0a)
        cum = sb("cum", [P, T, E], scope=l0a)
        onesE = sb("onesE", [P, E], scope=l0a)
        cmax = sb("cmax", [P, 1], scope=l0a)

        proj_done, proj_v, proj_s = sem("proj_done"), sem("proj_v"), sem("proj_s")
        with nc.Block() as block:
            @block.tensor
            def _(eng):
                for i in range(T * BP):
                    t, bp = divmod(i, BP)
                    if i >= 4:
                        eng.wait_ge(proj_v, i - 3)
                        eng.wait_ge(proj_s, i - 3)
                    nc.tensor.matmul(bank[i % 4][:, 0:258], hT[:, bp, t * P:(t + 1) * P], rhsW[:, :],
                                     start=True, stop=True).then_inc(proj_done, 1)

            @block.vector
            def _(eng):
                for i in range(T * BP):
                    t, bp = divmod(i, BP)
                    eng.wait_ge(proj_done, i + 1)
                    nc.vector.tensor_copy(hWi[:, t, bp * P:(bp + 1) * P], bank[i % 4][:, 130:258]).then_inc(proj_v, 1)
                eng.wait_ge(proj_v, T * BP)

            @block.scalar
            def _(eng):
                for i in range(T * BP):
                    t, bp = divmod(i, BP)
                    eng.wait_ge(proj_v, i + 1)
                    nc.scalar.activation(p_n[:, t, bp * 2:bp * 2 + 2], bank[i % 4][:, 128:130], ACT.Copy)
                    nc.scalar.activation(hW[:, t, bp * P:(bp + 1) * P], bank[i % 4][:, 0:128], ACT.Copy)\
                        .then_inc(proj_s, 1)
                eng.wait_ge(proj_s, T * BP)

        m_done, mt_done, mt_s = sem("mask_done"), sem("mask_t_done"), sem("mask_s")
        with nc.Block() as block:
            @block.vector
            def _(eng):
                st = Steps(eng, m_done)
                for j in range(2):
                    st.did(nc.vector.tensor_scalar(MN[:, :, j, :], H_s[:, :, :], 0.0, None, ALU.is_gt))
                st.did(nc.vector.memset(onesE[:, :], 1.0))
                st.wait()
                st.did(nc.vector.tensor_scalar(NN[:, :, :], MN[:, :, 0, :], -1.0, -NEG_EDGE, ALU.add, ALU.mult))
                st.did(nc.vector.tensor_reduce(ne[:, :], MN[:, :, 0, :], X, ALU.add))
                st.wait()
                st.did(nc.vector.tensor_scalar(ne[:, :], ne[:, :], 1.0, None, ALU.min))
                st.did(nc.vector.tensor_scalar(deg[:, :], rows[:, :], 1.0, None, ALU.max))
                st.wait()
                st.did(nc.vector.reciprocal(deg[:, :], deg[:, :]))
                st.did(nc.vector.tensor_scalar(cnt[:, :], ne[:, :], -1.0, 1.0, ALU.mult, ALU.add))
                st.wait()
                st.did(nc.vector.tensor_tensor(H_s[:, :, :], MN[:, :, 0, :],
                                               cnt[:, :].unsqueeze(2).to_broadcast([P, T, E]), ALU.max))
                st.wait()
                for t in range(T):
                    st.did(nc.vector.tensor_tensor_scan(cum[:, t, :], onesE[:, :], H_s[:, t, :], 0.0,
                                                        ALU.mult, ALU.add))
                st.wait()
                st.did(nc.vector.tensor_copy(cnt[:, :], cum[:, :, E - 1]))
                st.wait()
                st.did(nc.vector.tensor_tensor(cum[:, :, :], cum[:, :, :], H_s[:, :, :], ALU.mult))
                st.wait()
                st.did(nc.vector.tensor_reduce(cmax[:, :], cnt[:, :], X, ALU.max))
                eng.wait_ge(mt_done, 1)
                for h in range(2):
                    st.did(nc.vector.tensor_copy(MT[:, h * HALF:(h + 1) * HALF], bank[h][:, :]))
                    st.did(nc.vector.tensor_copy(rankT[:, h * HALF:(h + 1) * HALF], bank[2 + h][0:E, :]))
                st.wait()
                st.did(nc.vector.tensor_scalar(NT[:, :], MT[:, :], -1.0, -NEG_EDGE, ALU.add, ALU.mult))
                eng.wait_ge(mt_done, 2)
                st.did(nc.vector.tensor_reduce(cmax[0:1, :], bank[4][0:1, 0:P], X, ALU.max))
                st.wait()
                st.did(nc.vector.tensor_copy(flags[0:1, 0:1], cmax[0:1, :]))
                st.wait()

            @block.tensor
            def _(eng):
                eng.wait_ge(m_done, 21)
                for t in range(T):
                    h, j = divmod(t, 4)
                    nc.tensor.transpose(bank[h][:, j * P:(j + 1) * P],
                                        MN[:, t, :, :].rearrange("p a e -> p (a e)"), ident[:, :])
                    mm = nc.tensor.transpose(bank[2 + h][0:E, j * P:(j + 1) * P], cum[:, t, :], ident[:, :])
                mm.then_inc(mt_done, 1)
                nc.tensor.transpose(bank[4][0:1, 0:P], cmax[:, :], ident[:, :]).then_inc(mt_done, 1)

        LG = acc[:, :, :].rearrange("p (q c) n -> p q (c n)", c=2)
        alT = adjN[:, 0:BP, :].rearrange("p q (t e) -> p q t e", t=T)
        amax = sb("amax", [P, BP], scope=l0a)
        asum = sb("asum", [P, BP], scope=l0a)
        s_done, s_cp, a_v, a_pool, a_exp, a_tr, a_tc, a_agg, a_dots = (
            sem(f"alpha_{s}") for s in ("s", "cp", "v", "pool", "exp", "tr", "tc", "agg", "dots"))
        geb = sb("geb", [E, BF], scope=l0a)
        with nc.Block() as block:
            @block.tensor
            def _(eng):
                for i in range(BP * 2):
                    bp, h = divmod(i, 2)
                    if i >= 2:
                        eng.wait_ge(s_cp, i - 1)
                    nc.tensor.matmul(bank[h][:, :], s_rep[:, :], hT[:, bp, h * HALF:(h + 1) * HALF],
                                     start=True, stop=True).then_inc(s_done, 1)
                for i in range(BP * 2):
                    bp, h = divmod(i, 2)
                    if h == 0:
                        eng.wait_ge(a_exp, bp + 1)
                    if i >= 2:
                        eng.wait_ge(a_tc, i - 1)
                    for j in range(4):
                        t = h * 4 + j
                        mm = nc.tensor.transpose(bank[2 + h][:, j * P:(j + 1) * P],
                                                 LG[:, bp, t * P:(t + 1) * P], ident[:, :])
                    mm.then_inc(a_tr, 1)
                for bp in range(BP):
                    eng.wait_ge(a_tc, 2 * bp + 2)
                    for t in range(T):
                        mm = nc.tensor.matmul(bank[4 + bp][:, 0:P], alT[:, bp, t, :],
                                              hW[:, t, bp * P:(bp + 1) * P], start=t == 0, stop=t == T - 1)
                    mm.then_inc(a_agg, 1)

            @block.scalar
            def _(eng):
                for i in range(BP * 2):
                    bp, h = divmod(i, 2)
                    eng.wait_ge(s_done, i + 1)
                    nc.scalar.activation(LG[:, bp, h * HALF:(h + 1) * HALF], bank[h][:, :], ACT.Copy)\
                        .then_inc(s_cp, 1)
                for bp in range(BP):
                    eng.wait_ge(a_v, 3 * bp + 3)
                    nc.scalar.activation(LG[:, bp, :], LG[:, bp, :], ACT.Exp, bias=amax[:, bp:bp + 1],
                                         accum_out=asum[:, bp:bp + 1]).then_inc(a_exp, 1)
                for i in range(BP * 2):
                    bp, h = divmod(i, 2)
                    eng.wait_ge(a_tr, i + 1)
                    nc.scalar.activation(alT[:, bp, h * 4:h * 4 + 4, :].rearrange("p t e -> p (t e)"),
                                         bank[2 + h][:, :], ACT.Copy).then_inc(a_tc, 1)

            @block.gpsimd
            def _(eng):
                for bp in range(BP):
                    eng.wait_ge(a_v, 3 * bp + 1)
                    nc.gpsimd.tensor_tensor(LG[:, bp, :], LG[:, bp, :], MT[:, :], ALU.mult).then_inc(a_pool, 1)

            @block.vector
            def _(eng):
                st = Steps(eng, a_v)
                for bp in range(BP):
                    eng.wait_ge(s_cp, 2 * bp + 2)
                    st.did(nc.vector.scalar_tensor_tensor(LG[:, bp, :], LG[:, bp, :], 0.2, LG[:, bp, :],
                                                          ALU.mult, ALU.max))
                    eng.wait_ge(a_pool, bp + 1)
                    st.did(nc.vector.tensor_tensor(LG[:, bp, :], LG[:, bp, :], NT[:, :], ALU.add))
                    st.wait()
                    st.did(nc.vector.tensor_reduce(amax[:, bp:bp + 1], LG[:, bp, :], X, ALU.max, negate=True))
                eng.wait_ge(a_exp, BP)
                st.did(nc.vector.reciprocal(asum[:, :], asum[:, :]))
                st.wait()
                for bp in range(BP):
                    eng.wait_ge(a_agg, bp + 1)
                    for h in range(2):
                        b, s = 2 * bp + h, slice(h * E, (h + 1) * E)
                        st.did(nc.vector.tensor_scalar(aggx[:, b * F:(b + 1) * F], bank[4 + bp][s, s],
                                                       asum[s, bp:bp + 1], None, ALU.mult))
                st.wait()
                st.did(nc.vector.tensor_tensor(geb[:, :].rearrange("e (b f) -> e b f", b=B),
                                               aggx[:, :].rearrange("e (b f) -> e b f", b=B),
                                               ge_row[0:E, :].unsqueeze(1).to_broadcast([E, B, F]), ALU.mult))
                st.wait()
                st.did(nc.vector.tensor_reduce(qs[:, 0, :], geb[:, :].rearrange("e (b f) -> e b f", b=B), X, ALU.add))
                st.wait()

        heT = sb("heT", [P, BP, E], scope=l0a)
        th = sb("th", [P, 2, BP, E], scope=l0a)
        exg = sb("exg", [E, BF], scope=l0a)
        sc = adjN[:, BP:2 * BP, :].rearrange("p q (a b e) -> p (q a) b e", a=2, b=B)
        se_bc = sb("se_bc", [P, B, E], scope=l0a)
        e_exp, e_v, e_tr, e_z, e_th, e_se, e_sc = (sem(f"edge_{s}") for s in ("exp", "v", "tr", "z", "th", "se", "sc"))
        with nc.Block() as block:
            @block.scalar
            def _(eng):
                nc.scalar.activation(exg[:, :], aggx[:, :], ACT.Exp).then_inc(e_exp, 1)
                eng.wait_ge(e_z, 1)
                for h in range(2):
                    nc.scalar.activation(th[:, h, :, :].rearrange("k b e -> k (b e)"), bank[[1, 4][h]][:, 0:BP * E],
                                         ACT.Tanh, bias=fcb_col[:, :]).then_inc(e_th, 1)

            @block.tensor
            def _(eng):
                eng.wait_ge(e_v, 2)
                for bp in range(BP):
                    mm = nc.tensor.transpose(bank[0][:, bp * E:(bp + 1) * E], geb[:, bp * P:(bp + 1) * P],
                                             ident[0:E, 0:E])
                mm.then_inc(e_tr, 1)
                eng.wait_ge(e_v, 3)
                for h in range(2):
                    s = slice(h * F, (h + 1) * F)
                    mm = nc.tensor.matmul(bank[[1, 4][h]][:, 0:BP * E], fcW_s[s, :],
                                          heT[s, :, :].rearrange("f b e -> f (b e)"), start=True, stop=True)
                mm.then_inc(e_z, 1)
                eng.wait_ge(e_th, 2)
                nc.tensor.matmul(bank[2][:, :], av_rep[:, :], th[:, :, :, :].rearrange("k a b e -> k (a b e)"),
                                 start=True, stop=True)
                for b in range(B):
                    mm = nc.tensor.matmul(bank[3][0:E, b:b + 1], th[:, b % 2, b // 2, :], av_col[:, :],
                                          start=True, stop=True)
                mm.then_inc(e_se, 1)

            @block.vector
            def _(eng):
                st = Steps(eng, e_v)
                st.did(nc.vector.tensor_scalar(geb[:, :], aggx[:, :], 0.0, -1.0, ALU.max, ALU.add))
                eng.wait_ge(e_exp, 1)
                st.wait()
                st.did(nc.vector.scalar_tensor_tensor(geb[:, :], exg[:, :], 1.0, geb[:, :], ALU.min, ALU.add))
                eng.wait_ge(e_tr, 1)
                st.did(nc.vector.tensor_copy(heT[:, :, :].rearrange("f b e -> f (b e)"), bank[0][:, 0:BP * E]))
                eng.wait_ge(e_se, 1)
                st.did(nc.vector.tensor_copy(qs[:, 1, :], bank[3][0:E, 0:B]))
                st.did(nc.vector.tensor_copy(se_bc[:, :, :].rearrange("p (q a) e -> p a q e", a=2),
                                             bank[2][:, :].rearrange("p (a q e) -> p a q e", a=2, e=E)))
                st.wait()
                for t in range(T):
                    st.did(nc.vector.tensor_tensor(sc[:, t, :, :], se_bc[:, :, :],
                                                   MN[:, t, 0, :].unsqueeze(1).to_broadcast([P, B, E]), ALU.mult))
                st.wait()
                for t in range(T):
                    st.did(nc.vector.tensor_tensor(sc[:, t, :, :], sc[:, t, :, :],
                                                   NN[:, t, :].unsqueeze(1).to_broadcast([P, B, E]), ALU.add))
                st.wait()
                st.did(nc.vector.tensor_reduce(mx[:, :, :], sc[:, :, :, :], X, ALU.max))
                st.wait()

        l0a.close()

        l0b = ExitStack()
        kc = sb("kc", [P, 1], scope=l0b)
        zacc = sb("zacc", [P, T, B], scope=l0b)
        sel = sb("sel", [E, 2, N], scope=l0b)
        beta = sb("beta", [P, 2, T, B], scope=l0b)
        wgt = sb("wgt", [P, 2, T, B], scope=l0b)
        ex2 = sb("ex2", [P, 2, 2, T, B], scope=l0b)
        valid = sb("valid", [P, T], scope=l0b)
        R = 4
        dd, zz, ee = (adjN[:, 2 * i:2 * i + 2, :].rearrange("p q (a n) -> p (q a) n", a=2) for i in range(3))

        i_v = sem("init_v")
        with nc.Block() as block:
            @block.vector
            def _(eng):
                nc.vector.memset(acc[:, :, :], 0.0).then_inc(i_v, 1)
                nc.vector.memset(zacc[:, :, :], 0.0).then_inc(i_v, 1)
                nc.vector.memset(kc[:, :], 0.0).then_inc(i_v, 1)
                eng.wait_ge(i_v, 3)

        def slots_stage(name, count, guarded):
            sel_done, small_done, gath, small_v, exp2, b_done, d_done, d2_done, z_done, e_done, w_done, \
                wc_done, acc_done, kc_done, own_v = (sem(f"{name}_{s}") for s in (
                    "sel", "small", "gathered", "small_v", "exp2", "beta", "diff", "blend", "z", "elu_exp", "elu",
                    "weighed", "acc", "kc", "own_v"))

            def body(fn):
                def run(eng):
                    def loop():
                        with eng.Fori(0, count // 2) as i:
                            fn(eng, i)
                    if guarded:
                        need = eng.value_load(flags[0:1, 0:1], min_val=0, max_val=E)
                        with eng.If(need > BASE_SLOTS):
                            loop()
                    else:
                        loop()
                return run

            with nc.Block() as block:
                def pool(eng, i):
                    for u in range(2):
                        k = i * 2 + u
                        eng.wait_ge(b_done, k)
                        nc.gpsimd.tensor_tensor(kc[:, :], kc[:, :], one_col[:, :], ALU.add).then_inc(kc_done, 1)
                        eng.wait_ge(b_done, k + 1)
                        for s in range(T + 2):
                            if s < T:
                                t = s
                                eng.wait_ge(d_done, k * T + t + 1)
                                nc.gpsimd.tensor_tensor(
                                    dd[:, t % R, :].rearrange("p (b f) -> p b f", b=B),
                                    dd[:, t % R, :].rearrange("p (b f) -> p b f", b=B),
                                    beta[:, u, t, :].unsqueeze(2).to_broadcast([P, B, F]), ALU.mult)\
                                    .then_inc(d2_done, 1)
                            if s >= 2:
                                t = s - 2
                                eng.wait_ge(w_done, k * T + t + 1)
                                nc.gpsimd.tensor_tensor(
                                    ee[:, t % R, :].rearrange("p (b f) -> p b f", b=B),
                                    ee[:, t % R, :].rearrange("p (b f) -> p b f", b=B),
                                    wgt[:, u, t, :].unsqueeze(2).to_broadcast([P, B, F]), ALU.mult)\
                                    .then_inc(wc_done, 1)
                body_pool = body(pool)

                def tensor(eng, i):
                    for u in range(2):
                        k = i * 2 + u
                        eng.wait_ge(sel_done, k + 1)
                        eng.wait_ge(small_v, k)
                        for t in range(T):
                            mm = nc.tensor.matmul(bank[7][:, t * 16:(t + 1) * 16], sel[:, u, t * P:(t + 1) * P],
                                                  qs[:, :, :].rearrange("e a b -> e (a b)"), start=True, stop=True)
                        mm.then_inc(small_done, 1)
                        for t in range(T):
                            if t < R:
                                eng.wait_ge(z_done, k * T)
                            else:
                                eng.wait_ge(z_done, k * T + t - R + 1)
                            nc.tensor.matmul(bank[t % R][:, :], sel[:, u, t * P:(t + 1) * P], aggx[:, :],
                                             start=True, stop=True).then_inc(gath, 1)
                body_tensor = body(tensor)

                def scalar(eng, i):
                    for u in range(2):
                        k = i * 2 + u
                        eng.wait_ge(small_v, k + 1)
                        nc.scalar.activation(ex2[:, u, :, :, :].rearrange("p a t b -> p (a t b)"),
                                             ex2[:, u, :, :, :].rearrange("p a t b -> p (a t b)"), ACT.Exp)\
                            .then_inc(exp2, 1)
                        for t in range(T):
                            eng.wait_ge(z_done, k * T + t + 1)
                            if t < R:
                                eng.wait_ge(acc_done, k * T)
                            else:
                                eng.wait_ge(acc_done, k * T + t - R + 1)
                            nc.scalar.activation(ee[:, t % R, :], zz[:, t % R, :], ACT.Exp, bias=neg_one[:, :])\
                                .then_inc(e_done, 1)
                body_scalar = body(scalar)

                def vector(eng, i):
                    OWN = 6
                    for u in range(2):
                        k = i * 2 + u
                        eng.wait_ge(kc_done, k + 1)
                        eng.wait_ge(gath, k * T)
                        nc.vector.tensor_scalar(sel[:, u, :], rankT[:, :], kc[0:E, :], None, ALU.is_equal)\
                            .then_inc(sel_done, 1)
                        eng.wait_ge(small_done, k + 1)
                        sm = bank[7][:, 0:T * 16].rearrange("p (t a b) -> p a t b", a=2, b=B)
                        nc.vector.scalar_tensor_tensor(ex2[:, u, 0, :, :], sm[:, 0], -1.0, p_n[:, :, :],
                                                       ALU.mult, ALU.subtract).then_inc(own_v, 1)
                        nc.vector.tensor_tensor(ex2[:, u, 1, :, :], sm[:, 1], mx[:, :, :], ALU.subtract)\
                            .then_inc(own_v, 1)
                        eng.wait_ge(own_v, k * OWN + 2)
                        nc.vector.tensor_tensor(ex2[:, u, 1, :, :], ex2[:, u, 1, :, :],
                                                ne[:, :].unsqueeze(2).to_broadcast([P, T, B]), ALU.mult)\
                            .then_inc(small_v, 1)
                        eng.wait_ge(kc_done, k + 1)
                        nc.vector.tensor_scalar(valid[:, :], cnt[:, :], kc[:, :], None, ALU.is_ge).then_inc(own_v, 1)
                        eng.wait_ge(exp2, k + 1)
                        nc.vector.tensor_scalar(beta[:, u, :, :], ex2[:, u, 0, :, :], 1.0, None, ALU.add)\
                            .then_inc(own_v, 1)
                        eng.wait_ge(own_v, k * OWN + 4)
                        nc.vector.reciprocal(beta[:, u, :, :], beta[:, u, :, :]).then_inc(own_v, 1)
                        nc.vector.tensor_tensor(wgt[:, u, :, :], ex2[:, u, 1, :, :],
                                                valid[:, :].unsqueeze(2).to_broadcast([P, T, B]), ALU.mult)\
                            .then_inc(own_v, 1)
                        eng.wait_ge(own_v, k * OWN + 6)
                        nc.vector.tensor_tensor(zacc[:, :, :], zacc[:, :, :], wgt[:, u, :, :], ALU.add)\
                            .then_inc(b_done, 1)
                        for s in range(T + 3):
                            if s < T:
                                t = s
                                eng.wait_ge(gath, k * T + t + 1)
                                nc.vector.tensor_tensor(dd[:, t % R, :], hW[:, t, :], bank[t % R][:, :],
                                                        ALU.subtract).then_inc(d_done, 1)
                            if 1 <= s < T + 1:
                                t = s - 1
                                eng.wait_ge(d2_done, k * T + t + 1)
                                nc.vector.scalar_tensor_tensor(zz[:, t % R, :], dd[:, t % R, :], 1.0,
                                                               bank[t % R][:, :], ALU.add, ALU.add)\
                                    .then_inc(z_done, 1)
                            if 2 <= s < T + 2:
                                t = s - 2
                                eng.wait_ge(e_done, k * T + t + 1)
                                nc.vector.scalar_tensor_tensor(ee[:, t % R, :], ee[:, t % R, :], 1.0,
                                                               zz[:, t % R, :], ALU.min, ALU.max)\
                                    .then_inc(w_done, 1)
                            if s >= 3:
                                t = s - 3
                                eng.wait_ge(wc_done, k * T + t + 1)
                                nc.vector.tensor_tensor(acc[:, t, :], acc[:, t, :], ee[:, t % R, :], ALU.add)\
                                    .then_inc(acc_done, 1)
                    eng.wait_ge(acc_done, (i + 1) * 2 * T)
                body_vector = body(vector)

                block.gpsimd(body_pool)
                block.tensor(body_tensor)
                block.scalar(body_scalar)
                block.vector(body_vector)

        neg_one = sb("neg_one", [P, 1], scope=l0b)
        n1 = sem("neg_one_set")
        with nc.Block() as block:
            @block.vector
            def _(eng):
                nc.vector.memset(neg_one[:, :], -1.0).then_inc(n1, 1)
                eng.wait_ge(n1, 1)

        slots_stage("slots", BASE_SLOTS, False)
        slots_stage("more_slots", E - BASE_SLOTS, True)
        l0b_keep = zacc

        ind = hn
        i_done, i_read, g_v = sem("ind_done"), sem("ind_read"), sem("g_v")
        with nc.Block() as block:
            @block.tensor
            def _(eng):
                for nt in range(T):
                    for mt in range(T):
                        mm = nc.tensor.matmul(bank[nt][:, :], adjT[:, mt, nt * P:(nt + 1) * P], hWi[:, mt, :],
                                              start=mt == 0, stop=mt == T - 1)
                    mm.then_inc(i_done, 1)

            @block.scalar
            def _(eng):
                for nt in range(T):
                    eng.wait_ge(i_done, nt + 1)
                    nc.scalar.activation(ind[:, nt, :], bank[nt][:, :], ACT.Copy, scale=deg[:, nt:nt + 1])\
                        .then_inc(i_read, 1)
                eng.wait_ge(i_read, T)

            @block.vector
            def _(eng):
                st = Steps(eng, g_v)
                st.did(nc.vector.reciprocal(zacc[:, :, :], zacc[:, :, :]))
                st.wait()
                st.did(nc.vector.tensor_tensor(views(acc), views(acc),
                                               zacc[:, :, :].rearrange("p t b -> p (t b)").unsqueeze(2)
                                               .to_broadcast([P, T * B, F]), ALU.mult))
                st.wait()
                st.did(nc.vector.tensor_scalar(acc[:, :, :], acc[:, :, :], -1.0, None, ALU.add))
                st.wait()
        l0b.close()

        l0c = ExitStack()
        prT = sb("prT", [P, 2, HALF], scope=l0c)
        thp = sb("thp", [P, 2, HALF], scope=l0c)
        scp = sb("scp", [P, 2, T, B], scope=l0c)
        dif = sb("dif", [P, T, B], scope=l0c)
        for kind, src in enumerate((ind, acc)):
            transpose_stage(f"pair{kind}_t", natural_to_transposed(src, hT))
            z_d, th_d, sc_d, sc_c = (sem(f"pair{kind}_{s}") for s in ("z", "tanh", "score", "copied"))
            with nc.Block() as block:
                @block.tensor
                def _(eng):
                    def scores(i):
                        bp, h, a = i // 4, i // 2 % 2, i % 2
                        eng.wait_ge(th_d, i + 1)
                        for j in range(4):
                            t, b = h * 4 + j, 2 * bp + a
                            mm = nc.tensor.matmul(bank[4][:, t * B + b:t * B + b + 1],
                                                  thp[:, i % 2, j * P:(j + 1) * P], av_col[:, :],
                                                  start=True, stop=True)
                        mm.then_inc(sc_d, 1)
                    for i in range(BP * 4):
                        bp, h, a = i // 4, i // 2 % 2, i % 2
                        s = slice(a * F, (a + 1) * F)
                        if i >= 2:
                            eng.wait_ge(th_d, i - 1)
                        nc.tensor.matmul(bank[i % 2][:, :], fcW_s[s, :], hT[s, bp, h * HALF:(h + 1) * HALF],
                                         start=True, stop=True).then_inc(z_d, 1)
                        if i >= 1:
                            scores(i - 1)
                    scores(BP * 4 - 1)

                @block.scalar
                def _(eng):
                    for i in range(BP * 4):
                        eng.wait_ge(z_d, i + 1)
                        if i >= 2:
                            eng.wait_ge(sc_d, i - 1)
                        nc.scalar.activation(thp[:, i % 2, :], bank[i % 2][:, :], ACT.Tanh, bias=fcb_col[:, :])\
                            .then_inc(th_d, 1)

                @block.vector
                def _(eng):
                    eng.wait_ge(sc_d, BP * 4)
                    nc.vector.tensor_copy(scp[:, kind, :, :].rearrange("p t b -> p (t b)"),
                                          bank[4][:, 0:T * B]).then_inc(sc_c, 1)
                    eng.wait_ge(sc_c, 1)

        f_v, f_s = sem("mix_v"), sem("mix_s")
        with nc.Block() as block:
            @block.vector
            def _(eng):
                st = Steps(eng, f_v)
                st.did(nc.vector.tensor_tensor(dif[:, :, :], scp[:, 1, :, :], scp[:, 0, :, :], ALU.subtract))
                st.did(nc.vector.tensor_tensor(ind[:, :, :], ind[:, :, :], acc[:, :, :], ALU.subtract))
                st.did(nc.vector.tensor_tensor(xs[:, :, :], xs[:, :, :], acc[:, :, :], ALU.add))
                eng.wait_ge(f_s, 1)
                st.did(nc.vector.tensor_scalar(dif[:, :, :], dif[:, :, :], 1.0, None, ALU.add))
                st.wait()
                st.did(nc.vector.reciprocal(dif[:, :, :], dif[:, :, :]))
                st.wait()
                st.did(nc.vector.tensor_tensor(views(ind), views(ind),
                                               dif[:, :, :].rearrange("p t b -> p (t b)").unsqueeze(2)
                                               .to_broadcast([P, T * B, F]), ALU.mult))
                st.wait()
                st.did(nc.vector.tensor_tensor(xs[:, :, :], xs[:, :, :], ind[:, :, :], ALU.add))
                st.wait()

            @block.scalar
            def _(eng):
                eng.wait_ge(f_v, 1)
                nc.scalar.activation(dif[:, :, :], dif[:, :, :], ACT.Exp).then_inc(f_s, 1)
        l0c.close()
        l0.close()
        retire_semaphores()

        l1 = ExitStack()
        effT = sb("effT", [P, BP, N], scope=l1)
        hidT = sb("hidT", [P, BP, N], scope=l1)
        layernorm_stage("ln1", xs, hn, effT[:, :, :].rearrange("p b (c n) -> p (b c) n", c=2))
        iv_in = sem("intervention_in")
        with nc.Block() as block:
            @block.sync
            def _(eng):
                for b in range(B):
                    eng.dma_start(hn[0:1, 0, b * F:(b + 1) * F], iv).then_inc(iv_in, 16)
                eng.wait_ge(iv_in, 16 * B)
        transpose_stage("v_t", natural_to_transposed(hn, hT))
        b2_b = b2_row[:, :].unsqueeze(1).to_broadcast([P, 2, F])

        e_d, e_c, h_d, h_c, v_d, v_c, n_d, n_c = (sem(f"l1_{s}") for s in (
            "effects", "effects_out", "hidden", "hidden_out", "vT", "vT_out", "v", "v_out"))
        G = BP * 2
        with nc.Block() as block:
            @block.tensor
            def _(eng):
                with eng.Fori(0, MAX_STEPS) as step:
                    eng.wait_ge(n_c, step * 4 * T)
                    for g in range(G):
                        bp, h = divmod(g, 2)
                        if g < 2:
                            eng.wait_ge(e_c, step * G)
                        else:
                            eng.wait_ge(e_c, step * G + g - 1)
                        for mt in range(T):
                            mm = nc.tensor.matmul(bank[g % 2][:, :], hn[:, mt, bp * P:(bp + 1) * P],
                                                  adjT[:, mt, h * HALF:(h + 1) * HALF],
                                                  start=mt == 0, stop=mt == T - 1)
                        mm.then_inc(e_d, 1)
                    for g in range(G):
                        bp, h = divmod(g, 2)
                        s = slice(h * HALF, (h + 1) * HALF)
                        if g == 0:
                            eng.wait_ge(v_c, step * G)
                        eng.wait_ge(e_c, step * G + g + 1)
                        if g < 2:
                            eng.wait_ge(h_c, step * G)
                        else:
                            eng.wait_ge(h_c, step * G + g - 1)
                        nc.tensor.matmul(bank[2 + g % 2][:, :], bd[:, 0, :], hT[:, bp, s], start=True, stop=False)
                        nc.tensor.matmul(bank[2 + g % 2][:, :], bd[:, 1, :], effT[:, bp, s], start=False, stop=True)\
                            .then_inc(h_d, 1)
                    for g in range(G):
                        bp, h = divmod(g, 2)
                        s = slice(h * HALF, (h + 1) * HALF)
                        eng.wait_ge(h_c, step * G + g + 1)
                        if g < 2:
                            eng.wait_ge(v_c, step * G)
                        else:
                            eng.wait_ge(v_c, step * G + g - 1)
                        nc.tensor.matmul(bank[4 + g % 2][:, :], bd[:, 2, :], hidT[:, bp, s], start=True, stop=True)\
                            .then_inc(v_d, 1)
                        for j in range(4):
                            q = g * 4 + j
                            if j == 0:
                                if g < 2:
                                    eng.wait_ge(n_c, step * 4 * T)
                                else:
                                    eng.wait_ge(n_c, step * 4 * T + (g - 1) * 4)
                            mm = nc.tensor.matmul(bank[6 + g % 2][:, j * P:(j + 1) * P],
                                                  hidT[:, bp, (h * 4 + j) * P:(h * 4 + j + 1) * P], bd[:, 2, :],
                                                  start=True, stop=True)
                        mm.then_inc(n_d, 1)

            @block.scalar
            def _(eng):
                with eng.Fori(0, MAX_STEPS) as step:
                    for g in range(G):
                        bp, h = divmod(g, 2)
                        eng.wait_ge(e_d, step * G + g + 1)
                        nc.scalar.activation(effT[:, bp, h * HALF:(h + 1) * HALF], bank[g % 2][:, :], ACT.Copy)\
                            .then_inc(e_c, 1)
                    for g in range(G):
                        bp, h = divmod(g, 2)
                        eng.wait_ge(h_d, step * G + g + 1)
                        nc.scalar.activation(hidT[:, bp, h * HALF:(h + 1) * HALF], bank[2 + g % 2][:, :], ACT.Relu,
                                             bias=b1_col[:, :]).then_inc(h_c, 1)
                    for g in range(G):
                        bp, h = divmod(g, 2)
                        eng.wait_ge(v_d, step * G + g + 1)
                        nc.scalar.activation(hT[:, bp, h * HALF:(h + 1) * HALF], bank[4 + g % 2][:, :], ACT.Identity,
                                             bias=b2_col[:, :]).then_inc(v_c, 1)

            @block.vector
            def _(eng):
                with eng.Fori(0, MAX_STEPS) as step:
                    for g in range(G):
                        bp, h = divmod(g, 2)
                        eng.wait_ge(n_d, step * G + g + 1)
                        for j in range(4):
                            t = h * 4 + j
                            nc.vector.tensor_tensor(
                                hn[:, t, bp * P:(bp + 1) * P].rearrange("p (a f) -> p a f", a=2),
                                bank[6 + g % 2][:, j * P:(j + 1) * P].rearrange("p (a f) -> p a f", a=2),
                                b2_b, ALU.add).then_inc(n_c, 1)
                eng.wait_ge(n_c, MAX_STEPS * 4 * T)
        l1.close()
        retire_semaphores()

        l2 = ExitStack()
        r2 = sb("r2", [P, T, BF], scope=l2)
        add_done = sem("add1")
        with nc.Block() as block:
            @block.vector
            def _(eng):
                nc.vector.tensor_tensor(xs[:, :, :], xs[:, :, :], hn[:, :, :], ALU.add).then_inc(add_done, 1)
                eng.wait_ge(add_done, 1)
        layernorm_stage("ln2", xs, hn, r2)
        transpose_stage("h2_t", natural_to_transposed(hn, hT))

        Wh_s = sb("Wh_s", [P, HEADS, HID], scope=l2)
        Wo_s = sb("Wo_s", [P, HEADS, F], scope=l2)
        bh_s = sb("bh_s", [P, HEADS], scope=l2)
        GG = sb("GG", [F, HP, P], scope=l2)
        WT = r2[:, 0, :].rearrange("p (h f) -> p h f", h=HEADS)
        w_in, w_t, w_tc, g_d, g_c = (sem(f"l2_{s}") for s in ("w", "wt", "wt_out", "g", "g_out"))
        with nc.Block() as block:
            @block.sync
            def _(eng):
                for h in range(2):
                    eng.dma_start(Wh_s[h * F:(h + 1) * F, :, :], Wh.rearrange("h f d -> f h d")).then_inc(w_in, 16)
                eng.dma_start(Wo_s[:, :, :], W_out.rearrange("(h d) o -> d h o", d=HID)).then_inc(w_in, 16)
                for h in range(HEADS):
                    eng.dma_start(bh_s[:, h:h + 1], bh[h, :].unsqueeze(1)).then_inc(w_in, 16)
                eng.wait_ge(w_in, 16 * (3 + HEADS))

            @block.tensor
            def _(eng):
                eng.wait_ge(w_in, 16 * (3 + HEADS))
                for h in range(HEADS):
                    mm = nc.tensor.transpose(bank[0][:, h * F:(h + 1) * F], Wh_s[0:F, h, :], ident[0:F, 0:F])
                mm.then_inc(w_t, 1)
                eng.wait_ge(w_tc, 1)
                for h in range(HEADS):
                    mm = nc.tensor.matmul(bank[1][0:F, h * F:(h + 1) * F], WT[:, h, :], WT[:, h, :],
                                          start=True, stop=True)
                mm.then_inc(g_d, 1)

            @block.vector
            def _(eng):
                eng.wait_ge(w_t, 1)
                nc.vector.tensor_copy(WT[:, :, :].rearrange("d h f -> d (h f)"), bank[0][:, :]).then_inc(w_tc, 1)
                eng.wait_ge(g_d, 1)
                nc.vector.tensor_copy(GG[:, :, :].rearrange("f a c -> f (a c)"), bank[1][0:F, :]).then_inc(g_c, 1)
                eng.wait_ge(g_c, 1)

        lo = sb("lo", [P, 1], scope=l2)

        l2a = ExitStack()
        iota1 = sb("iota1", [P, CAP], scope=l2a)
        adjB = sb("adjB", [P, T, N], bf16, scope=l2a)
        idT = sb("idT", [P, 2, F], bf16, scope=l2a)
        xsp = [sb(f"x{j + 1}", [P, T, BF], bf16, scope=l2a) for j in range(3)]
        in_xs, in_hn = (a[:, :, :].rearrange("p t n -> p (t n)").bitcast(bf16)
                        .rearrange("p (a b c) -> p a b c", a=2, b=B) for a in (xs, hn))
        Sel = in_hn[:, 0]
        RA, RB, RC = in_xs[:, 0], in_xs[:, 1], in_hn[:, 1]
        LA, LC = (sb(f"L{c}", [P, 2, HEADS, P], bf16, scope=l2a) for c in "AC")
        Y1 = sb("Y1", [P, HEADS * P], bf16, scope=l2a)
        YR = sb("YR", [P, HEADS * P], scope=l2a)
        Y2 = sb("Y2", [F, HEADS * P], bf16, scope=l2a)
        GD = sb("GD", [F, HEADS, 2, F], scope=l2a)
        xq = sb("xq", [F, B, P], scope=l2a)
        adjc = sb("adjc", [P, CAP], scope=l2a)
        Vc = sb("Vc", [P, B, CT, F + 1], scope=l2a)
        Uc = sb("Uc", [P, 2, CAP], scope=l2a)
        iota_i = Uc[:, 0, :].bitcast(i32)
        Pc = sb("Pc", [P, 2, CAP], scope=l2a)
        PTc = sb("PTc", [P, 2, CAP], scope=l2a)
        mst = sb("mst", [P, B * HEADS], scope=l2a)
        nmc = sb("nmc", [P, 2], scope=l2a)
        rzc = sb("rzc", [P, 2], scope=l2a)
        tick = sb("tick", [P, 1], scope=l2a)
        ob = sb("ob", [P, 2, HEADS * F], scope=l2a)
        oTc = sb("oTc", [P, HALF], scope=l2a)
        catc = sb("catc", [P, HEADS, P], scope=l2a)
        bh_aq = sb("bh_aq", [P, HEADS], scope=l2a)

        c_g, c_v, c_s, c_s2, c_p = (sem(f"split_{n}") for n in ("consts", "v", "s", "adj", "p"))
        saved = nc.dram_tensor("saved", (2, P, T, BF), fp32).ap()
        c_out = sem("split_saved")
        with nc.Block() as block:
            @block.sync
            def _(eng):
                for j, a in enumerate((xs, hn)):
                    eng.dma_start(saved[j], a[:, :, :]).then_inc(c_out, 16)
                eng.wait_ge(c_out, 32)

            @block.gpsimd
            def _(eng):
                nc.gpsimd.iota(iota_i, pattern=[[1, CAP]], base=1, channel_multiplier=0).then_inc(c_g, 1)
                nc.gpsimd.memset(Vc[:, :, :, F:F + 1], 1.0).then_inc(c_g, 1)
                eng.wait_ge(c_s, 1)
                nc.gpsimd.tensor_tensor(r2[:, :, :], hn[:, :, :], xsp[0][:, :, :], ALU.subtract).then_inc(c_p, 1)
                eng.wait_ge(c_s, 2)
                eng.wait_ge(c_p, 1)
                nc.gpsimd.tensor_tensor(xsp[2][:, :, :], r2[:, :, :], xsp[1][:, :, :], ALU.subtract).then_inc(c_p, 1)
                eng.wait_ge(c_p, 2)
                eng.wait_ge(c_g, 2)

            @block.scalar
            def _(eng):
                nc.scalar.activation(xsp[0][:, :, :], hn[:, :, :], ACT.Copy).then_inc(c_s, 1)
                nc.scalar.activation(adjB[:, :, :], adjT[:, :, :], ACT.Copy).then_inc(c_s2, 1)
                eng.wait_ge(c_s2, 1)
                eng.wait_ge(c_p, 1)
                nc.scalar.activation(xsp[1][:, :, :], r2[:, :, :], ACT.Copy).then_inc(c_s, 1)

            @block.vector
            def _(eng):
                st = Steps(eng, c_v)
                st.did(nc.vector.memset(idT[:, :, :], 0.0))
                st.did(nc.vector.memset(lo[:, :], NEG_GAT * 4))
                for a in range(2):
                    st.did(nc.vector.tensor_copy(GD[:, :, a, :], GG[:, :, :].rearrange("f q (a c) -> f (q a) c", a=2)))
                    st.did(nc.vector.tensor_copy(bh_aq[:, a * HP:(a + 1) * HP], bh_s[:, a:HEADS:2]))
                st.wait()
                for a in range(2):
                    s = slice(a * F, (a + 1) * F)
                    st.did(nc.vector.tensor_copy(idT[s, a, :], ident[s, s]))
                eng.wait_ge(c_g, 1)
                st.did(nc.vector.tensor_copy(iota1[:, :], iota_i))
                st.wait()

        f = {n: sem(f"quick_{n}") for n in (
            "sel", "xq", "gathered", "ga", "gv", "adj", "adj_out", "v", "v_out",
            "y", "y1", "yr", "y2", "copied", "y3", "s", "u", "own", "p", "tr", "tr_out", "o", "rz", "norm",
            "ot", "ot_out", "cat", "bias", "leaky", "h2", "h2_out", "lo", "tmin")}
        J = B * HEADS
        O_bank = [bank[2], bank[5]]
        LAST = J + HEADS + 2

        with nc.Block() as block:
            @block.tensor
            def _(eng):
                with eng.Fori(0, T) as t:
                    for k in range(3 * BP):
                        bp, j = divmod(k, 3)
                        if k == 0:
                            eng.wait_ge(f["sel"], t * T + T)
                            eng.wait_ge(f["u"], t * J)
                            eng.wait_ge(f["norm"], t * J)
                            eng.wait_ge(f["tr_out"], t * J)
                        if k >= 4:
                            w, jj = divmod(k - 4, 3)
                            if jj == 0:
                                eng.wait_ge(f["ga"], t * BP + w + 1)
                            else:
                                eng.wait_ge(f["gv"], t * 2 * BP + 2 * w + jj)
                        for mt in range(T):
                            mm = nc.tensor.matmul(bank[k % 4], xsp[j][:, mt, bp * P:(bp + 1) * P], Sel[:, mt, :],
                                                  start=mt == 0, stop=mt == T - 1)
                        mm.then_inc(f["gathered"], 1)
                    for mt in range(T):
                        mm = nc.tensor.matmul(bank[4], adjB[:, mt, bass.ts(t, P)], Sel[:, mt, :],
                                              start=mt == 0, stop=mt == T - 1)
                    mm.then_inc(f["adj"], 1)
                    eng.wait_ge(f["ga"], (t + 1) * BP)
                    eng.wait_ge(f["gv"], (t + 1) * 2 * BP)
                    eng.wait_ge(f["norm"], t * J)
                    eng.wait_ge(f["h2_out"], t * B)
                    for w in range(BP):
                        if w == 3:
                            eng.wait_ge(f["v_out"], t * BP + 1)
                        for g in range(2 * CT):
                            b, c = 2 * w + g // CT, g % CT
                            cs = slice(c * P, (c + 1) * P)
                            dst = bank[[5, 6, 7, 5][w]][:, g * F:(g + 1) * F]
                            nc.tensor.matmul(dst, RA[:, b, cs], idT[:, 0, :], start=True, stop=False)
                            nc.tensor.matmul(dst, RB[:, b, cs], idT[:, 0, :], start=False, stop=False)
                            mm = nc.tensor.matmul(dst, RC[:, b, cs], idT[:, 1, :], start=False, stop=True)
                        mm.then_inc(f["v"], 1)

                    def queries(b):
                        if b == 0:
                            eng.wait_ge(f["xq"], (t + 1) * 2)
                            eng.wait_ge(f["v_out"], t * BP + 3)
                        else:
                            eng.wait_ge(f["yr"], t * B + b)
                            eng.wait_ge(f["h2_out"], t * B + max(b - 2, 0))
                        for h in range(HEADS):
                            mm = nc.tensor.matmul(bank[6 + h // 4][:, h % 4 * P:(h % 4 + 1) * P],
                                                  GD[:, h, :, :].rearrange("f a c -> f (a c)"), xq[:, b, :],
                                                  start=True, stop=True)
                        mm.then_inc(f["y"], 1)

                    queries(0)
                    eng.wait_ge(f["v_out"], (t + 1) * BP)
                    for j in range(LAST):
                        b, i = divmod(j, HEADS)
                        if j < J:
                            if i == 0:
                                eng.wait_ge(f["y2"], t * B + b + 1)
                                eng.wait_ge(f["copied"], t * B + b + 1)
                                eng.wait_ge(f["y3"], t * B + b + 1)
                            if j >= 2:
                                eng.wait_ge(f["u"], t * J + j - 1)
                            dst = bank[j % 2]
                            nc.tensor.matmul(dst, LA[:, b % 2, i, :], RA[:, b, :], start=True, stop=False)
                            nc.tensor.matmul(dst, LA[:, b % 2, i, :], RB[:, b, :], start=False, stop=False)
                            nc.tensor.matmul(dst, LC[:, b % 2, i, :], RC[:, b, :], start=False, stop=True)\
                                .then_inc(f["s"], 1)
                        if 2 <= j <= J + 1:
                            k = j - 2
                            eng.wait_ge(f["p"], t * J + k + 1)
                            if k >= 2:
                                eng.wait_ge(f["tr_out"], t * J + k - 1)
                            elif k == 1:
                                eng.wait_ge(f["adj_out"], t + 1)
                            for c in range(CT):
                                mm = nc.tensor.transpose(bank[3 + k % 2][:, c * P:(c + 1) * P],
                                                         Pc[:, k % 2, c * P:(c + 1) * P], ident[:, :])
                            mm.then_inc(f["tr"], 1)
                        if 3 <= j <= J + 2:
                            k = j - 3
                            eng.wait_ge(f["tr_out"], t * J + k + 1)
                            if k >= 2:
                                eng.wait_ge(f["norm"], t * J + k - 1)
                            for c in range(CT):
                                mm = nc.tensor.matmul(O_bank[k % 2][:, 0:F + 1], PTc[:, k % 2, c * P:(c + 1) * P],
                                                      Vc[:, k // HEADS, c, :], start=c == 0, stop=c == CT - 1)
                            mm.then_inc(f["o"], 1)
                        if i == 2 and b + 1 < B:
                            queries(b + 1)
                        w = b - 1
                        if 0 <= w < B:
                            if i == 4:
                                eng.wait_ge(f["norm"], t * J + b * HEADS)
                                eng.wait_ge(f["yr"], t * B + min(b + 2, B))
                                eng.wait_ge(f["y1"], t * B + min(b + 2, B))
                                eng.wait_ge(f["h2_out"], t * B + max(b - 1, 0))
                                for c in range(4):
                                    mm = nc.tensor.transpose(bank[6][:, c * P:(c + 1) * P],
                                                             ob[:, w % 2, c * P:(c + 1) * P], ident[:, :])
                                mm.then_inc(f["ot"], 1)
                            if i == 6:
                                eng.wait_ge(f["ot_out"], t * B + w + 1)
                                for a in range(2):
                                    s = slice(a * F, (a + 1) * F)
                                    for c in range(HP):
                                        mm = nc.tensor.matmul(bank[6 + a][:, c * P:(c + 1) * P],
                                                              Wh_s[s, 2 * c + a, :], oTc[s, c * P:(c + 1) * P],
                                                              start=True, stop=True)
                                mm.then_inc(f["cat"], 1)
                        if i == 0 and 0 <= b - 2 < B:
                            eng.wait_ge(f["leaky"], t * B + b - 1)
                            for c in range(HEADS):
                                mm = nc.tensor.matmul(bank[6][:, 0:F], catc[:, c, :],
                                                      Wo_s[:, 2 * (c % HP) + c // HP, :],
                                                      start=c == 0, stop=c == HEADS - 1)
                            mm.then_inc(f["h2"], 1)

            @block.scalar
            def _(eng):
                with eng.Fori(0, T) as t:
                    for bp in range(BP):
                        eng.wait_ge(f["gathered"], t * 3 * BP + 3 * bp + 1)
                        for a in range(2):
                            src = bank[3 * bp % 4][a * F:(a + 1) * F, :]
                            b = 2 * bp + a
                            nc.scalar.activation(RA[0:F, b, :], src, ACT.Copy)
                            nc.scalar.activation(RA[F:P, b, :], src, ACT.Copy)
                            ins = nc.scalar.activation(RC[0:F, b, :], src, ACT.Copy)
                        ins.then_inc(f["ga"], 1)
                    eng.wait_ge(f["adj"], t + 1)
                    eng.wait_ge(f["u"], t * J)
                    nc.scalar.activation(adjc[:, :], bank[4], ACT.Copy).then_inc(f["adj_out"], 1)

                    def queries_1(b):
                        eng.wait_ge(f["y"], t * B + b + 1)
                        eng.wait_ge(f["copied"], t * B + b)
                        nc.scalar.activation(Y1[:, :], ps[:, 6:8, :].rearrange("p a c -> p (a c)"), ACT.Copy)\
                            .then_inc(f["y1"], 1)

                    def queries_2(b):
                        eng.wait_ge(f["yr"], t * B + b + 1)
                        eng.wait_ge(f["y3"], t * B + b)
                        if b >= 2:
                            eng.wait_ge(f["s"], t * J + (b - 1) * HEADS)
                        nc.scalar.activation(LA[F:P, b % 2, :, :].rearrange("p h n -> p (h n)"), YR[F:P, :], ACT.Copy)
                        nc.scalar.activation(Y2[:, :], YR[0:F, :], ACT.Copy).then_inc(f["y2"], 1)

                    queries_1(0)
                    queries_2(0)
                    for j in range(LAST):
                        b, i = divmod(j, HEADS)
                        if j < J:
                            eng.wait_ge(f["u"], t * J + j + 1)
                            if j >= 2:
                                eng.wait_ge(f["tr"], t * J + j - 1)
                            nc.scalar.activation(Pc[:, j % 2, :], Uc[:, j % 2, :], ACT.Exp,
                                                 bias=nmc[:, j % 2:j % 2 + 1]).then_inc(f["p"], 1)
                        if 2 <= j <= J + 1:
                            k = j - 2
                            eng.wait_ge(f["tr"], t * J + k + 1)
                            if k >= 2:
                                eng.wait_ge(f["o"], t * J + k - 1)
                            nc.scalar.activation(PTc[:, k % 2, :], bank[3 + k % 2], ACT.Copy).then_inc(f["tr_out"], 1)
                        if i == 3 and b + 1 < B:
                            queries_1(b + 1)
                        if i == 4 and b + 1 < B:
                            queries_2(b + 1)
                        if i == 5 and 0 <= b - 1 < B:
                            eng.wait_ge(f["ot"], t * B + b)
                            nc.scalar.activation(oTc[:, :], bank[6], ACT.Copy).then_inc(f["ot_out"], 1)
                        if i == 1 and 0 <= b - 2 < B:
                            w = b - 2
                            eng.wait_ge(f["h2"], t * B + w + 1)
                            nc.scalar.activation(r2[:, t, w * F:(w + 1) * F], bank[6][:, 0:F], ACT.Copy)\
                                .then_inc(f["h2_out"], 1)

            @block.gpsimd
            def _(eng):
                with eng.Fori(0, T) as t:
                    for b in range(B):
                        eng.wait_ge(f["y2"], t * B + b + 1)
                        if b >= 2:
                            eng.wait_ge(f["s"], t * J + (b - 1) * HEADS)
                        else:
                            eng.wait_ge(f["s"], t * J)
                        nc.gpsimd.tensor_tensor(LC[0:F, b % 2, :, :].rearrange("p h n -> p (h n)"), YR[0:F, :],
                                                Y2[:, :], ALU.subtract).then_inc(f["y3"], 1)

            @block.vector
            def _(eng):
                with eng.Fori(0, T) as t:
                    eng.wait_ge(f["adj"], t)
                    for mt in range(T):
                        nc.vector.tensor_scalar(Sel[:, mt, :], iota1[:, :], pos[:, mt, bass.ds(t, 1)], None,
                                                ALU.is_equal).then_inc(f["sel"], 1)
                    eng.wait_ge(f["y"], t * B)
                    for a in range(2):
                        nc.vector.tensor_copy(xq[:, a:B:2, :], hT[a * F:(a + 1) * F, :, bass.ts(t, P)])\
                            .then_inc(f["xq"], 1)
                    for bp in range(BP):
                        for j in (1, 2):
                            k = 3 * bp + j
                            eng.wait_ge(f["gathered"], t * 3 * BP + k + 1)
                            for a in range(2):
                                src = bank[k % 4][a * F:(a + 1) * F, :]
                                b = 2 * bp + a
                                if j == 1:
                                    nc.vector.tensor_copy(RB[0:F, b, :], src)
                                    ins = nc.vector.tensor_copy(RB[F:P, b, :], src)
                                else:
                                    ins = nc.vector.tensor_copy(RC[F:P, b, :], src)
                            ins.then_inc(f["gv"], 1)
                    for w in range(BP):
                        eng.wait_ge(f["v"], t * BP + w + 1)
                        nc.vector.tensor_copy(Vc[:, 2 * w:2 * w + 2, :, 0:F].rearrange("p b c f -> p (b c) f"),
                                              bank[[5, 6, 7, 5][w]].rearrange("p (g f) -> p g f", f=F))\
                            .then_inc(f["v_out"], 1)

                    def queries_v(b):
                        eng.wait_ge(f["y1"], t * B + b + 1)
                        eng.wait_ge(f["y2"], t * B + b)
                        eng.wait_ge(f["y3"], t * B + b)
                        nc.vector.tensor_tensor(YR[:, :], ps[:, 6:8, :].rearrange("p a c -> p (a c)"), Y1[:, :],
                                                ALU.subtract).then_inc(f["yr"], 1)
                        if b >= 2:
                            eng.wait_ge(f["s"], t * J + (b - 1) * HEADS)
                        nc.vector.tensor_copy(LA[0:F, b % 2, :, :].rearrange("p h n -> p (h n)"), Y1[0:F, :])
                        nc.vector.tensor_copy(LC[F:P, b % 2, :, :].rearrange("p h n -> p (h n)"), Y1[F:P, :])\
                            .then_inc(f["copied"], 1)

                    queries_v(0)
                    eng.wait_ge(f["adj_out"], t + 1)
                    for j in range(LAST):
                        b, i = divmod(j, HEADS)
                        if 4 <= j <= J + 3:
                            k = j - 4
                            eng.wait_ge(f["o"], t * J + k + 1)
                            if k >= 2:
                                eng.wait_ge(f["norm"], t * J + k - 1)
                            nc.vector.reciprocal(rzc[:, k % 2:k % 2 + 1], O_bank[k % 2][:, F:F + 1]).then_inc(f["rz"], 1)
                        if j < J:
                            eng.wait_ge(f["s"], t * J + j + 1)
                            if j >= 2:
                                eng.wait_ge(f["p"], t * J + j - 1)
                            else:
                                eng.wait_ge(f["lo"], t)
                            if j < 4:
                                nc.vector.memset(tick[:, :], 0.0)
                        if 4 <= j <= J + 3:
                            eng.wait_ge(f["rz"], t * J + k + 1)
                            w, h = divmod(k, HEADS)
                            if h == 0 and w >= 2:
                                eng.wait_ge(f["ot"], t * B + w - 1)
                            nc.vector.tensor_scalar(ob[:, w % 2, h * F:(h + 1) * F], O_bank[k % 2][:, 0:F],
                                                    rzc[:, k % 2:k % 2 + 1], None, ALU.mult).then_inc(f["norm"], 1)
                        if j < J:
                            nc.vector.tensor_tensor_reduce(Uc[:, j % 2, :], bank[j % 2], adjc[:, :], 1.0, -3.0e38,
                                                           ALU.mult, ALU.max, mst[:, j:j + 1]).then_inc(f["own"], 1)
                            eng.wait_ge(f["own"], t * J + j + 1)
                            nc.vector.tensor_scalar(nmc[:, j % 2:j % 2 + 1], mst[:, j:j + 1], -1.0, None, ALU.mult)\
                                .then_inc(f["u"], 1)
                        if i == 3 and b + 1 < B:
                            queries_v(b + 1)
                        if i == 7 and 0 <= b - 1 < B:
                            w = b - 1
                            eng.wait_ge(f["cat"], t * B + w + 1)
                            eng.wait_ge(f["h2"], t * B + w)
                            nc.vector.tensor_tensor(catc[:, :, :], ps[:, 6:8, :].rearrange("p a (c n) -> p (a c) n", n=P),
                                                    bh_aq[:, :].unsqueeze(2).to_broadcast([P, HEADS, P]), ALU.add)\
                                .then_inc(f["bias"], 1)
                            eng.wait_ge(f["bias"], t * B + w + 1)
                            nc.vector.scalar_tensor_tensor(catc[:, :, :], catc[:, :, :], 0.01, catc[:, :, :],
                                                           ALU.mult, ALU.max).then_inc(f["leaky"], 1)
                    eng.wait_ge(f["p"], (t + 1) * J)
                    nc.vector.tensor_reduce(nmc[:, 0:1], mst[:, :], X, ALU.min, negate=True).then_inc(f["tmin"], 1)
                    eng.wait_ge(f["tmin"], t + 1)
                    nc.vector.tensor_tensor(lo[:, :], lo[:, :], nmc[:, 0:1], ALU.max).then_inc(f["lo"], 1)
        l2a.close()

        l2b = ExitStack()
        adjN = sb("adjN2", [P, T, N], scope=l2b)
        xb = sb("xb", [P, T, 2, F], scope=l2b)
        V = sb("V", [P, T, F + 1], scope=l2b)
        kT = sb("kT", [P, N], scope=l2b)
        yT = sb("yT", [P, N], scope=l2b)
        G_s = sb("G_s", [F, P], scope=l2b)
        Wh_p = sb("Wh_p", [P, HID], scope=l2b)
        Wo_p = sb("Wo_p", [P, 2, F], scope=l2b)
        bh_p = sb("bh_p", [P, 2], scope=l2b)
        U = sb("U", [P, 2, N], scope=l2b)
        Pr = sb("Pr", [P, 2, N], scope=l2b)
        PT = sb("PT", [P, 2, N], scope=l2b)
        nm = sb("nm", [P, 2], scope=l2b)
        rz = sb("rz", [P, 2], scope=l2b)
        oh = sb("oh", [P, T, P], scope=l2b)
        oT = sb("oT", [P, HALF], scope=l2b)
        cat = sb("cat", [P, HALF], scope=l2b)
        h2 = sb("h2", [P, T, F], scope=l2b)
        top = sb("top", [P, 3], scope=l2b)

        S_bank = [0, 2]
        OP, MP = bank[6], bank[7]

        adj_in = sem("adj_in")
        with nc.Block() as block:
            @block.sync
            def _(eng):
                for j, a in enumerate((xs, hn)):
                    eng.dma_start(a[:, :, :], saved[j]).then_inc(adj_in, 16)
                eng.dma_start(adjN[:, :, :], adj.rearrange("(p t) m -> p t m", t=T)).then_inc(adj_in, 16)
                eng.wait_ge(adj_in, 48)

        def adj_row(t):
            return adjN[:, t, :].rearrange("p (m q) -> p q m", q=T)

        def attention_stage(name, general, heads):
            names = ("pool", "s", "u", "p", "tr", "tv", "ts", "o", "norm", "own", "x", "kt", "ktc", "y", "yc",
                     "ot", "otc", "cat", "catc", "catv", "h2", "h2c", "own2", "w")
            q = {n: sem(f"{name}_{n}") for n in names}
            UNROLL = 2 * T
            PER_B = (HP * UNROLL if heads else 0) + T

            def body(fn):
                def run(eng):
                    if general:
                        need = eng.value_load(flags[0:1, 1:2], min_val=0, max_val=1)
                        with eng.If(need > 0):
                            fn(eng)
                    else:
                        fn(eng)
                return run

            def tiles_tensor(eng, g0, tiles, y, k):
                def scores(i):
                    eng.wait_ge(q["u"], g0 + i)
                    for h in range(2):
                        mm = nc.tensor.matmul(bank[S_bank[i % 2] + h][:, :], y(i), k(i, h), start=True, stop=True)
                    mm.then_inc(q["s"], 1)

                def transposes(i):
                    eng.wait_ge(q["p"], g0 + i + 1)
                    for h in range(2):
                        eng.wait_ge(q["tv"] if h == 0 else q["ts"], g0 + i)
                        for j in range(4):
                            c = (h * 4 + j) * P
                            mm = nc.tensor.transpose(bank[4 + h][:, j * P:(j + 1) * P], Pr[:, i % 2, c:c + P],
                                                     ident[:, :])
                        mm.then_inc(q["tr"], 1)

                def values(i):
                    eng.wait_ge(q["tv"], g0 + i + 1)
                    eng.wait_ge(q["ts"], g0 + i + 1)
                    eng.wait_ge(q["norm"], g0 + i)
                    for mt in range(T):
                        mm = nc.tensor.matmul(OP[:, 0:F + 1], PT[:, i % 2, mt * P:(mt + 1) * P], V[:, mt, :],
                                              start=mt == 0, stop=mt == T - 1)
                    mm.then_inc(q["o"], 1)
                for s in range(tiles + 2):
                    if s < tiles:
                        scores(s)
                    if 1 <= s <= tiles:
                        transposes(s - 1)
                    if s >= 2:
                        values(s - 2)

            def tiles_scalar(eng, g0, tiles):
                for s in range(tiles + 1):
                    if s < tiles:
                        eng.wait_ge(q["u"], g0 + s + 2)
                        nc.scalar.activation(Pr[:, s % 2, :], U[:, s % 2, :], ACT.Exp, bias=nm[:, s % 2:s % 2 + 1])\
                            .then_inc(q["p"], 1)
                    if s >= 1:
                        i = s - 1
                        eng.wait_ge(q["tr"], (g0 + i) * 2 + 2)
                        eng.wait_ge(q["o"], g0 + i - 1 + 1) if i >= 1 else eng.wait_ge(q["o"], g0)
                        nc.scalar.activation(PT[:, i % 2, HALF:N], bank[5][:, :], ACT.Copy).then_inc(q["ts"], 1)

            def tiles_vector(eng, g0, tiles, row, out_of):
                OWN = 4 if general else 2
                for s in range(tiles + 2):
                    if s < tiles:
                        i, t = s, s % T
                        eng.wait_ge(q["s"], g0 + i + 1)
                        eng.wait_ge(q["p"], g0 + i - 1 if i >= 1 else g0)
                        m = nm[:, i % 2:i % 2 + 1]
                        sc2 = [bank[S_bank[i % 2] + h][:, :] for h in range(2)]
                        if not general:
                            nc.vector.memset(top[:, 2:3], 0.0)
                            nc.vector.tensor_tensor_reduce(
                                U[:, i % 2, :].rearrange("p (q m) -> p q m", q=T),
                                ps[:, S_bank[i % 2]:S_bank[i % 2] + 2, :].rearrange("p h (q m) -> p (h q) m", q=4),
                                row(t), 1.0, -3.0e38, ALU.mult, ALU.max, top[:, i % 2:i % 2 + 1])\
                                .then_inc(q["own"], 1)
                            eng.wait_ge(q["own"], (g0 + i) * OWN + 1)
                            nc.vector.tensor_scalar(m, top[:, i % 2:i % 2 + 1], -1.0, None, ALU.mult)\
                                .then_inc(q["own"], 1)
                            n = 1
                        else:
                            for h in range(2):
                                ins = nc.vector.tensor_tensor(
                                    U[:, i % 2, h * HALF:(h + 1) * HALF].rearrange("p (q m) -> p q m", q=4),
                                    sc2[h].rearrange("p (q m) -> p q m", q=4), row(t)[:, h * 4:h * 4 + 4, :],
                                    ALU.mult)
                            ins.then_inc(q["own"], 1)
                            eng.wait_ge(q["own"], (g0 + i) * OWN + 1)
                            nc.vector.tensor_scalar(Pr[:, i % 2, :], U[:, i % 2, :], 0.0, NEG_GAT,
                                                    ALU.is_equal, ALU.mult).then_inc(q["own"], 1)
                            eng.wait_ge(q["own"], (g0 + i) * OWN + 2)
                            nc.vector.tensor_tensor(U[:, i % 2, :], U[:, i % 2, :], Pr[:, i % 2, :], ALU.add)\
                                .then_inc(q["own"], 1)
                            eng.wait_ge(q["own"], (g0 + i) * OWN + 3)
                            n = 3
                            nc.vector.tensor_reduce(m, U[:, i % 2, :], X, ALU.max, negate=True).then_inc(q["own"], 1)
                        eng.wait_ge(q["own"], (g0 + i) * OWN + n + 1)
                        nc.vector.tensor_tensor(lo[:, :], lo[:, :], m, ALU.max).then_inc(q["u"], 1)
                    if 1 <= s <= tiles:
                        i = s - 1
                        eng.wait_ge(q["tr"], (g0 + i) * 2 + 1)
                        eng.wait_ge(q["o"], g0 + i)
                        nc.vector.tensor_copy(PT[:, i % 2, 0:HALF], bank[4][:, :]).then_inc(q["tv"], 1)
                    if s >= 2:
                        i = s - 2
                        eng.wait_ge(q["o"], g0 + i + 1)
                        nc.vector.reciprocal(rz[:, i % 2:i % 2 + 1], OP[:, F:F + 1]).then_inc(q["own2"], 1)
                        eng.wait_ge(q["own2"], g0 + i + 1)
                        nc.vector.tensor_scalar(out_of(i), OP[:, 0:F], rz[:, i % 2:i % 2 + 1], None, ALU.mult)\
                            .then_inc(q["norm"], 1)

            with nc.Block() as block:
                def pool(eng):
                    nc.gpsimd.memset(V[:, :, F:F + 1], 1.0).then_inc(q["pool"], 1)
                    eng.wait_ge(q["pool"], 1)
                    if heads:
                        with eng.Fori(0, B) as b:
                            eng.wait_ge(q["norm"], b * PER_B)
                            xv = hn[:, :, bass.ts(b, F)]
                            nc.gpsimd.tensor_copy(xb[:, :, 0, :], xv)
                            nc.gpsimd.tensor_copy(xb[:, :, 1, :], xv)
                            nc.gpsimd.tensor_copy(V[:, :, 0:F], xv).then_inc(q["x"], 1)
                block.gpsimd(body(pool))

                KEYS = 2 if heads else 1

                def keys_tensor(eng, n):
                    eng.wait_ge(q["x"], n + 1)
                    for h in range(2):
                        for j in range(4):
                            mm = nc.tensor.transpose(bank[4 + h][:, j * P:(j + 1) * P],
                                                     xb[:, h * 4 + j, :, :].rearrange("p a f -> p (a f)"),
                                                     ident[:, :])
                    mm.then_inc(q["kt"], 1)

                def pair_tensor(eng, b, hp):
                    n = b * HP + hp
                    eng.wait_ge(q["ktc"], b * 4 + 2)
                    eng.wait_ge(q["w"], (n + 1) * 5)
                    for h in range(2):
                        if h == 1:
                            eng.wait_ge(q["yc"], n * 2 + 1)
                        else:
                            eng.wait_ge(q["h2c"], n)
                        nc.tensor.matmul(MP[:, :], G_s[:, :], kT[0:F, h * HALF:(h + 1) * HALF],
                                         start=True, stop=True).then_inc(q["y"], 1)
                    eng.wait_ge(q["yc"], n * 2 + 2)

                    def part(i):
                        return slice((i // T) * F, (i // T + 1) * F)
                    tiles_tensor(eng, b * PER_B + hp * UNROLL, UNROLL,
                                 lambda i: yT[part(i), (i % T) * P:(i % T + 1) * P],
                                 lambda i, h: kT[part(i), h * HALF:(h + 1) * HALF])
                    eng.wait_ge(q["norm"], b * PER_B + (hp + 1) * UNROLL)
                    for h in range(2):
                        if h == 1:
                            eng.wait_ge(q["otc"], n * 2 + 1)
                        for j in range(4):
                            mm = nc.tensor.transpose(bank[4][:, j * P:(j + 1) * P], oh[:, h * 4 + j, :],
                                                     ident[:, :])
                        mm.then_inc(q["ot"], 1)
                        eng.wait_ge(q["otc"], n * 2 + h + 1)
                        for a in range(2):
                            s = slice(a * F, (a + 1) * F)
                            nc.tensor.matmul(bank[5][:, :], Wh_p[s, :], oT[s, :],
                                             start=True, stop=True).then_inc(q["cat"], 1)
                            eng.wait_ge(q["catv"], n * 4 + h * 2 + a + 1)
                            for j in range(4):
                                t = h * 4 + j
                                mm = nc.tensor.matmul(
                                    bank[a * 2][:, t * F:(t + 1) * F],
                                    cat[:, j * P:(j + 1) * P], Wo_p[:, a, :], start=True, stop=True)
                            mm.then_inc(q["h2"], 1)
                    eng.wait_ge(q["h2c"], n + 1)

                def tensor(eng):
                    eng.wait_ge(q["pool"], 1)
                    with eng.Fori(0, B) as b:
                        if heads:
                            keys_tensor(eng, b * KEYS)
                            with eng.Fori(0, HP) as hp:
                                pair_tensor(eng, b, hp)
                        keys_tensor(eng, b * KEYS + KEYS - 1)
                        eng.wait_ge(q["ktc"], (b + 1) * KEYS * 2)
                        tiles_tensor(eng, b * PER_B + (PER_B - T), T,
                                     lambda i: kT[0:F, i * P:(i + 1) * P],
                                     lambda i, h: kT[0:F, h * HALF:(h + 1) * HALF])
                        eng.wait_ge(q["norm"], (b + 1) * PER_B)
                block.tensor(body(tensor))

                def pair_scalar(eng, b, hp):
                    n = b * HP + hp
                    eng.wait_ge(q["h2c"], n)
                    for dst, src in ((G_s[:, :], GG[:, hp, :]), (Wh_p[0:F, :], Wh_s[0:F, hp * 2, :]),
                                     (Wh_p[F:P, :], Wh_s[F:P, hp * 2 + 1, :]),
                                     (Wo_p[:, :, :], Wo_s[:, bass.ts(hp, 2), :]),
                                     (bh_p[:, :], bh_s[:, bass.ts(hp, 2)])):
                        nc.scalar.activation(dst, src, ACT.Copy).then_inc(q["w"], 1)
                    for h in range(2):
                        eng.wait_ge(q["y"], n * 2 + h + 1)
                        nc.scalar.activation(yT[:, h * HALF:(h + 1) * HALF], MP[:, :], ACT.Copy)\
                            .then_inc(q["yc"], 1)
                    tiles_scalar(eng, b * PER_B + hp * UNROLL, UNROLL)
                    for c in range(4):
                        h, a = divmod(c, 2)
                        eng.wait_ge(q["cat"], n * 4 + c + 1)
                        eng.wait_ge(q["h2"], n * 4 + c)
                        eng.wait_ge(q["w"], (n + 1) * 5)
                        nc.scalar.activation(cat[:, :], bank[5][:, :], ACT.Identity, bias=bh_p[:, a:a + 1])\
                            .then_inc(q["catc"], 1)

                def scalar(eng):
                    with eng.Fori(0, B) as b:
                        if heads:
                            with eng.Fori(0, HP) as hp:
                                pair_scalar(eng, b, hp)
                            eng.wait_ge(q["h2c"], (b + 1) * HP)
                            src = h2[:, :, :]
                        else:
                            eng.wait_ge(q["norm"], b * PER_B)
                            src = r2[:, :, bass.ts(b, F)]
                        for a in range(2):
                            nc.scalar.activation(xb[:, :, a, :], src, ACT.Copy)
                        nc.scalar.activation(V[:, :, 0:F], src, ACT.Copy).then_inc(q["x"], 1)
                        tiles_scalar(eng, b * PER_B + (PER_B - T), T)
                block.scalar(body(scalar))

                def pair_vector(eng, b, hp):
                    n = b * HP + hp
                    tiles_vector(eng, b * PER_B + hp * UNROLL, UNROLL, adj_row,
                                 lambda i: oh[:, i % T, (i // T) * F:(i // T + 1) * F])
                    for h in range(2):
                        eng.wait_ge(q["ot"], n * 2 + h + 1)
                        nc.vector.tensor_copy(oT[:, :], bank[4][:, :]).then_inc(q["otc"], 1)
                        for a in range(2):
                            c = h * 2 + a
                            eng.wait_ge(q["catc"], n * 4 + c + 1)
                            nc.vector.scalar_tensor_tensor(cat[:, :], cat[:, :], 0.01, cat[:, :],
                                                           ALU.mult, ALU.max).then_inc(q["catv"], 1)
                    eng.wait_ge(q["h2"], n * 4 + 4)
                    eng.wait_ge(q["h2z"], b + 1)
                    h2f = h2[:, :, :].rearrange("p t f -> p (t f)")
                    nc.vector.tensor_tensor(h2f, h2f, bank[0], ALU.add).then_inc(q["h2v"], 1)
                    eng.wait_ge(q["h2v"], n + 1)
                    nc.vector.tensor_tensor(h2f, h2f, bank[2], ALU.add).then_inc(q["h2c"], 1)
                    eng.wait_ge(q["h2c"], n + 1)

                def vector(eng):
                    def copy_keys(n):
                        eng.wait_ge(q["kt"], n + 1)
                        for h in range(2):
                            nc.vector.tensor_copy(kT[:, h * HALF:(h + 1) * HALF], bank[4 + h][:, :])\
                                .then_inc(q["ktc"], 1)

                    if heads:
                        nc.vector.memset(lo[:, :], NEG_GAT * 4).then_inc(q["u"], 1)
                    else:
                        nc.vector.memset(nm[:, :], 0.0).then_inc(q["u"], 1)
                    eng.wait_ge(q["u"], 1)
                    with eng.Fori(0, B) as b:
                        if heads:
                            copy_keys(b * KEYS)
                            nc.vector.memset(h2[:, :, :], 0.0).then_inc(q["h2z"], 1)
                            with eng.Fori(0, HP) as hp:
                                pair_vector(eng, b, hp)
                        copy_keys(b * KEYS + KEYS - 1)
                        tiles_vector(eng, b * PER_B + (PER_B - T), T, adj_row, lambda i: oh[:, i, 0:F])
                        eng.wait_ge(q["norm"], (b + 1) * PER_B)
                        nc.vector.tensor_tensor(oh[:, :, 0:F], oh[:, :, 0:F],
                                                bout_row[:, :].unsqueeze(1).to_broadcast([P, T, F]), ALU.add)\
                            .then_inc(q["fin"], 1)
                        eng.wait_ge(q["fin"], b * 2 + 1)
                        nc.vector.scalar_tensor_tensor(r2[:, :, bass.ts(b, F)], oh[:, :, 0:F], 0.01, oh[:, :, 0:F],
                                                       ALU.mult, ALU.max).then_inc(q["fin"], 1)
                        eng.wait_ge(q["fin"], b * 2 + 2)
                for n in ("h2z", "h2v", "fin"):
                    q[n] = sem(f"{name}_{n}")
                block.vector(body(vector))

        attention_stage("gat2", False, False)

        lo_t, lo_v = sem("lo_t"), sem("lo_v")
        need = sb("need", [1, 4], scope=l2b)
        with nc.Block() as block:
            @block.tensor
            def _(eng):
                nc.tensor.transpose(bank[0][0:1, 0:P], lo[:, :], ident[:, :])
                nc.tensor.transpose(bank[0][0:1, P:2 * P], most[:, 0:1], ident[:, :])
                nc.tensor.transpose(bank[0][0:1, 2 * P:3 * P], most[:, 1:2], ident[:, :]).then_inc(lo_t, 1)

            @block.vector
            def _(eng):
                eng.wait_ge(lo_t, 1)
                nc.vector.tensor_reduce(need[0:1, 0:3], bank[0][0:1, 0:3 * P].rearrange("p (a c) -> p a c", a=3),
                                        X, ALU.max).then_inc(lo_v, 1)
                eng.wait_ge(lo_v, 1)
                for j, limit in enumerate((-SAFE_MAX, float(CAP), 0.0)):
                    nc.vector.tensor_scalar(need[0:1, j:j + 1], need[0:1, j:j + 1], limit, None, ALU.is_gt)\
                        .then_inc(lo_v, 1)
                eng.wait_ge(lo_v, 4)
                nc.vector.tensor_reduce(need[0:1, 3:4], need[0:1, 0:3], X, ALU.max).then_inc(lo_v, 1)
                eng.wait_ge(lo_v, 5)
                nc.vector.tensor_copy(flags[0:1, 1:2], need[0:1, 3:4]).then_inc(lo_v, 1)
                eng.wait_ge(lo_v, 6)
        attention_stage("gat_any", True, True)
        l2b.close()

        layernorm_stage_add = sem("add2")
        with nc.Block() as block:
            @block.vector
            def _(eng):
                nc.vector.tensor_tensor(xs[:, :, :], xs[:, :, :], r2[:, :, :], ALU.add)\
                    .then_inc(layernorm_stage_add, 1)
                eng.wait_ge(layernorm_stage_add, 1)
        layernorm_stage("ln3", xs, hn, r2)
        l2.close()
        retire_semaphores()
        l3 = ExitStack()
        dinv = sb("dinv", [P, T], scope=l3)
        z3 = sb("z3", [P, T, BF], scope=l3)
        d_v, d_s = sem("dinv_v"), sem("dinv_s")
        transpose_stage("h3_t", natural_to_transposed(hn, hT))
        with nc.Block() as block:
            @block.vector
            def _(eng):
                eng.wait_ge(d_s, 1)
                nc.vector.reciprocal(dinv[:, :], dinv[:, :]).then_inc(d_v, 1)
                eng.wait_ge(d_v, 1)

            @block.scalar
            def _(eng):
                nc.scalar.activation(dinv[:, :], rows[:, :], ACT.Sqrt, bias=one_col[:, :]).then_inc(d_s, 1)

        z_d, z_c, a_d, a_v, f_v, o_d = (sem(f"l3_{s}") for s in ("z", "z_out", "az", "az_v", "sum_v", "stored"))
        with nc.Block() as block:
            @block.tensor
            def _(eng):
                for t in range(T):
                    if t >= 4:
                        eng.wait_ge(z_c, t - 3)
                    for bp in range(BP):
                        mm = nc.tensor.matmul(bank[t % 4][:, bp * P:(bp + 1) * P], hT[:, bp, t * P:(t + 1) * P],
                                              bd[:, 3, :], start=True, stop=True)
                    mm.then_inc(z_d, 1)
                eng.wait_ge(z_c, T)
                for nt in range(T):
                    if nt >= 4:
                        eng.wait_ge(a_v, (nt - 3) * 2)
                    for mt in range(T):
                        mm = nc.tensor.matmul(bank[4 + nt % 4][:, :], adjT[:, mt, nt * P:(nt + 1) * P],
                                              z3[:, mt, :], start=mt == 0, stop=mt == T - 1)
                    mm.then_inc(a_d, 1)

            @block.scalar
            def _(eng):
                for t in range(T):
                    eng.wait_ge(z_d, t + 1)
                    nc.scalar.activation(z3[:, t, :], bank[t % 4][:, :], ACT.Copy, scale=dinv[:, t:t + 1])\
                        .then_inc(z_c, 1)

            @block.vector
            def _(eng):
                eng.wait_ge(z_c, T)
                for nt in range(T):
                    eng.wait_ge(a_d, nt + 1)
                    nc.vector.tensor_tensor(hn[:, nt, :], bank[4 + nt % 4][:, :], z3[:, nt, :], ALU.add)\
                        .then_inc(a_v, 1)
                    eng.wait_ge(a_v, nt * 2 + 1)
                    nc.vector.scalar_tensor_tensor(xs[:, nt, :], hn[:, nt, :], dinv[:, nt:nt + 1], xs[:, nt, :],
                                                   ALU.mult, ALU.add).then_inc(a_v, 1)

            @block.sync
            def _(eng):
                for t in range(T):
                    eng.wait_ge(a_v, t * 2 + 2)
                    eng.dma_start(out.rearrange("b (p t) f -> t p b f", t=T)[t],
                                  xs[:, t, :].rearrange("p (b f) -> p b f", b=B)).then_inc(o_d, 16)
                eng.wait_ge(o_d, 16 * T)
        l3.close()


_INS = ["x", "adj", "L0_gnn_H", "L0_gnn_W", "L0_gnn_W_ind", "L0_gnn_a_node", "L0_gnn_a_gn", "L0_gnn_a_ge",
        "L0_gnn_fcW", "L0_gnn_fcb", "L0_gnn_av", "L1_gnn_intervention_value", "L1_gnn_W1", "L1_gnn_b1",
        "L1_gnn_W2", "L1_gnn_b2", "L2_gnn_Wh", "L2_gnn_bh", "L2_gnn_W_out", "L2_gnn_b_out", "L3_gnn_W"]


def kernel(**inputs):
    import numpy as _np
    import concourse.bacc as _bacc
    from concourse import mybir as _mybir
    from concourse.bass_utils import run_bass_kernel_spmd as _run

    nc = _bacc.Bacc("TRN2", target_bir_lowering=False, num_devices=1)
    arrays, args = {}, []
    for name in _INS:
        a = _np.ascontiguousarray(inputs[name])
        arrays[f"in_{name}_dram"] = a
        args.append(nc.dram_tensor(f"in_{name}_dram", a.shape, _mybir.dt.from_np(a.dtype), kind="ExternalInput").ap())
    out = nc.dram_tensor("out_dram", (B, N, F), _mybir.dt.float32, kind="ExternalOutput").ap()
    hyper_gat_stack(nc, *args, out)
    r = _run(nc, [arrays], core_ids=[0])
    return r.results[0]["out_dram"]
```

```python
from contextlib import ExitStack

import concourse.bass as bass
from concourse import mybir

B, N, F = 8, 1024, 64
E = 64
P = 128
T = N // P
BF = B * F
BP = B // 2
HEADS, HID = 8, 128
HP = HEADS // 2
HALF = 512
EPS = 1e-5
NEG_EDGE = -1e9
NEG_GAT = -1e16
BASE_SLOTS = 10
SAFE_MAX = 104.0
MAX_STEPS = 3

CAP = 512
CT = CAP // P

fp32 = mybir.dt.float32
bf16 = mybir.dt.bfloat16
i32 = mybir.dt.int32
ALU = mybir.AluOpType
ACT = mybir.ActivationFunctionType
X = mybir.AxisListType.X


class Steps:

    def __init__(self, eng, sem):
        self.eng, self.sem, self.base, self.n = eng, sem, 0, 0

    def did(self, ins):
        ins.then_inc(self.sem, 1)
        self.n += 1
        return self.n

    def wait(self, back=0):
        self.eng.wait_ge(self.sem, self.base + (self.n - back))


def hyper_gat_stack(nc, x, adj, H, W, W_ind, a_node, a_gn, a_ge, fcW, fcb, av, iv, W1, b1, W2, b2,
                    Wh, bh, W_out, b_out, W3, out):
    life = ExitStack()
    with life:
        def sb(name, shape, dt=fp32, scope=life):
            return scope.enter_context(nc.sbuf_tensor(name, shape, dt))

        in_use = []

        def sem(name):
            in_use.append(nc.alloc_semaphore(name=name))
            return in_use[-1]

        def retire_semaphores():
            nc.clear_and_free_semaphores(list(in_use))
            in_use.clear()
            nc.all_engine_barrier()

        ps = life.enter_context(nc.psum_tensor("ps", [P, 8, HALF], fp32))
        bank = [ps[:, i, :] for i in range(8)]

        xs = sb("xs", [P, T, BF])
        hn = sb("hn", [P, T, BF])
        hT = sb("hT", [P, BP, N])
        adjT = sb("adjT", [P, T, N])
        pos = sb("pos", [P, T, T])
        most = sb("most", [P, 2])
        ident = sb("ident", [P, P])
        ln_sum = sb("ln_sum", [P, T * B])
        ln_std = sb("ln_std", [P, T * B])
        eps_col = sb("eps_col", [P, 1])
        one_col = sb("one_col", [P, 1])
        flags = sb("flags", [1, 2], i32)
        deg = sb("deg", [P, T])
        rows = sb("rows", [P, T])
        bd = sb("bd", [P, 4, P])
        b1_col = sb("b1_col", [P, 1])
        b2_col = sb("b2_col", [P, 1])
        b2_row = sb("b2_row", [P, F])
        bout_row = sb("bout_row", [P, F])

        def views(a):
            return a[:, :, :].rearrange("p t (b f) -> p (t b) f", b=B)

        def per_group(col):
            return col[:, :].unsqueeze(2).to_broadcast([P, T * B, F])

        def layernorm_stage(name, src_x, dst, scratch, adds=None, to=None):
            added, summed, own, centred, squared, sq_sum, rooted, inverted, normal, filled, emptied = (
                sem(f"{name}_{s}") for s in ("added", "summed", "own", "centred", "squared", "square_sum",
                                             "rooted", "inverted", "done", "filled", "emptied"))

            def groups(a, t):
                return a[:, t, :].rearrange("p (b f) -> p b f", b=B)

            def stat(a, t):
                return a[:, t * B:(t + 1) * B]

            def per_feature(a, t):
                return stat(a, t).unsqueeze(2).to_broadcast([P, B, F])

            with nc.Block() as block:
                @block.gpsimd
                def _(eng):
                    for s in range(T + 2):
                        if s < T and adds is not None:
                            nc.gpsimd.tensor_tensor(src_x[:, s, :], src_x[:, s, :], adds[:, s, :], ALU.add)\
                                .then_inc(added, 1)
                        if s >= 2:
                            t = s - 2
                            eng.wait_ge(own, t + 1)
                            nc.gpsimd.tensor_tensor(groups(dst, t), groups(src_x, t), per_feature(ln_sum, t),
                                                    ALU.subtract).then_inc(centred, 1)

                @block.scalar
                def _(eng):
                    for s in range(T + 2):
                        if s < T:
                            eng.wait_ge(centred, s + 1)
                            nc.scalar.activation(scratch[:, s, :], dst[:, s, :], ACT.Square).then_inc(squared, 1)
                        if s >= 2:
                            t = s - 2
                            eng.wait_ge(sq_sum, t + 1)
                            nc.scalar.activation(stat(ln_std, t), stat(ln_std, t), ACT.Sqrt, bias=eps_col[:, :],
                                                 scale=1.0 / F).then_inc(rooted, 1)
                        if to is not None and s >= T:
                            h = s - T
                            for bp in range(BP):
                                eng.wait_ge(filled, h * BP + bp + 1)
                                nc.scalar.activation(to[:, bp, h * HALF:(h + 1) * HALF], bank[h * BP + bp],
                                                     ACT.Copy).then_inc(emptied, 1)
                    if to is not None:
                        eng.wait_ge(emptied, 2 * BP)

                @block.vector
                def _(eng):
                    for s in range(T + 3):
                        if s < T:
                            if adds is not None:
                                eng.wait_ge(added, s + 1)
                            nc.vector.tensor_reduce(stat(ln_sum, s), groups(src_x, s), X, ALU.add)\
                                .then_inc(summed, 1)
                            eng.wait_ge(summed, s + 1)
                            nc.vector.tensor_scalar(stat(ln_sum, s), stat(ln_sum, s), 1.0 / F, None, ALU.mult)\
                                .then_inc(own, 1)
                        if 2 <= s < T + 2:
                            t = s - 2
                            eng.wait_ge(squared, t + 1)
                            nc.vector.tensor_reduce(stat(ln_std, t), groups(scratch, t), X, ALU.add)\
                                .then_inc(sq_sum, 1)
                        if s >= 3:
                            t = s - 3
                            eng.wait_ge(rooted, t + 1)
                            nc.vector.reciprocal(stat(ln_std, t), stat(ln_std, t)).then_inc(inverted, 1)
                            eng.wait_ge(inverted, t + 1)
                            nc.vector.scalar_tensor_tensor(groups(dst, t), groups(dst, t), 0.0,
                                                           per_feature(ln_std, t), ALU.max, ALU.mult)\
                                .then_inc(normal, 1)
                    eng.wait_ge(normal, T)

                @block.tensor
                def _(eng):
                    if to is not None:
                        for h in range(2):
                            eng.wait_ge(normal, (h + 1) * 4)
                            for bp in range(BP):
                                for j in range(4):
                                    mm = nc.tensor.transpose(bank[h * BP + bp][:, j * P:(j + 1) * P],
                                                             dst[:, h * 4 + j, bp * P:(bp + 1) * P], ident[:, :])
                                mm.then_inc(filled, 1)

        def transpose_stage(name, groups):
            filled, emptied = sem(f"{name}_filled"), [sem(f"{name}_emptied{i}") for i in range(2)]
            with nc.Block() as block:
                @block.tensor
                def _(eng):
                    for i, (_, srcs) in enumerate(groups):
                        if i >= 4:
                            eng.wait_ge(emptied[i % 2], (i - 4) // 2 + 1)
                        for j, s in enumerate(srcs):
                            mm = nc.tensor.transpose(bank[i % 4][:, j * P:(j + 1) * P], s, ident[:, :])
                        mm.then_inc(filled, 1)

                @block.vector
                def _(eng):
                    for i in range(0, len(groups), 2):
                        eng.wait_ge(filled, i + 1)
                        nc.vector.tensor_copy(groups[i][0], bank[i % 4][:, :]).then_inc(emptied[0], 1)
                    eng.wait_ge(emptied[0], (len(groups) + 1) // 2)

                @block.scalar
                def _(eng):
                    for i in range(1, len(groups), 2):
                        eng.wait_ge(filled, i + 1)
                        nc.scalar.activation(groups[i][0], bank[i % 4][:, :], ACT.Copy).then_inc(emptied[1], 1)
                    eng.wait_ge(emptied[1], len(groups) // 2)

        def natural_to_transposed(src, dst):
            return [(dst[:, bp, h * HALF:(h + 1) * HALF],
                     [src[:, h * 4 + j, bp * P:(bp + 1) * P] for j in range(4)])
                    for bp in range(BP) for h in range(2)]

        l0 = ExitStack()
        adjN = sb("adjN", [P, T, N], scope=l0)
        H_s = sb("H_s", [P, T, E], scope=l0)
        rhsW = sb("rhsW", [P, 258], scope=l0)
        W_dup = sb("W_dup", [P, F], scope=l0)
        node_row = sb("node_row", [P, F], scope=l0)
        gn_row = sb("gn_row", [P, F], scope=l0)
        ge_row = sb("ge_row", [P, F], scope=l0)
        fcW_s = sb("fcW_s", [P, 2 * F], scope=l0)
        fcb_col = sb("fcb_col", [P, 1], scope=l0)
        av_col = sb("av_col", [P, 1], scope=l0)
        av_rep = sb("av_rep", [P, P], scope=l0)
        s_rep = sb("s_rep", [P, P], scope=l0)
        w_prod = sb("w_prod", [P, 2, F], scope=l0)
        w_cols = sb("w_cols", [P, 2], scope=l0)
        raw = sb("raw", [P, 4, P], scope=l0)

        loaded, zeroed, id_done, cst_done = sem("loaded"), sem("zeroed"), sem("id_done"), sem("cst_done")
        blocks_loaded = sem("blocks_loaded")
        with nc.Block() as block:
            n_loads = []

            @block.sync
            def _(eng):
                def load(dst, src):
                    eng.dma_start(dst, src).then_inc(loaded, 16)
                    n_loads.append(1)
                for b in range(B):
                    load(xs[:, :, b * F:(b + 1) * F], x[b].rearrange("(p t) f -> p t f", t=T))
                load(adjN[:, :, :], adj.rearrange("(p t) m -> p t m", t=T))
                load(H_s[:, :, :], H.rearrange("(p t) e -> p t e", t=T))
                for h in range(2):
                    s = slice(h * F, (h + 1) * F)
                    load(W_dup[s, :], W)
                    load(fcW_s[s, :], fcW)
                    load(b1_col[s, :], b1.unsqueeze(1))
                    load(b2_col[s, :], b2.unsqueeze(1))
                for row, src in ((node_row, a_node), (gn_row, a_gn), (ge_row, a_ge), (b2_row, b2), (bout_row, b_out)):
                    load(row[:, :], src.unsqueeze(0).to_broadcast([P, F]))
                load(fcb_col[:, :], fcb.unsqueeze(1))
                load(av_col[:, :], av.unsqueeze(1))
                eng.wait_ge(loaded, 16 * len(n_loads))

            @block.gpsimd
            def _(eng):
                nc.gpsimd.memset(ident[:, :], 0.0).then_inc(id_done, 1)
                nc.gpsimd.memset(raw[:, :, :], 0.0).then_inc(zeroed, 1)
                nc.gpsimd.memset(rhsW[:, :], 0.0).then_inc(zeroed, 1)
                nc.gpsimd.memset(s_rep[:, :], 0.0).then_inc(zeroed, 1)
                nc.gpsimd.memset(eps_col[:, :], EPS).then_inc(cst_done, 1)
                nc.gpsimd.memset(one_col[:, :], 1.0).then_inc(cst_done, 1)
                nc.gpsimd.memset(flags[:, :], 0).then_inc(cst_done, 1)
                eng.wait_ge(id_done, 1)
                eng.affine_select(out=ident[:, :], in_=ident[:, :], compare_op=ALU.not_equal, fill=1.0,
                                  base=0, pattern=[[-1, P]], channel_multiplier=1).then_inc(id_done, 1)
                eng.wait_ge(id_done, 2)
                eng.wait_ge(cst_done, 3)

            @block.scalar
            def _(eng):
                eng.wait_ge(zeroed, 2)
                n = 0
                for h in range(2):
                    s = slice(h * F, (h + 1) * F)
                    for dst, src in ((raw[s, 0, s], W1[:, 0:F]), (raw[s, 1, s], W1[:, F:2 * F]),
                                     (raw[s, 2, s], W2), (raw[s, 3, s], W3),
                                     (rhsW[s, s], W), (rhsW[s, 130 + h * F:130 + (h + 1) * F], W_ind)):
                        eng.dma_start(dst, src).then_inc(blocks_loaded, 16)
                        n += 16
                eng.wait_ge(blocks_loaded, n)

        v_done, p_tr = sem("cst_v"), sem("bd_transposed")
        with nc.Block() as block:
            @block.vector
            def _(eng):
                st = Steps(eng, v_done)
                st.did(nc.vector.tensor_tensor(w_prod[:, 0, :], W_dup[:, :], node_row[:, :], ALU.mult))
                st.did(nc.vector.tensor_tensor(w_prod[:, 1, :], W_dup[:, :], gn_row[:, :], ALU.mult))
                st.wait()
                st.did(nc.vector.tensor_reduce(w_cols[:, :], w_prod[:, :, :], X, ALU.add))
                st.wait()
                for h in range(2):
                    s = slice(h * F, (h + 1) * F)
                    st.did(nc.vector.tensor_copy(s_rep[s, s], w_cols[s, 0:1].to_broadcast([F, F])))
                    st.did(nc.vector.tensor_copy(rhsW[s, P + h:P + h + 1], w_cols[s, 1:2]))
                st.did(nc.vector.tensor_copy(av_rep[:, :], av_col[:, :].to_broadcast([P, P])))
                eng.wait_ge(p_tr, 1)
                st.did(nc.vector.tensor_copy(bd[:, :, :].rearrange("p a c -> p (a c)"), bank[0][:, :]))
                st.wait()

            @block.tensor
            def _(eng):
                for j in range(4):
                    mm = nc.tensor.transpose(bank[0][:, j * P:(j + 1) * P], raw[:, j, :], ident[:, :])
                mm.then_inc(p_tr, 1)

        transpose_stage("adj_t", [(adjT[:, mt, h * HALF:(h + 1) * HALF],
                                   [adjN[:, h * 4 + j, mt:N:T] for j in range(4)])
                                  for mt in range(T) for h in range(2)])

        nb = ExitStack()
        adjR = sb("adjR", [P, T, N], bf16, scope=nb)
        anyf = sb("anyf", [P, T, T], scope=nb)
        anyb = sb("anyb", [P, T, T], bf16, scope=nb)
        tri = sb("tri", [P, P], bf16, scope=nb)
        oneb = sb("oneb", [P, P], bf16, scope=nb)
        nb_v, nb_g, nb_t, nb_s, nb_p = (sem(f"neighbours_{q}") for q in ("v", "tri", "counted", "rounded", "left"))
        with nc.Block() as block:
            @block.gpsimd
            def _(eng):
                nc.gpsimd.memset(tri[:, :], 1.0).then_inc(nb_g, 1)
                nc.gpsimd.memset(oneb[:, :], 1.0).then_inc(nb_g, 1)
                eng.wait_ge(nb_g, 2)
                eng.affine_select(out=tri[:, :], in_=tri[:, :], compare_op=ALU.is_ge, fill=0.0,
                                  base=0, pattern=[[1, P]], channel_multiplier=-1).then_inc(nb_g, 1)
                eng.wait_ge(nb_s, 1)
                nc.gpsimd.tensor_tensor(adjN[:, :, :], adjT[:, :, :], adjR[:, :, :], ALU.subtract).then_inc(nb_p, 1)
                eng.wait_ge(nb_p, 1)

            @block.scalar
            def _(eng):
                eng.wait_ge(nb_v, 1)
                nc.scalar.activation(adjR[:, :, :], adjT[:, :, :], ACT.Copy).then_inc(nb_s, 1)

            @block.tensor
            def _(eng):
                eng.wait_ge(nb_g, 3)
                eng.wait_ge(nb_v, 3)
                for mt in range(T):
                    for k in range(mt + 1):
                        mm = nc.tensor.matmul(bank[0][:, mt * T:(mt + 1) * T], (tri if k == mt else oneb)[:, :],
                                              anyb[:, k, :], start=k == 0, stop=k == mt)
                mm.then_inc(nb_t, 1)

            @block.vector
            def _(eng):
                st = Steps(eng, nb_v)
                st.did(nc.vector.tensor_reduce(rows[:, :], adjN[:, :, :], X, ALU.add))
                st.did(nc.vector.tensor_reduce(anyf[:, :, :], adjT[:, :, :].rearrange("p q (t n) -> p q t n", t=T),
                                               X, ALU.max, apply_absolute_value=True))
                st.wait()
                st.did(nc.vector.tensor_scalar(anyb[:, :, :], anyf[:, :, :], 0.0, None, ALU.is_gt))
                st.wait()
                eng.wait_ge(nb_t, 1)
                st.did(nc.vector.tensor_tensor(pos[:, :, :].rearrange("p q t -> p (q t)"), bank[0][:, 0:T * T],
                                               anyb[:, :, :].rearrange("p q t -> p (q t)"), ALU.mult))
                st.wait()
                st.did(nc.vector.tensor_reduce(most[:, 0:1], pos[:, :, :].rearrange("p q t -> p (q t)"), X, ALU.max))
                eng.wait_ge(nb_p, 1)
                st.did(nc.vector.tensor_reduce(most[:, 1:2], adjN[:, :, :].rearrange("p q n -> p (q n)"), X,
                                               ALU.max, apply_absolute_value=True))
                st.wait()
        nb.close()

        hW = sb("hW", [P, T, BF], scope=l0)
        hWi = sb("hWi", [P, T, BF], scope=l0)
        acc = sb("acc", [P, T, BF], scope=l0)
        layernorm_stage("ln0", xs, hn, acc, to=hT)

        p_n = sb("p_n", [P, T, B], scope=l0)
        mx = sb("mx", [P, T, B], scope=l0)
        ne = sb("ne", [P, T], scope=l0)
        cnt = sb("cnt", [P, T], scope=l0)
        rankT = sb("rankT", [E, N], scope=l0)
        aggx = sb("aggx", [E, BF], scope=l0)
        qs = sb("qs", [E, 2, B], scope=l0)

        l0a = ExitStack()
        MN = sb("MN", [P, T, 2, E], scope=l0a)
        MT = sb("MT", [P, N], scope=l0a)
        NT = sb("NT", [P, N], scope=l0a)
        NN = sb("NN", [P, T, E], scope=l0a)
        cum = sb("cum", [P, T, E], scope=l0a)
        onesE = sb("onesE", [P, E], scope=l0a)
        cmax = sb("cmax", [P, 1], scope=l0a)

        proj_done, proj_v, proj_s = sem("proj_done"), sem("proj_v"), sem("proj_s")
        with nc.Block() as block:
            @block.tensor
            def _(eng):
                for i in range(T * BP):
                    t, bp = divmod(i, BP)
                    if i >= 4:
                        eng.wait_ge(proj_v, i - 3)
                        eng.wait_ge(proj_s, i - 3)
                    nc.tensor.matmul(bank[i % 4][:, 0:258], hT[:, bp, t * P:(t + 1) * P], rhsW[:, :],
                                     start=True, stop=True).then_inc(proj_done, 1)

            @block.vector
            def _(eng):
                for i in range(T * BP):
                    t, bp = divmod(i, BP)
                    eng.wait_ge(proj_done, i + 1)
                    nc.vector.tensor_copy(hWi[:, t, bp * P:(bp + 1) * P], bank[i % 4][:, 130:258]).then_inc(proj_v, 1)
                eng.wait_ge(proj_v, T * BP)

            @block.scalar
            def _(eng):
                for i in range(T * BP):
                    t, bp = divmod(i, BP)
                    eng.wait_ge(proj_v, i + 1)
                    nc.scalar.activation(p_n[:, t, bp * 2:bp * 2 + 2], bank[i % 4][:, 128:130], ACT.Copy)
                    nc.scalar.activation(hW[:, t, bp * P:(bp + 1) * P], bank[i % 4][:, 0:128], ACT.Copy)\
                        .then_inc(proj_s, 1)
                eng.wait_ge(proj_s, T * BP)

        m_done, mt_done, mt_s = sem("mask_done"), sem("mask_t_done"), sem("mask_s")
        with nc.Block() as block:
            @block.vector
            def _(eng):
                st = Steps(eng, m_done)
                for j in range(2):
                    st.did(nc.vector.tensor_scalar(MN[:, :, j, :], H_s[:, :, :], 0.0, None, ALU.is_gt))
                st.did(nc.vector.memset(onesE[:, :], 1.0))
                st.wait()
                st.did(nc.vector.tensor_scalar(NN[:, :, :], MN[:, :, 0, :], -1.0, -NEG_EDGE, ALU.add, ALU.mult))
                st.did(nc.vector.tensor_reduce(ne[:, :], MN[:, :, 0, :], X, ALU.add))
                st.wait()
                st.did(nc.vector.tensor_scalar(ne[:, :], ne[:, :], 1.0, None, ALU.min))
                st.did(nc.vector.tensor_scalar(deg[:, :], rows[:, :], 1.0, None, ALU.max))
                st.wait()
                st.did(nc.vector.reciprocal(deg[:, :], deg[:, :]))
                st.did(nc.vector.tensor_scalar(cnt[:, :], ne[:, :], -1.0, 1.0, ALU.mult, ALU.add))
                st.wait()
                st.did(nc.vector.tensor_tensor(H_s[:, :, :], MN[:, :, 0, :],
                                               cnt[:, :].unsqueeze(2).to_broadcast([P, T, E]), ALU.max))
                st.wait()
                for t in range(T):
                    st.did(nc.vector.tensor_tensor_scan(cum[:, t, :], onesE[:, :], H_s[:, t, :], 0.0,
                                                        ALU.mult, ALU.add))
                st.wait()
                st.did(nc.vector.tensor_copy(cnt[:, :], cum[:, :, E - 1]))
                st.wait()
                st.did(nc.vector.tensor_tensor(cum[:, :, :], cum[:, :, :], H_s[:, :, :], ALU.mult))
                st.wait()
                st.did(nc.vector.tensor_reduce(cmax[:, :], cnt[:, :], X, ALU.max))
                eng.wait_ge(mt_done, 1)
                for h in range(2):
                    st.did(nc.vector.tensor_copy(MT[:, h * HALF:(h + 1) * HALF], bank[h][:, :]))
                    st.did(nc.vector.tensor_copy(rankT[:, h * HALF:(h + 1) * HALF], bank[2 + h][0:E, :]))
                st.wait()
                st.did(nc.vector.tensor_scalar(NT[:, :], MT[:, :], -1.0, -NEG_EDGE, ALU.add, ALU.mult))
                eng.wait_ge(mt_done, 2)
                st.did(nc.vector.tensor_reduce(cmax[0:1, :], bank[4][0:1, 0:P], X, ALU.max))
                st.wait()
                st.did(nc.vector.tensor_copy(flags[0:1, 0:1], cmax[0:1, :]))
                st.wait()

            @block.tensor
            def _(eng):
                eng.wait_ge(m_done, 21)
                for t in range(T):
                    h, j = divmod(t, 4)
                    nc.tensor.transpose(bank[h][:, j * P:(j + 1) * P],
                                        MN[:, t, :, :].rearrange("p a e -> p (a e)"), ident[:, :])
                    mm = nc.tensor.transpose(bank[2 + h][0:E, j * P:(j + 1) * P], cum[:, t, :], ident[:, :])
                mm.then_inc(mt_done, 1)
                nc.tensor.transpose(bank[4][0:1, 0:P], cmax[:, :], ident[:, :]).then_inc(mt_done, 1)

        LG = acc[:, :, :].rearrange("p (q c) n -> p q (c n)", c=2)
        alT = adjN[:, 0:BP, :].rearrange("p q (t e) -> p q t e", t=T)
        amax = sb("amax", [P, BP], scope=l0a)
        asum = sb("asum", [P, BP], scope=l0a)
        s_done, s_cp, a_v, a_pool, a_exp, a_tr, a_tc, a_agg, a_dots = (
            sem(f"alpha_{s}") for s in ("s", "cp", "v", "pool", "exp", "tr", "tc", "agg", "dots"))
        geb = sb("geb", [E, BF], scope=l0a)
        with nc.Block() as block:
            @block.tensor
            def _(eng):
                for i in range(BP * 2):
                    bp, h = divmod(i, 2)
                    if i >= 2:
                        eng.wait_ge(s_cp, i - 1)
                    nc.tensor.matmul(bank[h][:, :], s_rep[:, :], hT[:, bp, h * HALF:(h + 1) * HALF],
                                     start=True, stop=True).then_inc(s_done, 1)
                for i in range(BP * 2):
                    bp, h = divmod(i, 2)
                    if h == 0:
                        eng.wait_ge(a_exp, bp + 1)
                    if i >= 2:
                        eng.wait_ge(a_tc, i - 1)
                    for j in range(4):
                        t = h * 4 + j
                        mm = nc.tensor.transpose(bank[2 + h][:, j * P:(j + 1) * P],
                                                 LG[:, bp, t * P:(t + 1) * P], ident[:, :])
                    mm.then_inc(a_tr, 1)
                for bp in range(BP):
                    eng.wait_ge(a_tc, 2 * bp + 2)
                    for t in range(T):
                        mm = nc.tensor.matmul(bank[4 + bp][:, 0:P], alT[:, bp, t, :],
                                              hW[:, t, bp * P:(bp + 1) * P], start=t == 0, stop=t == T - 1)
                    mm.then_inc(a_agg, 1)

            @block.scalar
            def _(eng):
                for i in range(BP * 2):
                    bp, h = divmod(i, 2)
                    eng.wait_ge(s_done, i + 1)
                    nc.scalar.activation(LG[:, bp, h * HALF:(h + 1) * HALF], bank[h][:, :], ACT.Copy)\
                        .then_inc(s_cp, 1)
                for bp in range(BP):
                    eng.wait_ge(a_v, 3 * bp + 3)
                    nc.scalar.activation(LG[:, bp, :], LG[:, bp, :], ACT.Exp, bias=amax[:, bp:bp + 1],
                                         accum_out=asum[:, bp:bp + 1]).then_inc(a_exp, 1)
                for i in range(BP * 2):
                    bp, h = divmod(i, 2)
                    eng.wait_ge(a_tr, i + 1)
                    nc.scalar.activation(alT[:, bp, h * 4:h * 4 + 4, :].rearrange("p t e -> p (t e)"),
                                         bank[2 + h][:, :], ACT.Copy).then_inc(a_tc, 1)

            @block.gpsimd
            def _(eng):
                for bp in range(BP):
                    eng.wait_ge(a_v, 3 * bp + 1)
                    nc.gpsimd.tensor_tensor(LG[:, bp, :], LG[:, bp, :], MT[:, :], ALU.mult).then_inc(a_pool, 1)

            @block.vector
            def _(eng):
                st = Steps(eng, a_v)
                for bp in range(BP):
                    eng.wait_ge(s_cp, 2 * bp + 2)
                    st.did(nc.vector.scalar_tensor_tensor(LG[:, bp, :], LG[:, bp, :], 0.2, LG[:, bp, :],
                                                          ALU.mult, ALU.max))
                    eng.wait_ge(a_pool, bp + 1)
                    st.did(nc.vector.tensor_tensor(LG[:, bp, :], LG[:, bp, :], NT[:, :], ALU.add))
                    st.wait()
                    st.did(nc.vector.tensor_reduce(amax[:, bp:bp + 1], LG[:, bp, :], X, ALU.max, negate=True))
                eng.wait_ge(a_exp, BP)
                st.did(nc.vector.reciprocal(asum[:, :], asum[:, :]))
                st.wait()
                for bp in range(BP):
                    eng.wait_ge(a_agg, bp + 1)
                    for h in range(2):
                        b, s = 2 * bp + h, slice(h * E, (h + 1) * E)
                        st.did(nc.vector.tensor_scalar(aggx[:, b * F:(b + 1) * F], bank[4 + bp][s, s],
                                                       asum[s, bp:bp + 1], None, ALU.mult))
                st.wait()
                st.did(nc.vector.tensor_tensor(geb[:, :].rearrange("e (b f) -> e b f", b=B),
                                               aggx[:, :].rearrange("e (b f) -> e b f", b=B),
                                               ge_row[0:E, :].unsqueeze(1).to_broadcast([E, B, F]), ALU.mult))
                st.wait()
                st.did(nc.vector.tensor_reduce(qs[:, 0, :], geb[:, :].rearrange("e (b f) -> e b f", b=B), X, ALU.add))
                st.wait()

        heT = sb("heT", [P, BP, E], scope=l0a)
        th = sb("th", [P, 2, BP, E], scope=l0a)
        exg = sb("exg", [E, BF], scope=l0a)
        sc = adjN[:, BP:2 * BP, :].rearrange("p q (a b e) -> p (q a) b e", a=2, b=B)
        se_bc = sb("se_bc", [P, B, E], scope=l0a)
        e_exp, e_v, e_tr, e_z, e_th, e_se, e_sc = (sem(f"edge_{s}") for s in ("exp", "v", "tr", "z", "th", "se", "sc"))
        with nc.Block() as block:
            @block.scalar
            def _(eng):
                nc.scalar.activation(exg[:, :], aggx[:, :], ACT.Exp).then_inc(e_exp, 1)
                eng.wait_ge(e_z, 1)
                for h in range(2):
                    nc.scalar.activation(th[:, h, :, :].rearrange("k b e -> k (b e)"), bank[[1, 4][h]][:, 0:BP * E],
                                         ACT.Tanh, bias=fcb_col[:, :]).then_inc(e_th, 1)

            @block.tensor
            def _(eng):
                eng.wait_ge(e_v, 2)
                for bp in range(BP):
                    mm = nc.tensor.transpose(bank[0][:, bp * E:(bp + 1) * E], geb[:, bp * P:(bp + 1) * P],
                                             ident[0:E, 0:E])
                mm.then_inc(e_tr, 1)
                eng.wait_ge(e_v, 3)
                for h in range(2):
                    s = slice(h * F, (h + 1) * F)
                    mm = nc.tensor.matmul(bank[[1, 4][h]][:, 0:BP * E], fcW_s[s, :],
                                          heT[s, :, :].rearrange("f b e -> f (b e)"), start=True, stop=True)
                mm.then_inc(e_z, 1)
                eng.wait_ge(e_th, 2)
                nc.tensor.matmul(bank[2][:, :], av_rep[:, :], th[:, :, :, :].rearrange("k a b e -> k (a b e)"),
                                 start=True, stop=True)
                for b in range(B):
                    mm = nc.tensor.matmul(bank[3][0:E, b:b + 1], th[:, b % 2, b // 2, :], av_col[:, :],
                                          start=True, stop=True)
                mm.then_inc(e_se, 1)

            @block.vector
            def _(eng):
                st = Steps(eng, e_v)
                st.did(nc.vector.tensor_scalar(geb[:, :], aggx[:, :], 0.0, -1.0, ALU.max, ALU.add))
                eng.wait_ge(e_exp, 1)
                st.wait()
                st.did(nc.vector.scalar_tensor_tensor(geb[:, :], exg[:, :], 1.0, geb[:, :], ALU.min, ALU.add))
                eng.wait_ge(e_tr, 1)
                st.did(nc.vector.tensor_copy(heT[:, :, :].rearrange("f b e -> f (b e)"), bank[0][:, 0:BP * E]))
                eng.wait_ge(e_se, 1)
                st.did(nc.vector.tensor_copy(qs[:, 1, :], bank[3][0:E, 0:B]))
                st.did(nc.vector.tensor_copy(se_bc[:, :, :].rearrange("p (q a) e -> p a q e", a=2),
                                             bank[2][:, :].rearrange("p (a q e) -> p a q e", a=2, e=E)))
                st.wait()
                for t in range(T):
                    st.did(nc.vector.tensor_tensor(sc[:, t, :, :], se_bc[:, :, :],
                                                   MN[:, t, 0, :].unsqueeze(1).to_broadcast([P, B, E]), ALU.mult))
                st.wait()
                for t in range(T):
                    st.did(nc.vector.tensor_tensor(sc[:, t, :, :], sc[:, t, :, :],
                                                   NN[:, t, :].unsqueeze(1).to_broadcast([P, B, E]), ALU.add))
                st.wait()
                st.did(nc.vector.tensor_reduce(mx[:, :, :], sc[:, :, :, :], X, ALU.max))
                st.wait()

        l0a.close()

        l0b = ExitStack()
        kc = sb("kc", [P, 1], scope=l0b)
        zacc = sb("zacc", [P, T, B], scope=l0b)
        sel = sb("sel", [E, 2, N], scope=l0b)
        beta = sb("beta", [P, 2, T, B], scope=l0b)
        wgt = sb("wgt", [P, 2, T, B], scope=l0b)
        ex2 = sb("ex2", [P, 2, 2, T, B], scope=l0b)
        valid = sb("valid", [P, T], scope=l0b)
        R = 4
        dd, zz, ee = (adjN[:, 2 * i:2 * i + 2, :].rearrange("p q (a n) -> p (q a) n", a=2) for i in range(3))

        i_v = sem("init_v")
        with nc.Block() as block:
            @block.vector
            def _(eng):
                nc.vector.memset(acc[:, :, :], 0.0).then_inc(i_v, 1)
                nc.vector.memset(zacc[:, :, :], 0.0).then_inc(i_v, 1)
                nc.vector.memset(kc[:, :], 0.0).then_inc(i_v, 1)
                eng.wait_ge(i_v, 3)

        def slots_stage(name, count, guarded):
            sel_done, small_done, gath, small_v, exp2, b_done, d_done, d2_done, z_done, e_done, w_done, \
                wc_done, acc_done, kc_done, own_v = (sem(f"{name}_{s}") for s in (
                    "sel", "small", "gathered", "small_v", "exp2", "beta", "diff", "blend", "z", "elu_exp", "elu",
                    "weighed", "acc", "kc", "own_v"))

            def body(first, slot):
                def run(eng):
                    def loop():
                        first(eng)
                        with eng.Fori(0, count // 2 - 1) as i:
                            for u in range(2):
                                slot(eng, i * 2 + u, u, True, None if guarded else i)
                        for u in range(2):
                            slot(eng, count - 2 + u, u, u == 0, None)
                    if guarded:
                        need = eng.value_load(flags[0:1, 0:1], min_val=0, max_val=E)
                        with eng.If(need > BASE_SLOTS):
                            loop()
                    else:
                        loop()
                return run

            with nc.Block() as block:
                def next_rank(eng, k):
                    if not isinstance(k, int) or k > 0:
                        eng.wait_ge(b_done, k)
                    nc.gpsimd.tensor_tensor(kc[:, :], kc[:, :], one_col[:, :], ALU.add).then_inc(kc_done, 1)

                def pool(eng, k, u, more, part):
                    eng.wait_ge(b_done, k + 1)
                    if more:
                        next_rank(eng, k + 1)
                    for s in range(T + 2):
                        if s < T:
                            t = s
                            eng.wait_ge(d_done, k * T + t + 1)
                            nc.gpsimd.tensor_tensor(
                                dd[:, t % R, :].rearrange("p (b f) -> p b f", b=B),
                                dd[:, t % R, :].rearrange("p (b f) -> p b f", b=B),
                                beta[:, u, t, :].unsqueeze(2).to_broadcast([P, B, F]), ALU.mult)\
                                .then_inc(d2_done, 1)
                        if s >= 2:
                            t = s - 2
                            eng.wait_ge(w_done, k * T + t + 1)
                            nc.gpsimd.tensor_tensor(
                                ee[:, t % R, :].rearrange("p (b f) -> p b f", b=B),
                                ee[:, t % R, :].rearrange("p (b f) -> p b f", b=B),
                                wgt[:, u, t, :].unsqueeze(2).to_broadcast([P, B, F]), ALU.mult)\
                                .then_inc(wc_done, 1)
                body_pool = body(lambda eng: next_rank(eng, 0), pool)

                def small(eng, k, u):
                    eng.wait_ge(sel_done, k + 1)
                    if not isinstance(k, int) or k > 0:
                        eng.wait_ge(small_v, k)
                    for t in range(T):
                        mm = nc.tensor.matmul(bank[7][:, t * 16:(t + 1) * 16], sel[:, u, t * P:(t + 1) * P],
                                              qs[:, :, :].rearrange("e a b -> e (a b)"), start=True, stop=True)
                    mm.then_inc(small_done, 1)

                def tensor(eng, k, u, more, part):
                    for t in range(T):
                        if t < R:
                            eng.wait_ge(z_done, k * T)
                        else:
                            eng.wait_ge(z_done, k * T + t - R + 1)
                        nc.tensor.matmul(bank[t % R][:, :], sel[:, u, t * P:(t + 1) * P], aggx[:, :],
                                         start=True, stop=True).then_inc(gath, 1)
                        if part is not None:
                            if t == 0:
                                eng.wait_ge(ind_out, part * 2)
                            bp = 2 * u + t // 4
                            for mt in range(t % 4 * 2, t % 4 * 2 + 2):
                                mm = nc.tensor.matmul(bank[4 + u][:, bp % 2 * PART:(bp % 2 + 1) * PART],
                                                      hWi[:, mt, bp * P:(bp + 1) * P],
                                                      adjT[:, mt, bass.ts(part, PART)],
                                                      start=mt == 0, stop=mt == T - 1)
                            if t == T - 1:
                                mm.then_inc(ind_part, 1)
                        if more and t == 6:
                            small(eng, k + 1, 1 - u)
                body_tensor = body(lambda eng: small(eng, 0, 0), tensor)

                def weights_exp(eng, k, u):
                    eng.wait_ge(small_v, k + 1)
                    nc.scalar.activation(ex2[:, u, :, :, :].rearrange("p a t b -> p (a t b)"),
                                         ex2[:, u, :, :, :].rearrange("p a t b -> p (a t b)"), ACT.Exp)\
                        .then_inc(exp2, 1)

                def scalar(eng, k, u, more, part):
                    for t in range(T):
                        eng.wait_ge(z_done, k * T + t + 1)
                        if t < R:
                            eng.wait_ge(acc_done, k * T)
                        else:
                            eng.wait_ge(acc_done, k * T + t - R + 1)
                        nc.scalar.activation(ee[:, t % R, :], zz[:, t % R, :], ACT.Exp, bias=neg_one[:, :])\
                            .then_inc(e_done, 1)
                        if more and t == 5:
                            weights_exp(eng, k + 1, 1 - u)
                    if part is not None:
                        eng.wait_ge(ind_part, k + 1)
                        nc.scalar.activation(hT[:, 2 * u:2 * u + 2, bass.ts(part, PART)],
                                             bank[4 + u].rearrange("p (a n) -> p a n", a=2), ACT.Copy)\
                            .then_inc(ind_out, 1)
                body_scalar = body(lambda eng: weights_exp(eng, 0, 0), scalar)

                OWN = 6

                def choice(eng, k, u):
                    eng.wait_ge(kc_done, k + 1)
                    if not isinstance(k, int) or k > 1:
                        eng.wait_ge(gath, (k - 1) * T)
                    nc.vector.tensor_scalar(sel[:, u, :], rankT[:, :], kc[0:E, :], None, ALU.is_equal)\
                        .then_inc(sel_done, 1)

                def exponents(eng, k, u):
                    eng.wait_ge(small_done, k + 1)
                    sm = bank[7][:, 0:T * 16].rearrange("p (t a b) -> p a t b", a=2, b=B)
                    nc.vector.scalar_tensor_tensor(ex2[:, u, 0, :, :], sm[:, 0], -1.0, p_n[:, :, :],
                                                   ALU.mult, ALU.subtract).then_inc(own_v, 1)
                    nc.vector.tensor_tensor(ex2[:, u, 1, :, :], sm[:, 1], mx[:, :, :], ALU.subtract)\
                        .then_inc(own_v, 1)
                    eng.wait_ge(own_v, k * OWN + 2)
                    nc.vector.tensor_tensor(ex2[:, u, 1, :, :], ex2[:, u, 1, :, :],
                                            ne[:, :].unsqueeze(2).to_broadcast([P, T, B]), ALU.mult)\
                        .then_inc(small_v, 1)
                    nc.vector.tensor_scalar(valid[:, :], cnt[:, :], kc[:, :], None, ALU.is_ge).then_inc(own_v, 1)

                def weights(eng, k, u):
                    eng.wait_ge(exp2, k + 1)
                    if not isinstance(k, int) or k > 1:
                        eng.wait_ge(wc_done, (k - 1) * T)
                    nc.vector.tensor_scalar(beta[:, u, :, :], ex2[:, u, 0, :, :], 1.0, None, ALU.add)\
                        .then_inc(own_v, 1)
                    eng.wait_ge(own_v, k * OWN + 4)
                    nc.vector.reciprocal(beta[:, u, :, :], beta[:, u, :, :]).then_inc(own_v, 1)
                    nc.vector.tensor_tensor(wgt[:, u, :, :], ex2[:, u, 1, :, :],
                                            valid[:, :].unsqueeze(2).to_broadcast([P, T, B]), ALU.mult)\
                        .then_inc(own_v, 1)
                    eng.wait_ge(own_v, k * OWN + 6)
                    if not isinstance(k, int) or k > 0:
                        eng.wait_ge(b_done, k)
                    nc.vector.tensor_tensor(zacc[:, :, :], zacc[:, :, :], wgt[:, u, :, :], ALU.add)\
                        .then_inc(b_done, 1)

                def vector(eng, k, u, more, part):
                    for s in range(T + 3):
                        if s < T:
                            t = s
                            eng.wait_ge(gath, k * T + t + 1)
                            nc.vector.tensor_tensor(dd[:, t % R, :], hW[:, t, :], bank[t % R][:, :],
                                                    ALU.subtract).then_inc(d_done, 1)
                        if 1 <= s < T + 1:
                            t = s - 1
                            eng.wait_ge(d2_done, k * T + t + 1)
                            nc.vector.scalar_tensor_tensor(zz[:, t % R, :], dd[:, t % R, :], 1.0,
                                                           bank[t % R][:, :], ALU.add, ALU.add)\
                                .then_inc(z_done, 1)
                        if 2 <= s < T + 2:
                            t = s - 2
                            eng.wait_ge(e_done, k * T + t + 1)
                            nc.vector.scalar_tensor_tensor(ee[:, t % R, :], ee[:, t % R, :], 1.0,
                                                           zz[:, t % R, :], ALU.min, ALU.max)\
                                .then_inc(w_done, 1)
                        if s >= 3:
                            t = s - 3
                            eng.wait_ge(wc_done, k * T + t + 1)
                            nc.vector.tensor_tensor(acc[:, t, :], acc[:, t, :], ee[:, t % R, :], ALU.add)\
                                .then_inc(acc_done, 1)
                        if more and s == 2:
                            choice(eng, k + 1, 1 - u)
                        if more and s == 6:
                            exponents(eng, k + 1, 1 - u)
                        if more and s == 8:
                            weights(eng, k + 1, 1 - u)
                    eng.wait_ge(acc_done, (k + 1) * T)

                def vector_first(eng):
                    choice(eng, 0, 0)
                    exponents(eng, 0, 0)
                    weights(eng, 0, 0)
                body_vector = body(vector_first, vector)

                block.gpsimd(body_pool)
                block.tensor(body_tensor)
                block.scalar(body_scalar)
                block.vector(body_vector)

        neg_one = sb("neg_one", [P, 1], scope=l0b)
        n1 = sem("neg_one_set")
        with nc.Block() as block:
            @block.vector
            def _(eng):
                nc.vector.memset(neg_one[:, :], -1.0).then_inc(n1, 1)
                eng.wait_ge(n1, 1)

        PART = N // (BASE_SLOTS // 2 - 1)
        ind_part, ind_out = sem("industry_part"), sem("industry_out")
        slots_stage("slots", BASE_SLOTS, False)
        slots_stage("more_slots", E - BASE_SLOTS, True)

        ind = hn
        i_done, i_read, g_v = sem("ind_done"), sem("ind_read"), sem("g_v")
        with nc.Block() as block:
            @block.tensor
            def _(eng):
                for nt in range(T):
                    for bp in range(BP):
                        mm = nc.tensor.transpose(bank[nt][:, bp * P:(bp + 1) * P], hT[:, bp, nt * P:(nt + 1) * P],
                                                 ident[:, :])
                    mm.then_inc(i_done, 1)

            @block.scalar
            def _(eng):
                for nt in range(T):
                    eng.wait_ge(i_done, nt + 1)
                    nc.scalar.activation(ind[:, nt, :], bank[nt][:, :], ACT.Copy, scale=deg[:, nt:nt + 1])\
                        .then_inc(i_read, 1)
                eng.wait_ge(i_read, T)

            @block.vector
            def _(eng):
                st = Steps(eng, g_v)
                st.did(nc.vector.reciprocal(zacc[:, :, :], zacc[:, :, :]))
                st.wait()
                st.did(nc.vector.tensor_tensor(views(acc), views(acc),
                                               zacc[:, :, :].rearrange("p t b -> p (t b)").unsqueeze(2)
                                               .to_broadcast([P, T * B, F]), ALU.mult))
                st.wait()
                st.did(nc.vector.tensor_scalar(acc[:, :, :], acc[:, :, :], -1.0, None, ALU.add))
                st.wait()
        l0b.close()

        l0c = ExitStack()
        avd = sb("avd", [P, B, B], scope=l0c)
        scT = sb("scT", [B, N], scope=l0c)
        a_set = sem("avd_set")
        with nc.Block() as block:
            @block.vector
            def _(eng):
                nc.vector.memset(avd[:, :, :], 0.0).then_inc(a_set, 1)
                eng.wait_ge(a_set, 1)
                for b in range(B):
                    nc.vector.tensor_copy(avd[:, b, b:b + 1], av_col[:, :]).then_inc(a_set, 1)
                eng.wait_ge(a_set, 1 + B)
        thp = sb("thp", [P, 3, HALF], scope=l0c)
        scp = sb("scp", [P, 2, T, B], scope=l0c)
        dif = sb("dif", [P, T, B], scope=l0c)
        for kind, src in enumerate((ind, acc)):
            transpose_stage(f"pair{kind}_t", natural_to_transposed(src, hT))
            z_d, th_d, sc_d, sc_c, nat_d = (sem(f"pair{kind}_{s}") for s in ("z", "tanh", "score", "copied", "natural"))
            with nc.Block() as block:
                @block.tensor
                def _(eng):
                    def scores(i):
                        h, b = divmod(i, B)
                        eng.wait_ge(th_d, i + 1)
                        nc.tensor.matmul(bank[4 + h][0:B, :], avd[:, b, :], thp[:, i % 3, :],
                                         start=b == 0, stop=b == B - 1).then_inc(sc_d, 1)
                    for i in range(2 * B):
                        h, b = divmod(i, B)
                        s = slice(b % 2 * F, (b % 2 + 1) * F)
                        if i >= 3:
                            eng.wait_ge(th_d, i - 2)
                        nc.tensor.matmul(bank[i % 3][:, :], fcW_s[s, :], hT[s, b // 2, h * HALF:(h + 1) * HALF],
                                         start=True, stop=True).then_inc(z_d, 1)
                        if i >= 2:
                            scores(i - 2)
                    scores(2 * B - 2)
                    scores(2 * B - 1)
                    eng.wait_ge(sc_c, 2)
                    for t in range(T):
                        mm = nc.tensor.matmul(bank[6][:, t * B:(t + 1) * B], scT[:, t * P:(t + 1) * P],
                                              ident[0:B, 0:B], start=True, stop=True)
                    mm.then_inc(nat_d, 1)

                @block.scalar
                def _(eng):
                    for i in range(2 * B):
                        eng.wait_ge(z_d, i + 1)
                        if i >= 3:
                            eng.wait_ge(sc_d, i - 2)
                        nc.scalar.activation(thp[:, i % 3, :], bank[i % 3][:, :], ACT.Tanh, bias=fcb_col[:, :])\
                            .then_inc(th_d, 1)

                @block.vector
                def _(eng):
                    for h in range(2):
                        eng.wait_ge(sc_d, (h + 1) * B)
                        nc.vector.tensor_copy(scT[:, h * HALF:(h + 1) * HALF], bank[4 + h][0:B, :]).then_inc(sc_c, 1)
                    eng.wait_ge(nat_d, 1)
                    nc.vector.tensor_copy(scp[:, kind, :, :].rearrange("p t b -> p (t b)"),
                                          bank[6][:, 0:T * B]).then_inc(sc_c, 1)
                    eng.wait_ge(sc_c, 3)

        f_v, f_s = sem("mix_v"), sem("mix_s")
        with nc.Block() as block:
            @block.vector
            def _(eng):
                st = Steps(eng, f_v)
                st.did(nc.vector.tensor_tensor(dif[:, :, :], scp[:, 1, :, :], scp[:, 0, :, :], ALU.subtract))
                st.did(nc.vector.tensor_tensor(ind[:, :, :], ind[:, :, :], acc[:, :, :], ALU.subtract))
                st.did(nc.vector.tensor_tensor(xs[:, :, :], xs[:, :, :], acc[:, :, :], ALU.add))
                eng.wait_ge(f_s, 1)
                st.did(nc.vector.tensor_scalar(dif[:, :, :], dif[:, :, :], 1.0, None, ALU.add))
                st.wait()
                st.did(nc.vector.reciprocal(dif[:, :, :], dif[:, :, :]))
                st.wait()
                st.did(nc.vector.tensor_tensor(views(ind), views(ind),
                                               dif[:, :, :].rearrange("p t b -> p (t b)").unsqueeze(2)
                                               .to_broadcast([P, T * B, F]), ALU.mult))
                st.wait()
                st.did(nc.vector.tensor_tensor(xs[:, :, :], xs[:, :, :], ind[:, :, :], ALU.add))
                st.wait()

            @block.scalar
            def _(eng):
                eng.wait_ge(f_v, 1)
                nc.scalar.activation(dif[:, :, :], dif[:, :, :], ACT.Exp).then_inc(f_s, 1)
        l0c.close()
        l0.close()
        retire_semaphores()

        l1 = ExitStack()
        effT = sb("effT", [P, BP, N], scope=l1)
        hidT = sb("hidT", [P, BP, N], scope=l1)
        layernorm_stage("ln1", xs, hn, effT[:, :, :].rearrange("p b (c n) -> p (b c) n", c=2))
        iv_in = sem("intervention_in")
        with nc.Block() as block:
            @block.sync
            def _(eng):
                for b in range(B):
                    eng.dma_start(hn[0:1, 0, b * F:(b + 1) * F], iv).then_inc(iv_in, 16)
                eng.wait_ge(iv_in, 16 * B)
        transpose_stage("v_t", natural_to_transposed(hn, hT))
        b2_b = b2_row[:, :].unsqueeze(1).to_broadcast([P, 2, F])

        e_d, e_c, h_d, h_c, v_d, v_c, n_d, n_c = (sem(f"l1_{s}") for s in (
            "effects", "effects_out", "hidden", "hidden_out", "vT", "vT_out", "v", "v_out"))
        G = BP * 2
        with nc.Block() as block:
            @block.tensor
            def _(eng):
                with eng.Fori(0, MAX_STEPS) as step:
                    eng.wait_ge(n_c, step * 4 * T)
                    for g in range(G):
                        bp, h = divmod(g, 2)
                        if g < 2:
                            eng.wait_ge(e_c, step * G)
                        else:
                            eng.wait_ge(e_c, step * G + g - 1)
                        for mt in range(T):
                            mm = nc.tensor.matmul(bank[g % 2][:, :], hn[:, mt, bp * P:(bp + 1) * P],
                                                  adjT[:, mt, h * HALF:(h + 1) * HALF],
                                                  start=mt == 0, stop=mt == T - 1)
                        mm.then_inc(e_d, 1)
                    for g in range(G):
                        bp, h = divmod(g, 2)
                        s = slice(h * HALF, (h + 1) * HALF)
                        if g == 0:
                            eng.wait_ge(v_c, step * G)
                        eng.wait_ge(e_c, step * G + g + 1)
                        if g < 2:
                            eng.wait_ge(h_c, step * G)
                        else:
                            eng.wait_ge(h_c, step * G + g - 1)
                        nc.tensor.matmul(bank[2 + g % 2][:, :], bd[:, 0, :], hT[:, bp, s], start=True, stop=False)
                        nc.tensor.matmul(bank[2 + g % 2][:, :], bd[:, 1, :], effT[:, bp, s], start=False, stop=True)\
                            .then_inc(h_d, 1)
                    for g in range(G):
                        bp, h = divmod(g, 2)
                        s = slice(h * HALF, (h + 1) * HALF)
                        eng.wait_ge(h_c, step * G + g + 1)
                        if g < 2:
                            eng.wait_ge(v_c, step * G)
                        else:
                            eng.wait_ge(v_c, step * G + g - 1)
                        nc.tensor.matmul(bank[4 + g % 2][:, :], bd[:, 2, :], hidT[:, bp, s], start=True, stop=True)\
                            .then_inc(v_d, 1)
                        for j in range(4):
                            q = g * 4 + j
                            if j == 0:
                                if g < 2:
                                    eng.wait_ge(n_c, step * 4 * T)
                                else:
                                    eng.wait_ge(n_c, step * 4 * T + (g - 1) * 4)
                            mm = nc.tensor.matmul(bank[6 + g % 2][:, j * P:(j + 1) * P],
                                                  hidT[:, bp, (h * 4 + j) * P:(h * 4 + j + 1) * P], bd[:, 2, :],
                                                  start=True, stop=True)
                        mm.then_inc(n_d, 1)

            @block.scalar
            def _(eng):
                with eng.Fori(0, MAX_STEPS) as step:
                    for g in range(G):
                        bp, h = divmod(g, 2)
                        eng.wait_ge(e_d, step * G + g + 1)
                        nc.scalar.activation(effT[:, bp, h * HALF:(h + 1) * HALF], bank[g % 2][:, :], ACT.Copy)\
                            .then_inc(e_c, 1)
                    for g in range(G):
                        bp, h = divmod(g, 2)
                        eng.wait_ge(h_d, step * G + g + 1)
                        nc.scalar.activation(hidT[:, bp, h * HALF:(h + 1) * HALF], bank[2 + g % 2][:, :], ACT.Relu,
                                             bias=b1_col[:, :]).then_inc(h_c, 1)
                    for g in range(G):
                        bp, h = divmod(g, 2)
                        eng.wait_ge(v_d, step * G + g + 1)
                        nc.scalar.activation(hT[:, bp, h * HALF:(h + 1) * HALF], bank[4 + g % 2][:, :], ACT.Identity,
                                             bias=b2_col[:, :]).then_inc(v_c, 1)

            @block.vector
            def _(eng):
                with eng.Fori(0, MAX_STEPS) as step:
                    for g in range(G):
                        bp, h = divmod(g, 2)
                        eng.wait_ge(n_d, step * G + g + 1)
                        for j in range(4):
                            t = h * 4 + j
                            nc.vector.tensor_tensor(
                                hn[:, t, bp * P:(bp + 1) * P].rearrange("p (a f) -> p a f", a=2),
                                bank[6 + g % 2][:, j * P:(j + 1) * P].rearrange("p (a f) -> p a f", a=2),
                                b2_b, ALU.add).then_inc(n_c, 1)
                eng.wait_ge(n_c, MAX_STEPS * 4 * T)
        l1.close()
        retire_semaphores()

        l2 = ExitStack()
        r2 = sb("r2", [P, T, BF], scope=l2)
        layernorm_stage("ln2", xs, hn, r2, adds=hn, to=hT)

        Wh_s = sb("Wh_s", [P, HEADS, HID], scope=l2)
        Wo_s = sb("Wo_s", [P, HEADS, F], scope=l2)
        bh_s = sb("bh_s", [P, HEADS], scope=l2)
        GG = sb("GG", [F, HP, P], scope=l2)
        WT = r2[:, 0, :].rearrange("p (h f) -> p h f", h=HEADS)
        w_in, w_t, w_tc, g_d, g_c = (sem(f"l2_{s}") for s in ("w", "wt", "wt_out", "g", "g_out"))
        with nc.Block() as block:
            @block.sync
            def _(eng):
                for h in range(2):
                    eng.dma_start(Wh_s[h * F:(h + 1) * F, :, :], Wh.rearrange("h f d -> f h d")).then_inc(w_in, 16)
                eng.dma_start(Wo_s[:, :, :], W_out.rearrange("(h d) o -> d h o", d=HID)).then_inc(w_in, 16)
                for h in range(HEADS):
                    eng.dma_start(bh_s[:, h:h + 1], bh[h, :].unsqueeze(1)).then_inc(w_in, 16)
                eng.wait_ge(w_in, 16 * (3 + HEADS))

            @block.tensor
            def _(eng):
                eng.wait_ge(w_in, 16 * (3 + HEADS))
                for h in range(HEADS):
                    mm = nc.tensor.transpose(bank[0][:, h * F:(h + 1) * F], Wh_s[0:F, h, :], ident[0:F, 0:F])
                mm.then_inc(w_t, 1)
                eng.wait_ge(w_tc, 1)
                for h in range(HEADS):
                    mm = nc.tensor.matmul(bank[1][0:F, h * F:(h + 1) * F], WT[:, h, :], WT[:, h, :],
                                          start=True, stop=True)
                mm.then_inc(g_d, 1)

            @block.vector
            def _(eng):
                eng.wait_ge(w_t, 1)
                nc.vector.tensor_copy(WT[:, :, :].rearrange("d h f -> d (h f)"), bank[0][:, :]).then_inc(w_tc, 1)
                eng.wait_ge(g_d, 1)
                nc.vector.tensor_copy(GG[:, :, :].rearrange("f a c -> f (a c)"), bank[1][0:F, :]).then_inc(g_c, 1)
                eng.wait_ge(g_c, 1)

        lo = sb("lo", [P, 1], scope=l2)

        l2a = ExitStack()
        iota1 = sb("iota1", [P, CAP], scope=l2a)
        adjB = sb("adjB", [P, T, N], bf16, scope=l2a)
        idT = sb("idT", [P, 2, F], bf16, scope=l2a)
        xsp = [sb(f"x{j + 1}", [P, T, BF], bf16, scope=l2a) for j in range(3)]
        in_xs, in_hn = (a[:, :, :].rearrange("p t n -> p (t n)").bitcast(bf16)
                        .rearrange("p (a b c) -> p a b c", a=2, b=B) for a in (xs, hn))
        Sel = in_hn[:, 0]
        RA, RB, RC = in_xs[:, 0], in_xs[:, 1], in_hn[:, 1]
        LA, LC = (sb(f"L{c}", [P, 2, HEADS, P], bf16, scope=l2a) for c in "AC")
        Y1 = sb("Y1", [P, HEADS * P], bf16, scope=l2a)
        YR = sb("YR", [P, HEADS * P], scope=l2a)
        Y2 = sb("Y2", [P, HEADS * P], bf16, scope=l2a)
        GD = sb("GD", [F, HEADS, 2, F], scope=l2a)
        xq = sb("xq", [F, B, P], scope=l2a)
        adjc = sb("adjc", [P, CAP], scope=l2a)
        Vc = sb("Vc", [P, B, CT, F + 1], scope=l2a)
        Uc = sb("Uc", [P, 2, CAP], scope=l2a)
        iota_i = Uc[:, 0, :].bitcast(i32)
        Pc = sb("Pc", [P, 2, CAP], scope=l2a)
        PTc = sb("PTc", [P, 2, CAP], scope=l2a)
        mst = sb("mst", [P, B * HEADS], scope=l2a)
        nmc = sb("nmc", [P, 2], scope=l2a)
        rzc = sb("rzc", [P, 2], scope=l2a)
        low = sb("low", [P, 1], scope=l2a)
        tick = sb("tick", [P, 1], scope=l2a)
        ob = sb("ob", [P, 2, HEADS * F], scope=l2a)
        oTc = sb("oTc", [P, HALF], scope=l2a)
        catc = sb("catc", [P, HEADS, P], scope=l2a)
        bh_aq = sb("bh_aq", [P, HEADS], scope=l2a)

        c_g, c_v, c_s, c_s2, c_p, c_d = (sem(f"split_{n}") for n in ("consts", "v", "s", "adj", "p", "d"))
        saved = nc.dram_tensor("saved", (2, P, T, BF), fp32).ap()
        c_out = sem("split_saved")
        SHARE = 5

        def differences(eng, unit, t0, t1, done):
            eng.wait_ge(c_s, 1)
            unit.tensor_tensor(r2[:, t0:t1, :], hn[:, t0:t1, :], xsp[0][:, t0:t1, :], ALU.subtract).then_inc(done, 1)
            eng.wait_ge(c_s, 2)
            eng.wait_ge(done, 1)
            unit.tensor_tensor(xsp[2][:, t0:t1, :], r2[:, t0:t1, :], xsp[1][:, t0:t1, :], ALU.subtract)\
                .then_inc(done, 1)
            eng.wait_ge(done, 2)

        with nc.Block() as block:
            @block.sync
            def _(eng):
                for j, a in enumerate((xs, hn)):
                    eng.dma_start(saved[j], a[:, :, :]).then_inc(c_out, 16)
                eng.wait_ge(c_out, 32)

            @block.gpsimd
            def _(eng):
                nc.gpsimd.iota(iota_i, pattern=[[1, CAP]], base=1, channel_multiplier=0).then_inc(c_g, 1)
                nc.gpsimd.memset(Vc[:, :, :, F:F + 1], 1.0).then_inc(c_g, 1)
                differences(eng, nc.gpsimd, SHARE, T, c_p)
                eng.wait_ge(c_g, 2)

            @block.scalar
            def _(eng):
                nc.scalar.activation(xsp[0][:, :, :], hn[:, :, :], ACT.Copy).then_inc(c_s, 1)
                eng.wait_ge(c_p, 1)
                eng.wait_ge(c_d, 1)
                nc.scalar.activation(xsp[1][:, :, :], r2[:, :, :], ACT.Copy).then_inc(c_s, 1)
                nc.scalar.activation(adjB[:, :, :], adjT[:, :, :], ACT.Copy).then_inc(c_s2, 1)
                eng.wait_ge(c_s2, 1)

            @block.vector
            def _(eng):
                st = Steps(eng, c_v)
                st.did(nc.vector.memset(idT[:, :, :], 0.0))
                st.did(nc.vector.memset(lo[:, :], NEG_GAT * 4))
                for a in range(2):
                    st.did(nc.vector.tensor_copy(GD[:, :, a, :], GG[:, :, :].rearrange("f q (a c) -> f (q a) c", a=2)))
                    st.did(nc.vector.tensor_copy(bh_aq[:, a * HP:(a + 1) * HP], bh_s[:, a:HEADS:2]))
                st.wait()
                for a in range(2):
                    s = slice(a * F, (a + 1) * F)
                    st.did(nc.vector.tensor_copy(idT[s, a, :], ident[s, s]))
                eng.wait_ge(c_g, 1)
                st.did(nc.vector.tensor_copy(iota1[:, :], iota_i))
                differences(eng, nc.vector, 0, SHARE, c_d)
                st.wait()

        f = {n: sem(f"quick_{n}") for n in (
            "sel", "xq", "gathered", "ga", "gv", "adj", "adj_out", "v", "v_out",
            "y", "y1", "yr", "y2", "copied", "y3", "s", "u", "own", "p", "tr", "tr_out", "o", "rz", "norm",
            "ot", "ot_out", "cat", "bias", "leaky", "h2", "h2_out", "lo", "tmin")}
        J = B * HEADS
        O_bank = [bank[2], bank[5]]
        G_bank = [bank[0], bank[1], bank[3], bank[4]]

        def tile_of(t):
            return slice(t * P, (t + 1) * P) if isinstance(t, int) else bass.ts(t, P)

        def column_of(t):
            return slice(t, t + 1) if isinstance(t, int) else bass.ds(t, 1)

        with nc.Block() as block:
            @block.tensor
            def _(eng):
                def gather(t, ks):
                    for k in ks:
                        bp, j = divmod(k, 3)
                        if k == 0:
                            eng.wait_ge(f["u"], t * J)
                            for mt in range(T):
                                eng.wait_ge(f["sel"], t * T + mt + 1)
                        if k in (2, 3):
                            eng.wait_ge(f["tr_out"], t * J)
                        if k >= 4:
                            w, jj = divmod(k - 4, 3)
                            if jj == 0:
                                eng.wait_ge(f["ga"], t * BP + w + 1)
                            else:
                                eng.wait_ge(f["gv"], t * 2 * BP + 2 * w + jj)
                        for mt in range(T):
                            mm = nc.tensor.matmul(G_bank[k % 4], xsp[j][:, mt, bp * P:(bp + 1) * P], Sel[:, mt, :],
                                                  start=mt == 0, stop=mt == T - 1)
                        mm.then_inc(f["gathered"], 1)

                def rows_and_adj(t):
                    eng.wait_ge(f["norm"], t * J)
                    for mt in range(T):
                        mm = nc.tensor.matmul(bank[2], adjB[:, mt, tile_of(t)], Sel[:, mt, :],
                                              start=mt == 0, stop=mt == T - 1)
                    mm.then_inc(f["adj"], 1)
                    eng.wait_ge(f["y1"], t * B + 1)
                    eng.wait_ge(f["yr"], t * B + 1)
                    for w in range(BP):
                        eng.wait_ge(f["ga"], t * BP + w + 1)
                        eng.wait_ge(f["gv"], (t * BP + w + 1) * 2)
                        if w == 3:
                            eng.wait_ge(f["v_out"], t * BP + 1)
                        for g in range(2 * CT):
                            b, c = 2 * w + g // CT, g % CT
                            cs = slice(c * P, (c + 1) * P)
                            dst = bank[[5, 6, 7, 5][w]][:, g * F:(g + 1) * F]
                            nc.tensor.matmul(dst, RA[:, b, cs], idT[:, 0, :], start=True, stop=False)
                            nc.tensor.matmul(dst, RB[:, b, cs], idT[:, 0, :], start=False, stop=False)
                            mm = nc.tensor.matmul(dst, RC[:, b, cs], idT[:, 1, :], start=False, stop=True)
                        mm.then_inc(f["v"], 1)

                def queries(t, b):
                    eng.wait_ge(f["xq"], (t + 1) * 2)
                    if b == 0:
                        eng.wait_ge(f["h2_out"], t * B)
                        eng.wait_ge(f["leaky"], t * B)
                    else:
                        eng.wait_ge(f["yr"], t * B + b)
                        eng.wait_ge(f["h2_out"], t * B + max(b - 2, 0))
                        if b == 1:
                            eng.wait_ge(f["v_out"], (t + 1) * BP)
                    for h in range(HEADS):
                        mm = nc.tensor.matmul(bank[6 + h // 4][:, h % 4 * P:(h % 4 + 1) * P],
                                              GD[:, h, :, :].rearrange("f a c -> f (a c)"), xq[:, b, :],
                                              start=True, stop=True)
                    mm.then_inc(f["y"], 1)

                def scores(t, j):
                    b, i = divmod(j, HEADS)
                    if i == 0:
                        eng.wait_ge(f["y2"], t * B + b + 1)
                        eng.wait_ge(f["copied"], t * B + b + 1)
                        eng.wait_ge(f["y3"], t * B + b + 1)
                    if j >= 2:
                        eng.wait_ge(f["u"], t * J + j - 1)
                    dst = bank[j % 2]
                    nc.tensor.matmul(dst, LA[:, b % 2, i, :], RA[:, b, :], start=True, stop=False)
                    nc.tensor.matmul(dst, LA[:, b % 2, i, :], RB[:, b, :], start=False, stop=False)
                    nc.tensor.matmul(dst, LC[:, b % 2, i, :], RC[:, b, :], start=False, stop=True)\
                        .then_inc(f["s"], 1)

                def transposes(t, k):
                    eng.wait_ge(f["p"], t * J + k + 1)
                    if k >= 2:
                        eng.wait_ge(f["tr_out"], t * J + k - 1)
                    for c in range(CT):
                        mm = nc.tensor.transpose(bank[3 + k % 2][:, c * P:(c + 1) * P],
                                                 Pc[:, k % 2, c * P:(c + 1) * P], ident[:, :])
                    mm.then_inc(f["tr"], 1)

                def values(t, k):
                    eng.wait_ge(f["tr_out"], t * J + k + 1)
                    if k >= 2:
                        eng.wait_ge(f["norm"], t * J + k - 1)
                    for c in range(CT):
                        mm = nc.tensor.matmul(O_bank[k % 2][:, 0:F + 1], PTc[:, k % 2, c * P:(c + 1) * P],
                                              Vc[:, k // HEADS, c, :], start=c == 0, stop=c == CT - 1)
                    mm.then_inc(f["o"], 1)

                def heads_transposed(t, w):
                    eng.wait_ge(f["norm"], t * J + (w + 1) * HEADS)
                    eng.wait_ge(f["y1"], t * B + min(w + 3, B))
                    eng.wait_ge(f["yr"], t * B + min(w + 3, B))
                    eng.wait_ge(f["h2_out"], t * B + w)
                    for c in range(4):
                        mm = nc.tensor.transpose(bank[6][:, c * P:(c + 1) * P],
                                                 ob[:, w % 2, c * P:(c + 1) * P], ident[:, :])
                    mm.then_inc(f["ot"], 1)

                def heads_weighed(t, w):
                    eng.wait_ge(f["ot_out"], t * B + w + 1)
                    for a in range(2):
                        s = slice(a * F, (a + 1) * F)
                        for c in range(HP):
                            mm = nc.tensor.matmul(bank[6 + a][:, c * P:(c + 1) * P],
                                                  Wh_s[s, 2 * c + a, :], oTc[s, c * P:(c + 1) * P],
                                                  start=True, stop=True)
                    mm.then_inc(f["cat"], 1)

                def heads_joined(t, w):
                    eng.wait_ge(f["leaky"], t * B + w + 1)
                    for c in range(HEADS):
                        mm = nc.tensor.matmul(bank[6][:, 0:F], catc[:, c, :], Wo_s[:, 2 * (c % HP) + c // HP, :],
                                              start=c == 0, stop=c == HEADS - 1)
                    mm.then_inc(f["h2"], 1)

                def steps(t):
                    for j in range(J):
                        b, i = divmod(j, HEADS)
                        if i == 1 and b >= 2:
                            heads_joined(t, b - 2)
                        scores(t, j)
                        if j >= 2:
                            transposes(t, j - 2)
                        if j >= 3:
                            values(t, j - 3)
                        if i == 1 and b + 1 < B:
                            queries(t, b + 1)
                        if i == 4 and b >= 1:
                            heads_transposed(t, b - 1)
                        if i == 6 and b >= 1:
                            heads_weighed(t, b - 1)

                def tail(t, more):
                    transposes(t, J - 2)
                    values(t, J - 3)
                    heads_joined(t, B - 2)
                    more(range(0, 2))
                    transposes(t, J - 1)
                    values(t, J - 2)
                    values(t, J - 1)
                    more(range(2, 4))
                    heads_transposed(t, B - 1)
                    more(range(4, 6))
                    heads_weighed(t, B - 1)
                    more(range(6, 8))
                    heads_joined(t, B - 1)

                gather(0, range(8))
                queries(0, 0)
                gather(0, range(8, 3 * BP))
                rows_and_adj(0)
                with eng.Fori(0, T - 1) as t:
                    steps(t)
                    tail(t, lambda ks: gather(t + 1, ks))
                    gather(t + 1, [8])
                    queries(t + 1, 0)
                    gather(t + 1, range(9, 3 * BP))
                    rows_and_adj(t + 1)
                steps(T - 1)
                tail(T - 1, lambda ks: None)

            @block.scalar
            def _(eng):
                def gathered(t, bp):
                    eng.wait_ge(f["gathered"], t * 3 * BP + 3 * bp + 1)
                    for a in range(2):
                        src = G_bank[3 * bp % 4][a * F:(a + 1) * F, :]
                        b = 2 * bp + a
                        nc.scalar.activation(RA[0:F, b, :], src, ACT.Copy)
                        nc.scalar.activation(RA[F:P, b, :], src, ACT.Copy)
                        ins = nc.scalar.activation(RC[0:F, b, :], src, ACT.Copy)
                    ins.then_inc(f["ga"], 1)

                def adj_out(t):
                    eng.wait_ge(f["adj"], t + 1)
                    eng.wait_ge(f["u"], t * J)
                    nc.scalar.activation(adjc[:, :], bank[2], ACT.Copy).then_inc(f["adj_out"], 1)

                def queries_1(t, b):
                    eng.wait_ge(f["y"], t * B + b + 1)
                    eng.wait_ge(f["copied"], t * B + b)
                    nc.scalar.activation(Y1[:, :], ps[:, 6:8, :].rearrange("p a c -> p (a c)"), ACT.Copy)\
                        .then_inc(f["y1"], 1)

                def queries_2(t, b):
                    eng.wait_ge(f["yr"], t * B + b + 1)
                    eng.wait_ge(f["y3"], t * B + b)
                    nc.scalar.activation(Y2[:, :], YR[:, :], ACT.Copy).then_inc(f["y2"], 1)

                def transposed(t, k):
                    eng.wait_ge(f["tr"], t * J + k + 1)
                    if k >= 2:
                        eng.wait_ge(f["o"], t * J + k - 1)
                    nc.scalar.activation(PTc[:, k % 2, :], bank[3 + k % 2], ACT.Copy).then_inc(f["tr_out"], 1)

                def heads_transposed(t, w):
                    eng.wait_ge(f["ot"], t * B + w + 1)
                    nc.scalar.activation(oTc[:, :], bank[6], ACT.Copy).then_inc(f["ot_out"], 1)

                def heads_joined(t, w):
                    eng.wait_ge(f["h2"], t * B + w + 1)
                    nc.scalar.activation(r2[:, t, w * F:(w + 1) * F], bank[6][:, 0:F], ACT.Copy)\
                        .then_inc(f["h2_out"], 1)

                def steps(t):
                    for j in range(J):
                        b, i = divmod(j, HEADS)
                        if i == 1 and b >= 2:
                            heads_joined(t, b - 2)
                        if i == 2 and b + 1 < B:
                            queries_1(t, b + 1)
                        if j >= 2:
                            transposed(t, j - 2)
                        eng.wait_ge(f["u"], t * J + j + 1)
                        if j >= 2:
                            eng.wait_ge(f["tr"], t * J + j - 1)
                        nc.scalar.activation(Pc[:, j % 2, :], Uc[:, j % 2, :], ACT.Exp,
                                             bias=nmc[:, j % 2:j % 2 + 1]).then_inc(f["p"], 1)
                        if i == 3 and b + 1 < B:
                            queries_2(t, b + 1)
                        if i == 5 and b >= 1:
                            heads_transposed(t, b - 1)

                def tail(t, more):
                    transposed(t, J - 2)
                    heads_joined(t, B - 2)
                    transposed(t, J - 1)
                    more(0)
                    more(1)
                    heads_transposed(t, B - 1)
                    more(2)
                    heads_joined(t, B - 1)

                for bp in range(3):
                    gathered(0, bp)
                queries_1(0, 0)
                gathered(0, 3)
                queries_2(0, 0)
                adj_out(0)
                with eng.Fori(0, T - 1) as t:
                    steps(t)
                    tail(t, lambda bp: gathered(t + 1, bp))
                    queries_1(t + 1, 0)
                    gathered(t + 1, 3)
                    queries_2(t + 1, 0)
                    adj_out(t + 1)
                steps(T - 1)
                tail(T - 1, lambda bp: None)

            @block.gpsimd
            def _(eng):
                with eng.Fori(0, T) as t:
                    for b in range(B):
                        eng.wait_ge(f["y2"], t * B + b + 1)
                        if b >= 2:
                            eng.wait_ge(f["s"], t * J + (b - 1) * HEADS)
                        else:
                            eng.wait_ge(f["s"], t * J)
                        nc.gpsimd.tensor_tensor(LC[0:F, b % 2, :, :].rearrange("p h n -> p (h n)"), YR[0:F, :],
                                                Y2[0:F, :], ALU.subtract)
                        nc.gpsimd.tensor_copy(LA[F:P, b % 2, :, :].rearrange("p h n -> p (h n)"), Y2[F:P, :])\
                            .then_inc(f["y3"], 1)

            @block.vector
            def _(eng):
                def choice(t, mt):
                    if mt == 0:
                        eng.wait_ge(f["adj"], t)
                    nc.vector.tensor_scalar(Sel[:, mt, :], iota1[:, :], pos[:, mt, column_of(t)], None,
                                            ALU.is_equal).then_inc(f["sel"], 1)

                def own_rows(t):
                    eng.wait_ge(f["y"], t * B)
                    for a in range(2):
                        nc.vector.tensor_copy(xq[:, a:B:2, :], hT[a * F:(a + 1) * F, :, tile_of(t)])\
                            .then_inc(f["xq"], 1)

                def gathered(t, bp, j):
                    k = 3 * bp + j
                    eng.wait_ge(f["gathered"], t * 3 * BP + k + 1)
                    for a in range(2):
                        src = G_bank[k % 4][a * F:(a + 1) * F, :]
                        b = 2 * bp + a
                        if j == 1:
                            nc.vector.tensor_copy(RB[0:F, b, :], src)
                            ins = nc.vector.tensor_copy(RB[F:P, b, :], src)
                        else:
                            ins = nc.vector.tensor_copy(RC[F:P, b, :], src)
                    ins.then_inc(f["gv"], 1)

                def rows_out(t):
                    for w in range(BP):
                        eng.wait_ge(f["v"], t * BP + w + 1)
                        nc.vector.tensor_copy(Vc[:, 2 * w:2 * w + 2, :, 0:F].rearrange("p b c f -> p (b c) f"),
                                              bank[[5, 6, 7, 5][w]].rearrange("p (g f) -> p g f", f=F))\
                            .then_inc(f["v_out"], 1)

                def queries_v(t, b):
                    eng.wait_ge(f["y1"], t * B + b + 1)
                    eng.wait_ge(f["y2"], t * B + b)
                    eng.wait_ge(f["y3"], t * B + b)
                    nc.vector.tensor_tensor(YR[:, :], ps[:, 6:8, :].rearrange("p a c -> p (a c)"), Y1[:, :],
                                            ALU.subtract).then_inc(f["yr"], 1)

                def queries_copied(t, b):
                    if b >= 2:
                        eng.wait_ge(f["s"], t * J + (b - 1) * HEADS)
                    nc.vector.tensor_copy(LA[0:F, b % 2, :, :].rearrange("p h n -> p (h n)"), Y1[0:F, :])
                    nc.vector.tensor_copy(LC[F:P, b % 2, :, :].rearrange("p h n -> p (h n)"), Y1[F:P, :])\
                        .then_inc(f["copied"], 1)

                def inverse(t, k):
                    eng.wait_ge(f["o"], t * J + k + 1)
                    if k >= 2:
                        eng.wait_ge(f["norm"], t * J + k - 1)
                    nc.vector.reciprocal(rzc[:, k % 2:k % 2 + 1], O_bank[k % 2][:, F:F + 1]).then_inc(f["rz"], 1)

                def normalised(t, k):
                    eng.wait_ge(f["rz"], t * J + k + 1)
                    w, h = divmod(k, HEADS)
                    if h == 0 and w >= 2:
                        eng.wait_ge(f["ot"], t * B + w - 1)
                    nc.vector.tensor_scalar(ob[:, w % 2, h * F:(h + 1) * F], O_bank[k % 2][:, 0:F],
                                            rzc[:, k % 2:k % 2 + 1], None, ALU.mult).then_inc(f["norm"], 1)

                def masked(t, j):
                    if j >= 4:
                        inverse(t, j - 4)
                    eng.wait_ge(f["s"], t * J + j + 1)
                    if j >= 2:
                        eng.wait_ge(f["p"], t * J + j - 1)
                    else:
                        eng.wait_ge(f["p"], t * J)
                        eng.wait_ge(f["lo"], t)
                    if j < 4:
                        nc.vector.memset(tick[:, :], 0.0)
                    else:
                        normalised(t, j - 4)
                    nc.vector.tensor_tensor_reduce(Uc[:, j % 2, :], bank[j % 2], adjc[:, :], 1.0, -3.0e38,
                                                   ALU.mult, ALU.max, mst[:, j:j + 1]).then_inc(f["own"], 1)
                    eng.wait_ge(f["own"], t * J + j + 1)
                    nc.vector.tensor_scalar(nmc[:, j % 2:j % 2 + 1], mst[:, j:j + 1], -1.0, None, ALU.mult)\
                        .then_inc(f["u"], 1)

                def heads_biased(t, w):
                    eng.wait_ge(f["cat"], t * B + w + 1)
                    eng.wait_ge(f["h2"], t * B + w)
                    nc.vector.tensor_tensor(catc[:, :, :], ps[:, 6:8, :].rearrange("p a (c n) -> p (a c) n", n=P),
                                            bh_aq[:, :].unsqueeze(2).to_broadcast([P, HEADS, P]), ALU.add)\
                        .then_inc(f["bias"], 1)

                def heads_leaky(t, w):
                    eng.wait_ge(f["bias"], t * B + w + 1)
                    nc.vector.scalar_tensor_tensor(catc[:, :, :], catc[:, :, :], 0.01, catc[:, :, :],
                                                   ALU.mult, ALU.max).then_inc(f["leaky"], 1)

                def steps(t, nxt):
                    eng.wait_ge(f["adj_out"], t + 1)
                    for j in range(J):
                        b, i = divmod(j, HEADS)
                        if i == 7 and b >= 1:
                            heads_biased(t, b - 1)
                        masked(t, j)
                        if i == 2 and b + 1 < B:
                            queries_v(t, b + 1)
                        if i == 3 and b + 1 < B:
                            queries_copied(t, b + 1)
                        if i == 7 and b >= 1:
                            heads_leaky(t, b - 1)
                        if nxt is not None and i == 4:
                            choice(nxt, b)
                        if nxt is not None and j == J - 3:
                            own_rows(nxt)

                def tail(t, more):
                    for k in range(J - 4, J):
                        inverse(t, k)
                        normalised(t, k)
                        if k == J - 3:
                            more(0, 1)
                    more(0, 2)
                    nc.vector.tensor_reduce(low[:, :], mst[:, :], X, ALU.min, negate=True).then_inc(f["tmin"], 1)
                    eng.wait_ge(f["tmin"], t + 1)
                    nc.vector.tensor_tensor(lo[:, :], lo[:, :], low[:, :], ALU.max).then_inc(f["lo"], 1)
                    more(1, 1)
                    more(1, 2)
                    heads_biased(t, B - 1)
                    heads_leaky(t, B - 1)
                    more(2, 1)
                    more(2, 2)

                for mt in range(T):
                    choice(0, mt)
                own_rows(0)
                for bp in range(3):
                    for j in (1, 2):
                        gathered(0, bp, j)
                queries_v(0, 0)
                queries_copied(0, 0)
                for j in (1, 2):
                    gathered(0, 3, j)
                rows_out(0)
                with eng.Fori(0, T - 1) as t:
                    steps(t, t + 1)
                    tail(t, lambda bp, j: gathered(t + 1, bp, j))
                    queries_v(t + 1, 0)
                    queries_copied(t + 1, 0)
                    for j in (1, 2):
                        gathered(t + 1, 3, j)
                    rows_out(t + 1)
                steps(T - 1, None)
                tail(T - 1, lambda bp, j: None)
        l2a.close()
        l2b = ExitStack()
        adjN = sb("adjN2", [P, T, N], scope=l2b)
        xb = sb("xb", [P, T, 2, F], scope=l2b)
        V = sb("V", [P, T, F + 1], scope=l2b)
        kT = sb("kT", [P, N], scope=l2b)
        yT = sb("yT", [P, N], scope=l2b)
        G_s = sb("G_s", [F, P], scope=l2b)
        Wh_p = sb("Wh_p", [P, HID], scope=l2b)
        Wo_p = sb("Wo_p", [P, 2, F], scope=l2b)
        bh_p = sb("bh_p", [P, 2], scope=l2b)
        U = sb("U", [P, 2, N], scope=l2b)
        Pr = sb("Pr", [P, 2, N], scope=l2b)
        PT = sb("PT", [P, 2, N], scope=l2b)
        nm = sb("nm", [P, 2], scope=l2b)
        rz = sb("rz", [P, 2], scope=l2b)
        oh = sb("oh", [P, T, P], scope=l2b)
        oT = sb("oT", [P, HALF], scope=l2b)
        cat = sb("cat", [P, HALF], scope=l2b)
        h2 = sb("h2", [P, T, F], scope=l2b)
        kT2 = sb("kT2", [F, 2, N], scope=l2b)
        V2 = sb("V2", [P, 2, T, F + 1], scope=l2b)
        top = sb("top", [P, 2, T], scope=l2b)
        on = sb("on", [P, 2, F], scope=l2b)
        low = sb("low2", [P, 1], scope=l2b)
        tick = sb("tick2", [P, 1], scope=l2b)

        S_bank = [0, 2]
        OP, MP = bank[6], bank[7]

        def adj_row(t):
            return adjN[:, t, :].rearrange("p (m q) -> p q m", q=T)


        z = {n: sem(f"second_{n}") for n in (
            "ones", "kt", "ktc", "v", "s", "own", "u", "p", "trl", "trr", "tv", "ts", "o", "rz", "norm", "out",
            "adj0", "adj1", "adj2", "back", "tmin", "lo")}

        def batch(b):
            return slice(b * F, (b + 1) * F) if isinstance(b, int) else bass.ds(b * F, F)

        def over_batches(eng, body):
            with eng.Fori(0, B // 2 - 1) as pair:
                body(pair * 2, 0, pair * 2 + 1)
                body(pair * 2 + 1, 1, pair * 2 + 2)
            body(B - 2, 0, B - 1)
            body(B - 1, 1, None)

        with nc.Block() as block:
            @block.sync
            def _(eng):
                rows_of = adj.rearrange("(p t) m -> p t m", t=T)
                for name, t0, t1 in (("adj0", 0, 1), ("adj1", 1, 3), ("adj2", 3, T)):
                    eng.dma_start(adjN[:, t0:t1, :], rows_of[:, t0:t1, :]).then_inc(z[name], 16)
                for j, a in enumerate((xs, hn)):
                    eng.dma_start(a[:, :, :], saved[j]).then_inc(z["back"], 16)
                for name in ("adj0", "adj1", "adj2"):
                    eng.wait_ge(z[name], 16)
                eng.wait_ge(z["back"], 32)

            @block.gpsimd
            def _(eng):
                nc.gpsimd.memset(V2[:, :, :, F:F + 1], 1.0).then_inc(z["ones"], 1)

            @block.tensor
            def _(eng):
                def keys_wait(b, h):
                    eng.wait_ge(z["v"], b + 1)
                    eng.wait_ge(z["ktc"], b * 2 + h)

                def keys(p, h):
                    for j in range(4):
                        mm = nc.tensor.transpose(bank[7][0:F, j * P:(j + 1) * P], V2[:, p, h * 4 + j, 0:F],
                                                 ident[:, :])
                    mm.then_inc(z["kt"], 1)

                def scores(b, p, i):
                    g = b * T + i
                    if i == 0:
                        eng.wait_ge(z["ktc"], (b + 1) * 2)
                    if not (isinstance(b, int) and b * T + i < 2):
                        eng.wait_ge(z["u"], b * T + (i - 1))
                    for h in range(2):
                        mm = nc.tensor.matmul(bank[2 * (i % 2) + h], kT2[:, p, i * P:(i + 1) * P],
                                              kT2[:, p, h * HALF:(h + 1) * HALF], start=True, stop=True)
                    mm.then_inc(z["s"], 1)

                def transposes(b, i):
                    g = b * T + i
                    eng.wait_ge(z["p"], g + 1)
                    for h, left, done in ((0, "tv", "trl"), (1, "ts", "trr")):
                        eng.wait_ge(z[left], g)
                        for j in range(4):
                            c = (h * 4 + j) * P
                            mm = nc.tensor.transpose(bank[4 + h][:, j * P:(j + 1) * P], Pr[:, i % 2, c:c + P],
                                                     ident[:, :])
                        mm.then_inc(z[done], 1)

                def values(b, p, i):
                    g = b * T + i
                    eng.wait_ge(z["tv"], g + 1)
                    eng.wait_ge(z["ts"], g + 1)
                    eng.wait_ge(z["norm"], g)
                    for mt in range(T):
                        mm = nc.tensor.matmul(bank[6][:, 0:F + 1], PT[:, i % 2, mt * P:(mt + 1) * P],
                                              V2[:, p, mt, :], start=mt == 0, stop=mt == T - 1)
                    mm.then_inc(z["o"], 1)

                def body(b, p, nxt):
                    for s in range(2, T + 2):
                        if s < T:
                            scores(b, p, s)
                        elif nxt is not None:
                            scores(nxt, 1 - p, s - T)
                        if s - 1 < T:
                            transposes(b, s - 1)
                        elif nxt is not None:
                            transposes(nxt, s - 1 - T)
                        if nxt is not None and s in (4, 5):
                            keys_wait(nxt, s - 4)
                        values(b, p, s - 2)
                        if nxt is not None and s in (4, 5):
                            keys(1 - p, s - 4)

                eng.wait_ge(z["ones"], 1)
                for h in range(2):
                    keys_wait(0, h)
                    keys(0, h)
                scores(0, 0, 0)
                scores(0, 0, 1)
                transposes(0, 0)
                over_batches(eng, body)

            @block.scalar
            def _(eng):
                def keys(b, p, h):
                    eng.wait_ge(z["kt"], b * 2 + (h + 1))
                    nc.scalar.activation(kT2[:, p, h * HALF:(h + 1) * HALF], bank[7][0:F, :], ACT.Copy)\
                        .then_inc(z["ktc"], 1)

                def rows_out(b, p):
                    nc.scalar.activation(V2[:, p, :, 0:F], r2[:, :, batch(b)], ACT.Copy).then_inc(z["v"], 1)

                def weights(b, i):
                    g = b * T + i
                    eng.wait_ge(z["u"], g + 1)
                    if not (isinstance(b, int) and b * T + i < 2):
                        eng.wait_ge(z["trr"], b * T + (i - 1))
                    nc.scalar.activation(Pr[:, i % 2, :], U[:, i % 2, :], ACT.Exp, bias=nm[:, i % 2:i % 2 + 1])\
                        .then_inc(z["p"], 1)

                def transposed(b, i):
                    g = b * T + i
                    eng.wait_ge(z["trr"], g + 1)
                    if not (isinstance(b, int) and b * T + i < 2):
                        eng.wait_ge(z["o"], b * T + (i - 1))
                    nc.scalar.activation(PT[:, i % 2, HALF:N], bank[5], ACT.Copy).then_inc(z["ts"], 1)

                def body(b, p, nxt):
                    for s in range(2, T + 2):
                        if s - 1 < T:
                            transposed(b, s - 1)
                        elif nxt is not None:
                            transposed(nxt, s - 1 - T)
                        if s < T:
                            weights(b, s)
                        elif nxt is not None:
                            weights(nxt, s - T)
                        if nxt is not None and s == 3:
                            eng.wait_ge(z["s"], b * T)
                            eng.wait_ge(z["o"], b * T)
                            rows_out(nxt, 1 - p)
                        if nxt is not None and s in (4, 5):
                            keys(nxt, 1 - p, s - 4)

                rows_out(0, 0)
                keys(0, 0, 0)
                keys(0, 0, 1)
                weights(0, 0)
                transposed(0, 0)
                weights(0, 1)
                over_batches(eng, body)

            @block.vector
            def _(eng):
                def masked(b, p, i):
                    g = b * T + i
                    if i in (0, 1, 3):
                        eng.wait_ge(z[{0: "adj0", 1: "adj1", 3: "adj2"}[i]], 16)
                    eng.wait_ge(z["s"], g + 1)
                    if not (isinstance(b, int) and b * T + i < 2):
                        eng.wait_ge(z["p"], b * T + (i - 1))
                    nc.vector.memset(tick[:, :], 0.0)
                    nc.vector.tensor_tensor_reduce(
                        U[:, i % 2, :].rearrange("p (q m) -> p q m", q=T),
                        ps[:, 2 * (i % 2):2 * (i % 2) + 2, :].rearrange("p h (q m) -> p (h q) m", q=4),
                        adj_row(i), 1.0, -3.0e38, ALU.mult, ALU.max, top[:, p, i:i + 1]).then_inc(z["own"], 1)
                    eng.wait_ge(z["own"], g + 1)
                    nc.vector.tensor_scalar(nm[:, i % 2:i % 2 + 1], top[:, p, i:i + 1], -1.0, None, ALU.mult)\
                        .then_inc(z["u"], 1)

                def transposed(b, i):
                    g = b * T + i
                    eng.wait_ge(z["trl"], g + 1)
                    if not (isinstance(b, int) and b * T + i < 2):
                        eng.wait_ge(z["o"], b * T + (i - 1))
                    nc.vector.tensor_copy(PT[:, i % 2, 0:HALF], bank[4]).then_inc(z["tv"], 1)

                def normalised(b, i):
                    g = b * T + i
                    eng.wait_ge(z["o"], g + 1)
                    eng.wait_ge(z["norm"], b * T + max(i - 1, 0))
                    eng.wait_ge(z["out"], b * T + max(i - 1, 0))
                    nc.vector.reciprocal(rz[:, i % 2:i % 2 + 1], bank[6][:, F:F + 1]).then_inc(z["rz"], 1)
                    eng.wait_ge(z["rz"], g + 1)
                    nc.vector.scalar_tensor_tensor(on[:, i % 2, :], bank[6][:, 0:F], rz[:, i % 2:i % 2 + 1],
                                                   bout_row[:, :], ALU.mult, ALU.add).then_inc(z["norm"], 1)
                    eng.wait_ge(z["norm"], g + 1)
                    nc.vector.scalar_tensor_tensor(r2[:, i, batch(b)], on[:, i % 2, :], 0.01, on[:, i % 2, :],
                                                   ALU.mult, ALU.max).then_inc(z["out"], 1)

                def body(b, p, nxt):
                    for s in range(2, T + 2):
                        if s < T:
                            masked(b, p, s)
                        elif nxt is not None:
                            if s == T:
                                eng.wait_ge(z["lo"], b)
                            masked(nxt, 1 - p, s - T)
                        if s - 1 < T:
                            transposed(b, s - 1)
                        elif nxt is not None:
                            transposed(nxt, s - 1 - T)
                        normalised(b, s - 2)
                    nc.vector.tensor_reduce(low[:, :], top[:, p, :], X, ALU.min, negate=True)\
                        .then_inc(z["tmin"], 1)
                    eng.wait_ge(z["tmin"], b + 1)
                    nc.vector.tensor_tensor(lo[:, :], lo[:, :], low[:, :], ALU.max).then_inc(z["lo"], 1)

                masked(0, 0, 0)
                masked(0, 0, 1)
                transposed(0, 0)
                over_batches(eng, body)


        def attention_stage(name):
            names = ("pool", "s", "u", "p", "tr", "tv", "ts", "o", "norm", "own", "x", "kt", "ktc", "y", "yc",
                     "ot", "otc", "cat", "catc", "catv", "h2", "h2c", "own2", "w")
            q = {n: sem(f"{name}_{n}") for n in names}
            UNROLL = 2 * T
            PER_B = HP * UNROLL + T

            def body(fn):
                def run(eng):
                    need = eng.value_load(flags[0:1, 1:2], min_val=0, max_val=1)
                    with eng.If(need > 0):
                        fn(eng)
                return run

            def tiles_tensor(eng, g0, tiles, y, k):
                def scores(i):
                    eng.wait_ge(q["u"], g0 + i)
                    for h in range(2):
                        mm = nc.tensor.matmul(bank[S_bank[i % 2] + h][:, :], y(i), k(i, h), start=True, stop=True)
                    mm.then_inc(q["s"], 1)

                def transposes(i):
                    eng.wait_ge(q["p"], g0 + i + 1)
                    for h in range(2):
                        eng.wait_ge(q["tv"] if h == 0 else q["ts"], g0 + i)
                        for j in range(4):
                            c = (h * 4 + j) * P
                            mm = nc.tensor.transpose(bank[4 + h][:, j * P:(j + 1) * P], Pr[:, i % 2, c:c + P],
                                                     ident[:, :])
                        mm.then_inc(q["tr"], 1)

                def values(i):
                    eng.wait_ge(q["tv"], g0 + i + 1)
                    eng.wait_ge(q["ts"], g0 + i + 1)
                    eng.wait_ge(q["norm"], g0 + i)
                    for mt in range(T):
                        mm = nc.tensor.matmul(OP[:, 0:F + 1], PT[:, i % 2, mt * P:(mt + 1) * P], V[:, mt, :],
                                              start=mt == 0, stop=mt == T - 1)
                    mm.then_inc(q["o"], 1)
                for s in range(tiles + 2):
                    if s < tiles:
                        scores(s)
                    if 1 <= s <= tiles:
                        transposes(s - 1)
                    if s >= 2:
                        values(s - 2)

            def tiles_scalar(eng, g0, tiles):
                for s in range(tiles + 1):
                    if s < tiles:
                        eng.wait_ge(q["u"], g0 + s + 2)
                        nc.scalar.activation(Pr[:, s % 2, :], U[:, s % 2, :], ACT.Exp, bias=nm[:, s % 2:s % 2 + 1])\
                            .then_inc(q["p"], 1)
                    if s >= 1:
                        i = s - 1
                        eng.wait_ge(q["tr"], (g0 + i) * 2 + 2)
                        eng.wait_ge(q["o"], g0 + i - 1 + 1) if i >= 1 else eng.wait_ge(q["o"], g0)
                        nc.scalar.activation(PT[:, i % 2, HALF:N], bank[5][:, :], ACT.Copy).then_inc(q["ts"], 1)

            def tiles_vector(eng, g0, tiles, row, out_of):
                OWN = 4
                for s in range(tiles + 2):
                    if s < tiles:
                        i, t = s, s % T
                        eng.wait_ge(q["s"], g0 + i + 1)
                        eng.wait_ge(q["p"], g0 + i - 1 if i >= 1 else g0)
                        m = nm[:, i % 2:i % 2 + 1]
                        sc2 = [bank[S_bank[i % 2] + h][:, :] for h in range(2)]
                        for h in range(2):
                            ins = nc.vector.tensor_tensor(
                                U[:, i % 2, h * HALF:(h + 1) * HALF].rearrange("p (q m) -> p q m", q=4),
                                sc2[h].rearrange("p (q m) -> p q m", q=4), row(t)[:, h * 4:h * 4 + 4, :],
                                ALU.mult)
                        ins.then_inc(q["own"], 1)
                        eng.wait_ge(q["own"], (g0 + i) * OWN + 1)
                        nc.vector.tensor_scalar(Pr[:, i % 2, :], U[:, i % 2, :], 0.0, NEG_GAT,
                                                ALU.is_equal, ALU.mult).then_inc(q["own"], 1)
                        eng.wait_ge(q["own"], (g0 + i) * OWN + 2)
                        nc.vector.tensor_tensor(U[:, i % 2, :], U[:, i % 2, :], Pr[:, i % 2, :], ALU.add)\
                            .then_inc(q["own"], 1)
                        eng.wait_ge(q["own"], (g0 + i) * OWN + 3)
                        nc.vector.tensor_reduce(m, U[:, i % 2, :], X, ALU.max, negate=True).then_inc(q["own"], 1)
                        eng.wait_ge(q["own"], (g0 + i + 1) * OWN)
                        nc.vector.tensor_tensor(lo[:, :], lo[:, :], m, ALU.max).then_inc(q["u"], 1)
                    if 1 <= s <= tiles:
                        i = s - 1
                        eng.wait_ge(q["tr"], (g0 + i) * 2 + 1)
                        eng.wait_ge(q["o"], g0 + i)
                        nc.vector.tensor_copy(PT[:, i % 2, 0:HALF], bank[4][:, :]).then_inc(q["tv"], 1)
                    if s >= 2:
                        i = s - 2
                        eng.wait_ge(q["o"], g0 + i + 1)
                        nc.vector.reciprocal(rz[:, i % 2:i % 2 + 1], OP[:, F:F + 1]).then_inc(q["own2"], 1)
                        eng.wait_ge(q["own2"], g0 + i + 1)
                        nc.vector.tensor_scalar(out_of(i), OP[:, 0:F], rz[:, i % 2:i % 2 + 1], None, ALU.mult)\
                            .then_inc(q["norm"], 1)

            with nc.Block() as block:
                def pool(eng):
                    nc.gpsimd.memset(V[:, :, F:F + 1], 1.0).then_inc(q["pool"], 1)
                    eng.wait_ge(q["pool"], 1)
                    with eng.Fori(0, B) as b:
                        eng.wait_ge(q["norm"], b * PER_B)
                        xv = hn[:, :, bass.ts(b, F)]
                        nc.gpsimd.tensor_copy(xb[:, :, 0, :], xv)
                        nc.gpsimd.tensor_copy(xb[:, :, 1, :], xv)
                        nc.gpsimd.tensor_copy(V[:, :, 0:F], xv).then_inc(q["x"], 1)
                block.gpsimd(body(pool))

                KEYS = 2

                def keys_tensor(eng, n):
                    eng.wait_ge(q["x"], n + 1)
                    for h in range(2):
                        for j in range(4):
                            mm = nc.tensor.transpose(bank[4 + h][:, j * P:(j + 1) * P],
                                                     xb[:, h * 4 + j, :, :].rearrange("p a f -> p (a f)"),
                                                     ident[:, :])
                    mm.then_inc(q["kt"], 1)

                def pair_tensor(eng, b, hp):
                    n = b * HP + hp
                    eng.wait_ge(q["ktc"], b * 4 + 2)
                    eng.wait_ge(q["w"], (n + 1) * 5)
                    for h in range(2):
                        if h == 1:
                            eng.wait_ge(q["yc"], n * 2 + 1)
                        else:
                            eng.wait_ge(q["h2c"], n)
                        nc.tensor.matmul(MP[:, :], G_s[:, :], kT[0:F, h * HALF:(h + 1) * HALF],
                                         start=True, stop=True).then_inc(q["y"], 1)
                    eng.wait_ge(q["yc"], n * 2 + 2)

                    def part(i):
                        return slice((i // T) * F, (i // T + 1) * F)
                    tiles_tensor(eng, b * PER_B + hp * UNROLL, UNROLL,
                                 lambda i: yT[part(i), (i % T) * P:(i % T + 1) * P],
                                 lambda i, h: kT[part(i), h * HALF:(h + 1) * HALF])
                    eng.wait_ge(q["norm"], b * PER_B + (hp + 1) * UNROLL)
                    for h in range(2):
                        if h == 1:
                            eng.wait_ge(q["otc"], n * 2 + 1)
                        for j in range(4):
                            mm = nc.tensor.transpose(bank[4][:, j * P:(j + 1) * P], oh[:, h * 4 + j, :],
                                                     ident[:, :])
                        mm.then_inc(q["ot"], 1)
                        eng.wait_ge(q["otc"], n * 2 + h + 1)
                        for a in range(2):
                            s = slice(a * F, (a + 1) * F)
                            nc.tensor.matmul(bank[5][:, :], Wh_p[s, :], oT[s, :],
                                             start=True, stop=True).then_inc(q["cat"], 1)
                            eng.wait_ge(q["catv"], n * 4 + h * 2 + a + 1)
                            for j in range(4):
                                t = h * 4 + j
                                mm = nc.tensor.matmul(
                                    bank[a * 2][:, t * F:(t + 1) * F],
                                    cat[:, j * P:(j + 1) * P], Wo_p[:, a, :], start=True, stop=True)
                            mm.then_inc(q["h2"], 1)
                    eng.wait_ge(q["h2c"], n + 1)

                def tensor(eng):
                    eng.wait_ge(q["pool"], 1)
                    with eng.Fori(0, B) as b:
                        keys_tensor(eng, b * KEYS)
                        with eng.Fori(0, HP) as hp:
                            pair_tensor(eng, b, hp)
                        keys_tensor(eng, b * KEYS + KEYS - 1)
                        eng.wait_ge(q["ktc"], (b + 1) * KEYS * 2)
                        tiles_tensor(eng, b * PER_B + (PER_B - T), T,
                                     lambda i: kT[0:F, i * P:(i + 1) * P],
                                     lambda i, h: kT[0:F, h * HALF:(h + 1) * HALF])
                        eng.wait_ge(q["norm"], (b + 1) * PER_B)
                block.tensor(body(tensor))

                def pair_scalar(eng, b, hp):
                    n = b * HP + hp
                    eng.wait_ge(q["h2c"], n)
                    for dst, src in ((G_s[:, :], GG[:, hp, :]), (Wh_p[0:F, :], Wh_s[0:F, hp * 2, :]),
                                     (Wh_p[F:P, :], Wh_s[F:P, hp * 2 + 1, :]),
                                     (Wo_p[:, :, :], Wo_s[:, bass.ts(hp, 2), :]),
                                     (bh_p[:, :], bh_s[:, bass.ts(hp, 2)])):
                        nc.scalar.activation(dst, src, ACT.Copy).then_inc(q["w"], 1)
                    for h in range(2):
                        eng.wait_ge(q["y"], n * 2 + h + 1)
                        nc.scalar.activation(yT[:, h * HALF:(h + 1) * HALF], MP[:, :], ACT.Copy)\
                            .then_inc(q["yc"], 1)
                    tiles_scalar(eng, b * PER_B + hp * UNROLL, UNROLL)
                    for c in range(4):
                        h, a = divmod(c, 2)
                        eng.wait_ge(q["cat"], n * 4 + c + 1)
                        eng.wait_ge(q["h2"], n * 4 + c)
                        eng.wait_ge(q["w"], (n + 1) * 5)
                        nc.scalar.activation(cat[:, :], bank[5][:, :], ACT.Identity, bias=bh_p[:, a:a + 1])\
                            .then_inc(q["catc"], 1)

                def scalar(eng):
                    with eng.Fori(0, B) as b:
                        with eng.Fori(0, HP) as hp:
                            pair_scalar(eng, b, hp)
                        eng.wait_ge(q["h2c"], (b + 1) * HP)
                        src = h2[:, :, :]
                        for a in range(2):
                            nc.scalar.activation(xb[:, :, a, :], src, ACT.Copy)
                        nc.scalar.activation(V[:, :, 0:F], src, ACT.Copy).then_inc(q["x"], 1)
                        tiles_scalar(eng, b * PER_B + (PER_B - T), T)
                block.scalar(body(scalar))

                def pair_vector(eng, b, hp):
                    n = b * HP + hp
                    tiles_vector(eng, b * PER_B + hp * UNROLL, UNROLL, adj_row,
                                 lambda i: oh[:, i % T, (i // T) * F:(i // T + 1) * F])
                    for h in range(2):
                        eng.wait_ge(q["ot"], n * 2 + h + 1)
                        nc.vector.tensor_copy(oT[:, :], bank[4][:, :]).then_inc(q["otc"], 1)
                        for a in range(2):
                            c = h * 2 + a
                            eng.wait_ge(q["catc"], n * 4 + c + 1)
                            nc.vector.scalar_tensor_tensor(cat[:, :], cat[:, :], 0.01, cat[:, :],
                                                           ALU.mult, ALU.max).then_inc(q["catv"], 1)
                    eng.wait_ge(q["h2"], n * 4 + 4)
                    eng.wait_ge(q["h2z"], b + 1)
                    h2f = h2[:, :, :].rearrange("p t f -> p (t f)")
                    nc.vector.tensor_tensor(h2f, h2f, bank[0], ALU.add).then_inc(q["h2v"], 1)
                    eng.wait_ge(q["h2v"], n + 1)
                    nc.vector.tensor_tensor(h2f, h2f, bank[2], ALU.add).then_inc(q["h2c"], 1)
                    eng.wait_ge(q["h2c"], n + 1)

                def vector(eng):
                    def copy_keys(n):
                        eng.wait_ge(q["kt"], n + 1)
                        for h in range(2):
                            nc.vector.tensor_copy(kT[:, h * HALF:(h + 1) * HALF], bank[4 + h][:, :])\
                                .then_inc(q["ktc"], 1)

                    nc.vector.memset(lo[:, :], NEG_GAT * 4).then_inc(q["u"], 1)
                    eng.wait_ge(q["u"], 1)
                    with eng.Fori(0, B) as b:
                        copy_keys(b * KEYS)
                        nc.vector.memset(h2[:, :, :], 0.0).then_inc(q["h2z"], 1)
                        with eng.Fori(0, HP) as hp:
                            pair_vector(eng, b, hp)
                        copy_keys(b * KEYS + KEYS - 1)
                        tiles_vector(eng, b * PER_B + (PER_B - T), T, adj_row, lambda i: oh[:, i, 0:F])
                        eng.wait_ge(q["norm"], (b + 1) * PER_B)
                        nc.vector.tensor_tensor(oh[:, :, 0:F], oh[:, :, 0:F],
                                                bout_row[:, :].unsqueeze(1).to_broadcast([P, T, F]), ALU.add)\
                            .then_inc(q["fin"], 1)
                        eng.wait_ge(q["fin"], b * 2 + 1)
                        nc.vector.scalar_tensor_tensor(r2[:, :, bass.ts(b, F)], oh[:, :, 0:F], 0.01, oh[:, :, 0:F],
                                                       ALU.mult, ALU.max).then_inc(q["fin"], 1)
                        eng.wait_ge(q["fin"], b * 2 + 2)
                for n in ("h2z", "h2v", "fin"):
                    q[n] = sem(f"{name}_{n}")
                block.vector(body(vector))

        lo_t, lo_v = sem("lo_t"), sem("lo_v")
        need = sb("need", [1, 4], scope=l2b)
        with nc.Block() as block:
            @block.tensor
            def _(eng):
                nc.tensor.transpose(bank[0][0:1, 0:P], lo[:, :], ident[:, :])
                nc.tensor.transpose(bank[0][0:1, P:2 * P], most[:, 0:1], ident[:, :])
                nc.tensor.transpose(bank[0][0:1, 2 * P:3 * P], most[:, 1:2], ident[:, :]).then_inc(lo_t, 1)

            @block.vector
            def _(eng):
                eng.wait_ge(lo_t, 1)
                nc.vector.tensor_reduce(need[0:1, 0:3], bank[0][0:1, 0:3 * P].rearrange("p (a c) -> p a c", a=3),
                                        X, ALU.max).then_inc(lo_v, 1)
                eng.wait_ge(lo_v, 1)
                for j, limit in enumerate((-SAFE_MAX, float(CAP), 0.0)):
                    nc.vector.tensor_scalar(need[0:1, j:j + 1], need[0:1, j:j + 1], limit, None, ALU.is_gt)\
                        .then_inc(lo_v, 1)
                eng.wait_ge(lo_v, 4)
                nc.vector.tensor_reduce(need[0:1, 3:4], need[0:1, 0:3], X, ALU.max).then_inc(lo_v, 1)
                eng.wait_ge(lo_v, 5)
                nc.vector.tensor_copy(flags[0:1, 1:2], need[0:1, 3:4]).then_inc(lo_v, 1)
                eng.wait_ge(lo_v, 6)
        attention_stage("gat_any")
        l2b.close()

        layernorm_stage("ln3", xs, hn, r2, adds=r2, to=hT)
        l2.close()
        retire_semaphores()
        l3 = ExitStack()
        dinv = sb("dinv", [P, T], scope=l3)
        z3 = sb("z3", [P, T, BF], scope=l3)
        d_v, d_s = sem("dinv_v"), sem("dinv_s")
        with nc.Block() as block:
            @block.vector
            def _(eng):
                eng.wait_ge(d_s, 1)
                nc.vector.reciprocal(dinv[:, :], dinv[:, :]).then_inc(d_v, 1)
                eng.wait_ge(d_v, 1)

            @block.scalar
            def _(eng):
                nc.scalar.activation(dinv[:, :], rows[:, :], ACT.Sqrt, bias=one_col[:, :]).then_inc(d_s, 1)

        z_d, z_c, a_d, a_v, f_v, o_d = (sem(f"l3_{s}") for s in ("z", "z_out", "az", "az_v", "sum_v", "stored"))
        with nc.Block() as block:
            @block.tensor
            def _(eng):
                for t in range(T):
                    if t >= 4:
                        eng.wait_ge(z_c, t - 3)
                    for bp in range(BP):
                        mm = nc.tensor.matmul(bank[t % 4][:, bp * P:(bp + 1) * P], hT[:, bp, t * P:(t + 1) * P],
                                              bd[:, 3, :], start=True, stop=True)
                    mm.then_inc(z_d, 1)
                eng.wait_ge(z_c, T)
                for nt in range(T):
                    if nt >= 4:
                        eng.wait_ge(a_v, (nt - 3) * 2)
                    for mt in range(T):
                        mm = nc.tensor.matmul(bank[4 + nt % 4][:, :], adjT[:, mt, nt * P:(nt + 1) * P],
                                              z3[:, mt, :], start=mt == 0, stop=mt == T - 1)
                    mm.then_inc(a_d, 1)

            @block.scalar
            def _(eng):
                for t in range(T):
                    eng.wait_ge(z_d, t + 1)
                    nc.scalar.activation(z3[:, t, :], bank[t % 4][:, :], ACT.Copy, scale=dinv[:, t:t + 1])\
                        .then_inc(z_c, 1)

            @block.vector
            def _(eng):
                eng.wait_ge(z_c, T)
                for nt in range(T):
                    eng.wait_ge(a_d, nt + 1)
                    nc.vector.tensor_tensor(hn[:, nt, :], bank[4 + nt % 4][:, :], z3[:, nt, :], ALU.add)\
                        .then_inc(a_v, 1)
                    eng.wait_ge(a_v, nt * 2 + 1)
                    nc.vector.scalar_tensor_tensor(xs[:, nt, :], hn[:, nt, :], dinv[:, nt:nt + 1], xs[:, nt, :],
                                                   ALU.mult, ALU.add).then_inc(a_v, 1)

            @block.sync
            def _(eng):
                for t in range(T):
                    eng.wait_ge(a_v, t * 2 + 2)
                    eng.dma_start(out.rearrange("b (p t) f -> t p b f", t=T)[t],
                                  xs[:, t, :].rearrange("p (b f) -> p b f", b=B)).then_inc(o_d, 16)
                eng.wait_ge(o_d, 16 * T)
        l3.close()


_INS = ["x", "adj", "L0_gnn_H", "L0_gnn_W", "L0_gnn_W_ind", "L0_gnn_a_node", "L0_gnn_a_gn", "L0_gnn_a_ge",
        "L0_gnn_fcW", "L0_gnn_fcb", "L0_gnn_av", "L1_gnn_intervention_value", "L1_gnn_W1", "L1_gnn_b1",
        "L1_gnn_W2", "L1_gnn_b2", "L2_gnn_Wh", "L2_gnn_bh", "L2_gnn_W_out", "L2_gnn_b_out", "L3_gnn_W"]


def kernel(**inputs):
    import numpy as _np
    import concourse.bacc as _bacc
    from concourse import mybir as _mybir
    from concourse.bass_utils import run_bass_kernel_spmd as _run

    nc = _bacc.Bacc("TRN2", target_bir_lowering=False, num_devices=1)
    arrays, args = {}, []
    for name in _INS:
        a = _np.ascontiguousarray(inputs[name])
        arrays[f"in_{name}_dram"] = a
        args.append(nc.dram_tensor(f"in_{name}_dram", a.shape, _mybir.dt.from_np(a.dtype), kind="ExternalInput").ap())
    out = nc.dram_tensor("out_dram", (B, N, F), _mybir.dt.float32, kind="ExternalOutput").ap()
    hyper_gat_stack(nc, *args, out)
    r = _run(nc, [arrays], core_ids=[0])
    return r.results[0]["out_dram"]
```
